# Optimizing a Trainium2 kernel written in Bass

```python
import numpy as np
import jax
import jax.numpy as jnp

def _softmax(x, axis=-1):
    return jax.nn.softmax(x, axis=axis)

def _gelu(x):
    return jax.nn.gelu(x, approximate=True)

def _silu(x):
    return jax.nn.silu(x)

def _sigmoid(x):
    return jax.nn.sigmoid(x)

def _layernorm(x, axis=-1, eps=1e-05):
    m = jnp.mean(x, axis=axis, keepdims=True)
    v = jnp.var(x, axis=axis, keepdims=True)
    return (x - m) / jnp.sqrt(v + eps)

def _scatter_add(tgt, idx, src, axis=0):
    return tgt.at[idx].add(src)

def _segment_sum(src, seg, n):
    return jax.ops.segment_sum(src, seg, n)
kernel_name = 'mk_flamingo_gated_d2_seqx_r4_2a418d'

def setup_inputs(seed: int=0):
    np.random.seed(seed)
    _w = jnp.asarray

    def _rec_inputs():
        import jax
        import jax.numpy as jnp
        _rk = jax.random.key(seed)
        x = -0.0003929 + 0.9999 * jax.random.normal(jax.random.fold_in(_rk, 1), (8, 100, 256), jnp.float32)
        _lenS = 100 - jax.random.randint(jax.random.fold_in(_rk, 7), (8,), 0, max(1, 100 // 4) + 1, jnp.int32)
        _lenS2 = 361 - jax.random.randint(jax.random.fold_in(_rk, 8), (8,), 0, max(1, 361 // 4) + 1, jnp.int32)
        _ctx_768P = jax.random.normal(jax.random.fold_in(_rk, 11), (8, 16, 192), jnp.float32)
        _ctx_768c = jax.random.dirichlet(jax.random.fold_in(_rk, 511), 0.3 * jnp.ones((16,), jnp.float32), (8, 361))
        _ctx_768t = jnp.einsum('bsk,bkd->bsd', _ctx_768c, _ctx_768P)
        _ctx_768t = _ctx_768t * jax.lax.rsqrt(jnp.mean(jnp.square(_ctx_768t)) + 1e-12) * 0.953939
        ctx_768 = 2.09791e-05 + 1.00001 * (_ctx_768t + 0.3 * jax.random.normal(jax.random.fold_in(_rk, 611), (8, 361, 192), jnp.float32))
        _validS = jnp.arange(100)[None, :] < _lenS[:, None]
        _validS2 = jnp.arange(361)[None, :] < _lenS2[:, None]
        _causal = jnp.tril(jnp.ones((100, 100), dtype=bool))
        mask_BxS2_bk0 = jnp.logical_not(jnp.broadcast_to(_validS2[:, :], (8, 361)))
        _g = jax.random.normal(jax.random.fold_in(_rk, 9001), (2, 2), jnp.float32)
        _g = jnp.sign(_g) * jnp.maximum(jnp.abs(_g), 1.0) + (_g == 0) * 1.0
        g_xattn = _g[0]
        g_ffn = _g[1]
        return (x, ctx_768, mask_BxS2_bk0, g_xattn, g_ffn)
    x, ctx_768, mask_BxS2_bk0, g_xattn, g_ffn = _rec_inputs()

    def _L0_xattn_setup():
        import jax, jax.numpy as jnp
        import numpy as np
        HEADS = 8
        DIM_HEAD = 64
        QUERY_DIM = 256
        CONTEXT_DIM = 192
        INNER = HEADS * DIM_HEAD
        key = jax.random.key(seed)
        ks = jax.random.split(key, 7)
        B, Sq, Skv = (4, 1024, 256)
        x = jax.random.normal(ks[0], (B, Sq, QUERY_DIM), dtype=jnp.float32)
        context = jax.random.normal(ks[1], (B, Skv, CONTEXT_DIM), dtype=jnp.float32)
        Wq = jax.random.normal(ks[2], (QUERY_DIM, INNER), dtype=jnp.float32) * QUERY_DIM ** (-0.5)
        Wk = jax.random.normal(ks[3], (CONTEXT_DIM, INNER), dtype=jnp.float32) * CONTEXT_DIM ** (-0.5)
        Wv = jax.random.normal(ks[4], (CONTEXT_DIM, INNER), dtype=jnp.float32) * CONTEXT_DIM ** (-0.5)
        Wo = jax.random.normal(ks[5], (INNER, QUERY_DIM), dtype=jnp.float32) * INNER ** (-0.5)
        bo = jax.random.normal(ks[6], (QUERY_DIM,), dtype=jnp.float32) * 0.01
        return {'x': x, 'context': context, 'Wq': Wq, 'Wk': Wk, 'Wv': Wv, 'Wo': Wo, 'bo': bo}
    _L0_xattn_all = _L0_xattn_setup()
    _L0_xattn_in = {k: v for k, v in _L0_xattn_all.items() if k in ('Wq', 'Wk', 'Wv', 'Wo', 'bo')}
    del _L0_xattn_all

    def _L0_ffn_setup():
        import jax, jax.numpy as jnp
        import numpy as np
        from jax import lax
        T, B, I, M, O = (64, 64, 256, 256, 256)

        def _xavier(key, shape):
            fan_out, fan_in = shape
            limit = float(np.sqrt(6.0 / (fan_in + fan_out)))
            return jax.random.uniform(key, shape, jnp.float32, -limit, limit)
        key = jax.random.key(seed)
        ks = jax.random.split(key, 9)
        x = jax.random.normal(ks[0], (T, B, I), jnp.float32)
        return {'x': x, 'wf': _xavier(ks[1], (M, I)), 'uf': _xavier(ks[2], (M, M)), 'bf': jnp.zeros((M,), jnp.float32), 'wi': _xavier(ks[3], (M, I)), 'ui': _xavier(ks[4], (M, M)), 'bi': jnp.zeros((M,), jnp.float32), 'wc': _xavier(ks[5], (M, I)), 'uc': _xavier(ks[6], (M, M)), 'bc': jnp.zeros((M,), jnp.float32), 'wo': _xavier(ks[7], (O, I)), 'uo': _xavier(ks[8], (O, M)), 'bo': jnp.zeros((O,), jnp.float32), 'in_c': jnp.zeros((M,), jnp.float32)}
    _L0_ffn_all = _L0_ffn_setup()
    _L0_ffn_in = {k: v for k, v in _L0_ffn_all.items() if k in ('wf', 'uf', 'bf', 'wi', 'ui', 'bi', 'wc', 'uc', 'bc', 'wo', 'uo', 'bo', 'in_c')}
    del _L0_ffn_all

    def _L1_xattn_setup():
        import jax, jax.numpy as jnp
        import numpy as np
        DIM_IN, DIM_LAT, DIM_HEAD = (192, 256, 64)
        INNER = max(DIM_LAT, DIM_IN)
        HEADS = INNER // DIM_HEAD
        SCALE = DIM_HEAD ** (-0.5)
        RMS_EPS = 1e-08
        LN_EPS = 1e-05

        def layernorm(x, g, b):
            mu = jnp.mean(x, axis=-1, keepdims=True)
            var = jnp.mean((x - mu) ** 2, axis=-1, keepdims=True)
            return (x - mu) * jax.lax.rsqrt(var + LN_EPS) * g + b

        def rmsnorm(x, gamma):
            norm = jnp.sqrt(jnp.sum(x * x, axis=-1, keepdims=True)) * x.shape[-1] ** (-0.5)
            return x / jnp.maximum(norm, RMS_EPS) * gamma
        key = jax.random.key(seed)
        ks = jax.random.split(key, 12)
        b, n, m = (4, 1024, 128)
        x = jax.random.normal(ks[0], (b, n, DIM_IN), jnp.float32)
        latents = jax.random.normal(ks[1], (b, m, DIM_LAT), jnp.float32)
        mask = jax.random.randint(ks[2], (b, n), 0, 2).astype(bool)
        s = lambda k, sh, fan: jax.random.normal(k, sh, jnp.float32) * fan ** (-0.5)
        return {'x': x, 'latents': latents, 'mask': mask, 'ln_x_g': jnp.ones((DIM_IN,), jnp.float32), 'ln_x_b': jnp.zeros((DIM_IN,), jnp.float32), 'ln_l_g': jnp.ones((DIM_LAT,), jnp.float32), 'ln_l_b': jnp.zeros((DIM_LAT,), jnp.float32), 'qn_g': jnp.ones((DIM_HEAD,), jnp.float32), 'kn_g': jnp.ones((DIM_HEAD,), jnp.float32), 'Wq': s(ks[3], (INNER, DIM_LAT), DIM_LAT), 'Wkv': s(ks[4], (2 * INNER, DIM_IN), DIM_IN), 'Wlkv': s(ks[5], (2 * INNER, DIM_LAT), DIM_LAT), 'Wo': s(ks[6], (DIM_LAT, INNER), INNER), 'bo': jnp.zeros((DIM_LAT,), jnp.float32)}
    _L1_xattn_all = _L1_xattn_setup()
    _L1_xattn_in = {k: v for k, v in _L1_xattn_all.items() if k in ('ln_x_g', 'ln_x_b', 'ln_l_g', 'ln_l_b', 'qn_g', 'kn_g', 'Wq', 'Wkv', 'Wlkv', 'Wo', 'bo')}
    del _L1_xattn_all

    def _L1_ffn_setup():
        import jax, jax.numpy as jnp
        import numpy as np
        TOPK = 4
        key = jax.random.key(seed)
        ks = jax.random.split(key, 9)
        B, T, D = (4, 512, 256)
        E, H = (32, 128)
        HS = H * TOPK
        s = lambda k, shape, fan: jax.random.normal(k, shape, dtype=jnp.float32) / np.sqrt(fan)
        return {'x': jax.random.normal(ks[0], (B, T, D), dtype=jnp.float32), 'router_w': s(ks[1], (E, D), D), 'router_bias': jnp.zeros((E,), dtype=jnp.float32), 'gate_w': s(ks[2], (E, H, D), D), 'up_w': s(ks[3], (E, H, D), D), 'down_w': s(ks[4], (E, D, H), H), 'sgate_w': s(ks[5], (HS, D), D), 'sup_w': s(ks[6], (HS, D), D), 'sdown_w': s(ks[7], (D, HS), HS)}
    _L1_ffn_all = _L1_ffn_setup()
    _L1_ffn_in = {k: v for k, v in _L1_ffn_all.items() if k in ('router_w', 'router_bias', 'gate_w', 'up_w', 'down_w', 'sgate_w', 'sup_w', 'sdown_w')}
    del _L1_ffn_all
    return {'x': x, 'ctx_768': ctx_768, 'mask_BxS2_bk0': mask_BxS2_bk0, 'g_xattn': g_xattn, 'g_ffn': g_ffn, 'L0_xattn_Wq': _L0_xattn_in['Wq'], 'L0_xattn_Wk': _L0_xattn_in['Wk'], 'L0_xattn_Wv': _L0_xattn_in['Wv'], 'L0_xattn_Wo': _L0_xattn_in['Wo'], 'L0_xattn_bo': _L0_xattn_in['bo'], 'L0_ffn_wf': _L0_ffn_in['wf'], 'L0_ffn_uf': _L0_ffn_in['uf'], 'L0_ffn_bf': _L0_ffn_in['bf'], 'L0_ffn_wi': _L0_ffn_in['wi'], 'L0_ffn_ui': _L0_ffn_in['ui'], 'L0_ffn_bi': _L0_ffn_in['bi'], 'L0_ffn_wc': _L0_ffn_in['wc'], 'L0_ffn_uc': _L0_ffn_in['uc'], 'L0_ffn_bc': _L0_ffn_in['bc'], 'L0_ffn_wo': _L0_ffn_in['wo'], 'L0_ffn_uo': _L0_ffn_in['uo'], 'L0_ffn_bo': _L0_ffn_in['bo'], 'L0_ffn_in_c': _L0_ffn_in['in_c'], 'L1_xattn_ln_x_g': _L1_xattn_in['ln_x_g'], 'L1_xattn_ln_x_b': _L1_xattn_in['ln_x_b'], 'L1_xattn_ln_l_g': _L1_xattn_in['ln_l_g'], 'L1_xattn_ln_l_b': _L1_xattn_in['ln_l_b'], 'L1_xattn_qn_g': _L1_xattn_in['qn_g'], 'L1_xattn_kn_g': _L1_xattn_in['kn_g'], 'L1_xattn_Wq': _L1_xattn_in['Wq'], 'L1_xattn_Wkv': _L1_xattn_in['Wkv'], 'L1_xattn_Wlkv': _L1_xattn_in['Wlkv'], 'L1_xattn_Wo': _L1_xattn_in['Wo'], 'L1_xattn_bo': _L1_xattn_in['bo'], 'L1_ffn_router_w': _L1_ffn_in['router_w'], 'L1_ffn_router_bias': _L1_ffn_in['router_bias'], 'L1_ffn_gate_w': _L1_ffn_in['gate_w'], 'L1_ffn_up_w': _L1_ffn_in['up_w'], 'L1_ffn_down_w': _L1_ffn_in['down_w'], 'L1_ffn_sgate_w': _L1_ffn_in['sgate_w'], 'L1_ffn_sup_w': _L1_ffn_in['sup_w'], 'L1_ffn_sdown_w': _L1_ffn_in['sdown_w']}

def reference(x, ctx_768, mask_BxS2_bk0, g_xattn, g_ffn, L0_xattn_Wq, L0_xattn_Wk, L0_xattn_Wv, L0_xattn_Wo, L0_xattn_bo, L0_ffn_wf, L0_ffn_uf, L0_ffn_bf, L0_ffn_wi, L0_ffn_ui, L0_ffn_bi, L0_ffn_wc, L0_ffn_uc, L0_ffn_bc, L0_ffn_wo, L0_ffn_uo, L0_ffn_bo, L0_ffn_in_c, L1_xattn_ln_x_g, L1_xattn_ln_x_b, L1_xattn_ln_l_g, L1_xattn_ln_l_b, L1_xattn_qn_g, L1_xattn_kn_g, L1_xattn_Wq, L1_xattn_Wkv, L1_xattn_Wlkv, L1_xattn_Wo, L1_xattn_bo, L1_ffn_router_w, L1_ffn_router_bias, L1_ffn_gate_w, L1_ffn_up_w, L1_ffn_down_w, L1_ffn_sgate_w, L1_ffn_sup_w, L1_ffn_sdown_w):
    import jax
    import jax.numpy as jnp

    def _L0_xattn_ref(x, context, Wq, Wk, Wv, Wo, bo):
        import jax, jax.numpy as jnp
        import numpy as np
        HEADS = 8
        DIM_HEAD = 64
        QUERY_DIM = 256
        CONTEXT_DIM = 192
        INNER = HEADS * DIM_HEAD
        B, Sq, _ = x.shape
        h, d = (HEADS, DIM_HEAD)
        scale = d ** (-0.5)
        q = (x @ Wq).reshape(B, Sq, h, d).transpose(0, 2, 1, 3)
        k = (context @ Wk).reshape(B, -1, h, d).transpose(0, 2, 1, 3)
        v = (context @ Wv).reshape(B, -1, h, d).transpose(0, 2, 1, 3)
        scores = jnp.einsum('bhid,bhjd->bhij', q, k) * scale
        attn = jax.nn.softmax(scores, axis=-1)
        out = jnp.einsum('bhij,bhjd->bhid', attn, v)
        out = out.transpose(0, 2, 1, 3).reshape(B, Sq, h * d)
        return out @ Wo + bo

    def _L0_ffn_ref(x, wf, uf, bf, wi, ui, bi, wc, uc, bc, wo, uo, bo, in_c):
        import jax, jax.numpy as jnp
        import numpy as np
        from jax import lax
        T, B, I, M, O = (64, 64, 256, 256, 256)

        def _xavier(key, shape):
            fan_out, fan_in = shape
            limit = float(np.sqrt(6.0 / (fan_in + fan_out)))
            return jax.random.uniform(key, shape, jnp.float32, -limit, limit)
        batch = x.shape[1]
        c0 = jnp.broadcast_to(in_c, (batch, in_c.shape[0]))

        def step(c, xt):
            ft = jax.nn.sigmoid(xt @ wf.T + c @ uf.T + bf)
            it = jax.nn.sigmoid(xt @ wi.T + c @ ui.T + bi)
            gt = jnp.tanh(xt @ wc.T + c @ uc.T + bc)
            c = ft * c + it * gt
            return (c, None)
        c_final, _ = lax.scan(step, c0, x)
        h = jnp.tanh(jnp.einsum('tbi,oi->tbo', x, wo) + c_final @ uo.T + bo)
        return h

    def _L1_xattn_ref(x, latents, mask, ln_x_g, ln_x_b, ln_l_g, ln_l_b, qn_g, kn_g, Wq, Wkv, Wlkv, Wo, bo):
        import jax, jax.numpy as jnp
        import numpy as np
        DIM_IN, DIM_LAT, DIM_HEAD = (192, 256, 64)
        INNER = max(DIM_LAT, DIM_IN)
        HEADS = INNER // DIM_HEAD
        SCALE = DIM_HEAD ** (-0.5)
        RMS_EPS = 1e-08
        LN_EPS = 1e-05

        def layernorm(x, g, b):
            mu = jnp.mean(x, axis=-1, keepdims=True)
            var = jnp.mean((x - mu) ** 2, axis=-1, keepdims=True)
            return (x - mu) * jax.lax.rsqrt(var + LN_EPS) * g + b

        def rmsnorm(x, gamma):
            norm = jnp.sqrt(jnp.sum(x * x, axis=-1, keepdims=True)) * x.shape[-1] ** (-0.5)
            return x / jnp.maximum(norm, RMS_EPS) * gamma
        b, n, _ = x.shape
        m = latents.shape[1]
        xn = layernorm(x, ln_x_g, ln_x_b)
        ln = layernorm(latents, ln_l_g, ln_l_b)
        q = ln @ Wq.T
        kv = jnp.concatenate([xn @ Wkv.T, ln @ Wlkv.T], axis=1)
        k, v = (kv[..., :INNER], kv[..., INNER:])
        split_heads = lambda t: t.reshape(t.shape[0], t.shape[1], HEADS, DIM_HEAD).transpose(0, 2, 1, 3)
        q, k, v = (split_heads(q), split_heads(k), split_heads(v))
        qn = rmsnorm(q, qn_g) * SCALE
        kn = rmsnorm(k, kn_g)
        attn = jnp.einsum('bhid,bhjd->bhij', qn, kn)
        full_mask = jnp.pad(mask, ((0, 0), (0, m)), constant_values=True)
        attn = jnp.where(full_mask[:, None, None, :], attn, -jnp.finfo(attn.dtype).max)
        attn = jax.nn.softmax(attn, axis=-1)
        out = jnp.einsum('bhij,bhjd->bhid', attn, v)
        out = out.transpose(0, 2, 1, 3).reshape(b, m, INNER)
        return out @ Wo.T + bo

    def _L1_ffn_ref(x, router_w, router_bias, gate_w, up_w, down_w, sgate_w, sup_w, sdown_w):
        import jax, jax.numpy as jnp
        import numpy as np
        TOPK = 4
        B, T, D = x.shape
        flat = x.reshape(B * T, D)
        logits = flat.astype(jnp.float32) @ router_w.T + router_bias
        scores = jax.nn.softmax(logits, axis=-1)
        topk_scores, topk_idx = jax.lax.top_k(scores, TOPK)
        topk_scores = topk_scores / jnp.clip(topk_scores.sum(axis=-1, keepdims=True), 1e-12, None)
        h = jax.nn.silu(jnp.einsum('nd,ehd->neh', flat, gate_w)) * jnp.einsum('nd,ehd->neh', flat, up_w)
        expert_out = jnp.einsum('neh,edh->ned', h, down_w)
        sel = jnp.take_along_axis(expert_out, topk_idx[:, :, None], axis=1)
        out = (sel * topk_scores.astype(flat.dtype)[:, :, None]).sum(axis=1)
        out = out + jax.nn.silu(flat @ sgate_w.T) * (flat @ sup_w.T) @ sdown_w.T
        return out.reshape(B, T, D)
    x = x + jnp.tanh(g_xattn[0]) * _L0_xattn_ref(_layernorm(x, axis=-1), ctx_768, L0_xattn_Wq, L0_xattn_Wk, L0_xattn_Wv, L0_xattn_Wo, L0_xattn_bo)
    x = x + jnp.tanh(g_ffn[0]) * _L0_ffn_ref(_layernorm(x, axis=-1), L0_ffn_wf, L0_ffn_uf, L0_ffn_bf, L0_ffn_wi, L0_ffn_ui, L0_ffn_bi, L0_ffn_wc, L0_ffn_uc, L0_ffn_bc, L0_ffn_wo, L0_ffn_uo, L0_ffn_bo, L0_ffn_in_c)
    x = x + jnp.tanh(g_xattn[1]) * _L1_xattn_ref(ctx_768, _layernorm(x, axis=-1), mask_BxS2_bk0, L1_xattn_ln_x_g, L1_xattn_ln_x_b, L1_xattn_ln_l_g, L1_xattn_ln_l_b, L1_xattn_qn_g, L1_xattn_kn_g, L1_xattn_Wq, L1_xattn_Wkv, L1_xattn_Wlkv, L1_xattn_Wo, L1_xattn_bo)
    x = x + jnp.tanh(g_ffn[1]) * _L1_ffn_ref(_layernorm(x, axis=-1), L1_ffn_router_w, L1_ffn_router_bias, L1_ffn_gate_w, L1_ffn_up_w, L1_ffn_down_w, L1_ffn_sgate_w, L1_ffn_sup_w, L1_ffn_sdown_w)
    return x

_drawn_inputs = setup_inputs


def setup_inputs(seed=0):
    import zlib

    import numpy as np

    out = dict(_drawn_inputs(seed))
    spreads = {'g_ffn': (-1.0, 0.2),
     'L0_ffn_bf': (0.0, 0.578),
     'L0_ffn_bi': (0.0, 0.462),
     'L0_ffn_bc': (0.0, 0.1),
     'L0_ffn_bo': (0.0, 0.1),
     'L0_ffn_in_c': (0.0, 0.696),
     'L1_xattn_ln_x_g': (1.0, 0.2),
     'L1_xattn_ln_x_b': (0.0, 0.1),
     'L1_xattn_ln_l_g': (1.0, 0.2),
     'L1_xattn_ln_l_b': (0.0, 0.1),
     'L1_xattn_qn_g': (1.0, 0.2),
     'L1_xattn_kn_g': (1.0, 0.2),
     'L1_xattn_bo': (0.0, 0.1),
     'L1_ffn_router_bias': (0.0, 0.1)}
    factors = {'L0_xattn_bo': 3.636}
    for name, (base, spread) in spreads.items():
        noise = np.random.default_rng([zlib.crc32(name.encode()), seed]).standard_normal(out[name].shape)
        drawn = base * np.exp(spread * noise) if base else spread * noise
        out[name] = jnp.asarray(drawn.astype(out[name].dtype))
    for name, factor in factors.items():
        out[name] = (out[name] * factor).astype(out[name].dtype)
    return out
```

```python
import concourse.bass as bass
from concourse import mybir
from contextlib import ExitStack

NB = 8
S = 100
D = 256
KD = D // 128
C = 192
CR = C - 128
L = 361
LT = 3
LP = LT * 128
LR = L - 2 * 128
H0 = 8
H1 = 4
DH = 64
I0 = H0 * DH
I1 = H1 * DH
NK1 = LP + S
NE = 32
NSH = 4
TOK = NB * S
HALF = TOK // 2
BIG = 1e30


class Jobs:

    def __init__(self, banks, seq):
        self.banks = banks
        self.at = {}
        self.eng = {}
        self.left = []
        count = {"act": 0, "dve": 0}
        for n, (key, eng) in enumerate(seq):
            count[eng] += 1
            self.at[key] = n
            self.eng[key] = (eng, count[eng])
            self.left.append((eng, count[eng]))
        self.total = dict(count)

    def bank(self, key):
        return self.banks[self.at[key] % len(self.banks)]

    def done(self, key):
        return self.at[key] + 1

    def emptied(self, key):
        return self.eng[key]

    def before(self, key):
        n = self.at[key] - len(self.banks)
        return self.left[n] if n >= 0 else None


def build(nc, x, ctx, ctx_t, mask, rows, gate_rows, cols, wq0, wk0, wv0, wo0, wffn, wlat, wctx, wo1, wrt, wmoe,
          ident_in, sel_in, out):
    F = mybir.dt.float32
    BF = mybir.dt.bfloat16
    ALU = mybir.AluOpType
    ACT = mybir.ActivationFunctionType
    AX = mybir.AxisListType

    with ExitStack() as stack:
        def sb(name, shape, dt=F):
            return stack.enter_context(nc.sbuf_tensor(name, shape, dt))

        def sem(name):
            return stack.enter_context(nc.semaphore(name))

        ident = sb("ident", [128, 128])
        identb = sb("identb", [128, 128], BF)
        ROWS = 4 + 3 * D + NE
        rowb = sb("rowb", [128, ROWS])
        gbias = sb("gbias", [1, 3 * D])
        ones = sb("ones", [1, 128])
        onesb = sb("onesb", [1, 128], BF)
        maskb = sb("maskb", [1, NB, NK1], BF)
        mask8 = sb("mask8", [1, NB, L], mybir.dt.uint8)
        colv = sb("colv", [128, 12])
        gains = sb("gains", [128, 4])
        qk_gain = sb("qk_gain", [128, 1])
        nhalf = sb("nhalf", [128, 16])
        X = sb("X", [S, NB, D])
        XN = sb("XN", [S, NB, D])
        xT = sb("xT", [128, KD, TOK])
        yT = xT
        W0 = sb("W0", [128, 8 * I0])
        Wq0 = W0[:, 0:2 * I0].rearrange("p (k n) -> p k n", k=KD)
        Wk0 = W0[:, 2 * I0:4 * I0].rearrange("p (k n) -> p k n", k=2)
        Wv0 = W0[:, 4 * I0:6 * I0].rearrange("p (k n) -> p k n", k=2)
        Wo0 = W0[:, 6 * I0:8 * I0].rearrange("p (k n) -> p k n", k=I0 // 128)
        wexp = W0[:, 0:6 * D].rearrange("p (s n) -> p s n", s=2)
        sel = W0[0:96, 6 * D:6 * D + NE * 64].bitcast(BF)
        WF = sb("WF", [128, 8, KD, D])
        Wlat = sb("Wlat", [128, KD, 3 * I1])
        Wctx = sb("Wctx", [128, 2, 2 * I1])
        Wo1 = sb("Wo1", [128, KD, D])
        Wrt = sb("Wrt", [128, KD, NE])
        kT1 = sb("kT1", [128, NB, KD, NK1])
        V1 = sb("V1", [128, NB, LT + 1, I1])
        k1flat = kT1[:, :, :, :].rearrange("p b k n -> p (b k n)")
        cT = k1flat[:, 0:4 * L].rearrange("p (s k n) -> p s k n", s=2, k=2)
        qT0 = k1flat[:, 4 * L:4 * L + 8 * S].rearrange("p (s c n) -> p s c n", s=2, c=4)
        xnT0 = k1flat[:, 4 * L + 8 * S:4 * L + 12 * S].rearrange("p (s k n) -> p s k n", s=2, k=KD)
        sil = k1flat[:, 0:TOK].rearrange("p (h n) -> p h n", h=2)
        wbs = k1flat[:, TOK:2 * TOK].rearrange("p (h n) -> p h n", h=2)
        hid = k1flat[:, 2 * TOK:3 * TOK].rearrange("p (h n) -> p h n", h=2)
        resT = k1flat[:, 3 * TOK:5 * TOK].rearrange("p (k n) -> p k n", k=KD)
        U = sb("U", [128, 2 * LT * C + 3 * 2 * LT * I1])
        o = 2 * LT * C
        ctok = U[:, 0:o].rearrange("p (s t n) -> p s t n", s=2, t=LT)
        kraw = U[:, o:o + 2 * LT * I1].rearrange("p (s t n) -> p s t n", s=2, t=LT)
        o += 2 * LT * I1
        ksq = U[:, o:o + 2 * LT * I1].rearrange("p (s t n) -> p s t n", s=2, t=LT)
        kn = ksq
        o += 2 * LT * I1
        cnT = U[:, o:o + 4 * LP].rearrange("p (s k n) -> p s k n", s=2, k=2)
        qT1 = U[:, 0:NB * KD * S].rearrange("p (b k n) -> p b k n", b=NB, k=KD)
        o = NB * KD * S

        def rows_of(n, width, parts=S):
            nonlocal o
            o += width
            return U[0:parts, o - width:o]

        logit = rows_of(S, NB * NE).rearrange("p (b n) -> p b n", b=NB)
        prob = rows_of(S, NB * (NE + 8)).rearrange("p (b n) -> p b n", b=NB)
        rest = rows_of(S, NB * (NE + 8)).rearrange("p (b n) -> p b n", b=NB)
        w3f = rows_of(S, NB * 3 * NE).rearrange("p (b i n) -> p b i n", b=NB, i=3)
        w3b = rows_of(S, NB * 3 * NE // 2).bitcast(BF).rearrange("p (b n) -> p b n", b=NB)
        wT3 = rows_of(S, TOK // 2, 96).bitcast(BF)
        v1flat = V1[:, :, :, :].rearrange("p b t n -> p (b t n)")
        KT0 = 4 * L
        V0 = LT * I0
        kT0 = [v1flat[:, s * KT0:(s + 1) * KT0].rearrange("p (c n) -> p c n", c=4) for s in range(2)]
        v0 = [v1flat[:, 2 * KT0 + s * V0:2 * KT0 + (s + 1) * V0].rearrange("p (t n) -> p t n", t=LT) for s in range(2)]
        P = sb("P", [S, 2, 512])
        PTs = sb("PTs", [128, 2, 4 * S])
        osb = sb("osb", [S, 2, I0])
        oT = sb("oT", [128, 2, 4, S])
        gate_s = sb("gate_s", [128, 2, 4, S])
        gate_t = sb("gate_t", [128, 2, 2, S])
        fc = sb("fc", [128, 2, S])
        ig = sb("ig", [128, 2, S])
        cell = sb("cell", [128, 2, KD, S])
        cu = sb("cu", [S, D])
        XW = sb("XW", [S, NB, D])
        wfl = WF[:, :, :, :].rearrange("p g k n -> p (g k n)")
        qkraw = wfl[0:S, :].rearrange("p (b n) -> p b n", b=NB)
        bn = sb("bn", [128, NB, 6])
        mv = sb("mv", [128, NB, 2])
        rstd = sb("rstd", [128, NB])
        bn1 = sb("bn1", [128, NB, 6])
        mv1 = sb("mv1", [128, NB, 2])
        rstd1 = sb("rstd1", [128, NB])
        bn2 = sb("bn2", [128, NB, 6])
        mv2 = sb("mv2", [128, NB, 2])
        rstd2 = sb("rstd2", [128, NB])
        bn3 = sb("bn3", [128, NB, 6])
        mv3 = sb("mv3", [128, NB, 2])
        rstd3 = sb("rstd3", [128, NB])
        bn4 = sb("bn4", [128, NB, 6])
        mv4 = sb("mv4", [128, NB, 2])
        rstd4 = sb("rstd4", [128, NB])
        bnc = sb("bnc", [128, 2, LT, 6])
        mvc = sb("mvc", [128, 2, LT, 2])
        rstdc = sb("rstdc", [128, 2, LT])
        ssk = sb("ssk", [128, 2, LT * H1])
        rk = sb("rk", [128, 2, LT * H1])
        ssq = sb("ssq", [S, NB, 8])
        rq = sb("rq", [S, NB, 8])
        nmax = sb("nmax", [S, 96])
        psum_ = sb("psum_", [S, 96])
        rden = sb("rden", [S, 96])
        bob = sb("bob", [S, 3, D])
        top = sb("top", [S, NB, 8])
        lmax = sb("lmax", [S, NB])
        lsum = sb("lsum", [S, NB])
        lrec = sb("lrec", [S, NB])
        bank = [stack.enter_context(nc.psum_tensor(f"bank{i}", [128, 512], F)) for i in range(8)]

        ld_x = sem("ld_x")
        ld_small = sem("ld_small")
        ld_w0 = sem("ld_w0")
        ld_wf = sem("ld_wf")
        ld_w1 = sem("ld_w1")
        ld_ct = [sem("ld_ct0"), sem("ld_ct1")]
        ld_ck = [sem("ld_ck0"), sem("ld_ck1")]
        ld_we = [sem("ld_we0"), sem("ld_we1")]
        init = sem("init")
        initv = sem("initv")
        link = sem("link")
        plink = sem("plink")
        tanh_g = sem("tanh_g")
        st0 = sem("st0")
        rs0 = sem("rs0")
        xn0 = sem("xn0")
        j1 = sem("j1")
        e1a = sem("e1a")
        e1v = sem("e1v")
        scored = sem("scored")
        maxed = sem("maxed")
        expd = sem("expd")
        ptd = sem("ptd")
        pt_out = sem("pt_out")
        pvd = sem("pvd")
        normed = sem("normed")
        st1 = sem("st1")
        rs1 = sem("rs1")
        xn1 = sem("xn1")
        j2 = sem("j2")
        e2a = sem("e2a")
        e2v = sem("e2v")
        gated = sem("gated")
        sigd = sem("sigd")
        tand = sem("tand")
        celld = sem("celld")
        cst = sem("cst")
        crs = sem("crs")
        cnd = sem("cnd")
        ksqd = sem("ksqd")
        kss = sem("kss")
        knd = sem("knd")
        cud = sem("cud")
        cuv = sem("cuv")
        hpre = sem("hpre")
        htan = sem("htan")
        st2 = sem("st2")
        rs2 = sem("rs2")
        st3 = sem("st3")
        rs3 = sem("rs3")
        z2d = sem("z2d")
        j3 = sem("j3")
        e3a = sem("e3a")
        e3v = sem("e3v")
        qss = sem("qss")
        qrs = sem("qrs")
        qknd = sem("qknd")
        st4 = sem("st4")
        rs4 = sem("rs4")
        y4 = sem("y4")
        j4 = sem("j4")
        e4v = sem("e4v")
        lsub = sem("lsub")
        lexp = sem("lexp")
        w3r = sem("w3r")
        g_ready = sem("g_ready")
        u_ready = sem("u_ready")
        wb_ready = sem("wb_ready")
        sild = sem("sild")
        wbd = sem("wbd")
        hidd = sem("hidd")
        downd = sem("downd")
        oev = sem("oev")
        jf = sem("jf")
        fin = sem("fin")
        stored = sem("stored")

        J1E = {0: "dve", 1: "act", 2: "act", 3: "dve", 4: "act", 5: "act", 6: "act", 7: "dve", 8: "act", 9: "dve", 10: "dve"}
        seq = []
        for b in range(NB + 1):
            if b < NB:
                seq += [((b, j), J1E[j]) for j in range(9)]
            if b > 0:
                seq += [((b - 1, j), J1E[j]) for j in (9, 10)]
        J1 = Jobs(bank[0:2], seq)
        seq = [(("xt", b), "dve") for b in range(NB)] + [(("ct", 0, i), "dve") for i in range(LT)]
        for t in range(NB + 1):
            if t < NB:
                seq += [(("hx", t), "act")]
            if t + 1 < NB:
                seq += [(("ct", t + 1, i), "dve") for i in range(LT)]
            if t < NB:
                seq += [(("kv", t, i), "act") for i in range(LT)]
            if t > 0:
                seq += [(("kt", t - 1, i), "dve") for i in range(LT)]
        J2 = Jobs(bank[4:8], seq)
        seq = []
        for r in range(-2, NB + 1):
            if 0 <= r + 2 < NB:
                seq += [(("zt", r + 2), "dve"), (("qk", r + 2), "act"), (("vl", r + 2), "act")]
            if 0 <= r + 1 < NB:
                seq += [(("qt", r + 1), "dve")]
            if 0 <= r - 1 < NB:
                seq += [(("ot", r - 1), "dve"), (("wo", r - 1), "dve")]
        J3 = Jobs(bank[0:2], seq)
        HEADS0 = NB * H0

        block = stack.enter_context(nc.Block())

        def gate(i):
            return gains[:, i:i + 1]

        @block.sync
        def _(sp):
            def load_ct(b):
                s = b % 2
                if b >= 2:
                    sp.wait_ge(j1, J1.done((b - 2, 8)))
                sp.dma_start(cT[:, s, 0, :], ctx_t[0:128, b, :]).then_inc(ld_ct[s], 16)
                sp.dma_start(cT[0:CR, s, 1, :], ctx_t[128:C, b, :]).then_inc(ld_ct[s], 16)

            def load_ck(b):
                s = b % 2
                if b == 0:
                    sp.wait_ge(init, 8)
                if b >= 2:
                    sp.wait_ge(j2, J2.done(("ct", b - 2, LT - 1)))
                sp.dma_start(ctok[:, s, 0:2, :], ctx[b, 0:256, :].rearrange("(t p) c -> p t c", p=128)).then_inc(ld_ck[s], 16)
                sp.dma_start(ctok[0:LR, s, 2, :], ctx[b, 256:L, :]).then_inc(ld_ck[s], 16)

            sp.dma_start(X[:, :, :], x.rearrange("b s d -> s b d")).then_inc(ld_x, 16)
            sp.dma_start(ident[:, :], ident_in).then_inc(ld_x, 16)
            sp.dma_start(Wq0[:, :, :], wq0.rearrange("(k p) n -> p k n", p=128)).then_inc(ld_w0, 16)
            load_ct(0)
            sp.dma_start(Wk0[:, 0, :], wk0[0:128, :]).then_inc(ld_w0, 16)
            sp.dma_start(Wk0[0:CR, 1, :], wk0[128:C, :]).then_inc(ld_w0, 16)
            sp.dma_start(Wv0[:, 0, :], wv0[0:128, :]).then_inc(ld_w0, 16)
            sp.dma_start(Wv0[0:CR, 1, :], wv0[128:C, :]).then_inc(ld_w0, 16)
            sp.dma_start(Wo0[:, :, :], wo0.rearrange("(k p) n -> p k n", p=128)).then_inc(ld_w0, 16)
            load_ct(1)
            sp.dma_start(WF[:, :, :, :], wffn.rearrange("g (k p) n -> p g k n", p=128)).then_inc(ld_wf, 16)
            sp.dma_start(Wctx[:, 0, :], wctx[0:128, :]).then_inc(ld_w1, 16)
            sp.dma_start(Wctx[0:CR, 1, :], wctx[128:C, :]).then_inc(ld_w1, 16)
            sp.dma_start(Wlat[:, :, :], wlat.rearrange("(k p) n -> p k n", p=128)).then_inc(ld_w1, 16)
            sp.dma_start(Wo1[:, :, :], wo1.rearrange("(k p) n -> p k n", p=128)).then_inc(ld_w1, 16)
            sp.dma_start(Wrt[:, :, :], wrt.rearrange("(k p) n -> p k n", p=128)).then_inc(ld_w1, 16)
            load_ck(0)
            load_ck(1)
            for b in range(2, NB):
                load_ct(b)
            for b in range(2, NB):
                load_ck(b)
            sp.wait_ge(j1, len(J1.left))
            sp.dma_start(sel, sel_in).then_inc(ld_w1, 16)
            for e in range(2):
                sp.dma_start(wexp[:, e, :], wmoe[e, :, :]).then_inc(ld_we[e], 16)
            for e in range(2, NSH):
                sp.wait_ge(downd, 2 * (e - 1))
                sp.dma_start(wexp[:, e % 2, :], wmoe[e, :, :]).then_inc(ld_we[e % 2], 16)
            with sp.Fori(NSH // 2, (NSH + NE) // 2) as i:
                for s in range(2):
                    sp.wait_ge(downd, 4 * i + (2 * s - 2))
                    sp.dma_start(wexp[:, s, :], wmoe[bass.ds(2 * i + s, 1), :, :].rearrange("a p n -> p (a n)")).then_inc(ld_we[s], 16)
            for b in range(NB):
                sp.wait_ge(fin, b + 1)
                sp.dma_start(out[b, :, :], X[:, b, :]).then_inc(stored, 16)
            sp.wait_ge(stored, 16 * NB)

        @block.gpsimd
        def _(pool):
            chain = [0]

            def own(ins):
                chain[0] += 1
                ins.then_inc(plink, 1)
                pool.wait_ge(plink, chain[0])

            pool.dma_start(rowb[:, :], rows.partition_broadcast(128)).then_inc(ld_small, 16)
            pool.dma_start(colv[:, :], cols).then_inc(ld_small, 16)
            pool.dma_start(gbias[:, :], gate_rows).then_inc(ld_small, 16)
            pool.dma_start(mask8[:, :, :], mask).then_inc(ld_small, 16)
            pool.memset(nhalf[:, :], -0.5).then_inc(init, 1)
            pool.memset(ones[:, :], 1.0).then_inc(init, 1)
            pool.memset(onesb[:, :], 1.0).then_inc(init, 1)
            pool.memset(P[:, :, :], 0.0).then_inc(init, 1)
            pool.memset(kraw[:, :, :, :], 0.0).then_inc(init, 1)
            pool.memset(ctok[:, :, :, :], 0.0).then_inc(init, 1)
            pool.memset(maskb[:, :, 0:LP], -BIG).then_inc(init, 1)
            pool.memset(maskb[:, :, LP:NK1], 0.0).then_inc(init, 1)
            pool.wait_ge(init, 8)
            pool.wait_ge(ld_small, 64)
            pool.tensor_scalar(maskb[:, :, 0:L], mask8[:, :, :], BIG, -BIG, ALU.mult, ALU.add).then_inc(init, 1)

            def power(dst, src, width, given, want, done):
                pool.wait_ge(given, want)
                pool.tensor_tensor(dst, src, nhalf[0:dst.shape[0], 0:width], ALU.pow).then_inc(done, 1)

            for b in range(NB):
                power(rstd[0:S, b:b + 1], mv[0:S, b, 1:2], 1, st0, b + 1, rs0)

            def context_scale(b):
                s = b % 2
                power(rstdc[:, s, :], mvc[:, s, :, 1], LT, cst, b + 1, crs)

            for b in range(NB):
                power(rstd1[0:S, b:b + 1], mv1[0:S, b, 1:2], 1, st1, b + 1, rs1)
            context_scale(0)
            for t in range(NB + 1):
                if t + 1 < NB:
                    context_scale(t + 1)
                if t > 0:
                    b = t - 1
                    s = b % 2
                    pool.wait_ge(e2a, J2.emptied(("kv", b, LT - 1))[1])
                    pool.tensor_tensor(ksq[:, s, :, :], kraw[:, s, :, :], kraw[:, s, :, :], ALU.mult).then_inc(ksqd, 1)
                    pool.wait_ge(kss, b + 1)
                    own(pool.tensor_tensor(rk[:, s, :], ssk[:, s, :], nhalf[:, 0:LT * H1], ALU.pow))
                    if b >= 2:
                        pool.wait_ge(j2, J2.done(("kt", b - 2, LT - 1)))
                    pool.tensor_tensor(kn[:, s, :, :].rearrange("p t (h d) -> p (t h) d", d=DH),
                                       kraw[:, s, :, :].rearrange("p t (h d) -> p (t h) d", d=DH),
                                       rk[:, s, :].unsqueeze(2).broadcast_to([128, LT * H1, DH]), ALU.mult).then_inc(knd, 1)
            for b in range(NB):
                power(rstd2[0:S, b:b + 1], mv2[0:S, b, 1:2], 1, st2, b + 1, rs2)
            for b in range(NB):
                power(rstd3[0:S, b:b + 1], mv3[0:S, b, 1:2], 1, st3, b + 1, rs3)
            for b in range(NB):
                power(rq[:, b, :], ssq[:, b, :], 8, qss, b + 1, qrs)
            for b in range(NB):
                power(rstd4[0:S, b:b + 1], mv4[0:S, b, 1:2], 1, st4, b + 1, rs4)

        @block.tensor
        def _(pe):
            def empty(jobs, key, ev):
                before = jobs.before(key)
                if before:
                    pe.wait_ge(ev[before[0]], before[1])

            def emptied(jobs, key, ev):
                eng, n = jobs.emptied(key)
                pe.wait_ge(ev[eng], n)

            E1 = {"act": e1a, "dve": e1v}
            E2 = {"act": e2a, "dve": e2v}
            E3 = {"act": e3a, "dve": e3v}

            def head(g, q, k, nk, mask_row):
                if g >= 2:
                    pe.wait_ge(expd, g - 1)
                dst = bank[2 + g % 2][0:S, 0:nk]
                if mask_row is not None:
                    pe.matmul(dst, onesb[0:1, 0:S], mask_row, start=True, stop=False)
                pe.matmul(dst, q, k, start=mask_row is None, stop=True).then_inc(scored, 1)

            def turn(g, tiles):
                pe.wait_ge(expd, g + 1)
                if g >= 2:
                    pe.wait_ge(pt_out, g - 1)
                for i in range(tiles):
                    m = pe.transpose(bank[4 + g % 2][:, i * S:(i + 1) * S], P[:, g % 2, i * 128:(i + 1) * 128], ident[0:S, 0:S])
                m.then_inc(ptd, 1)

            def values(g, h, bt, vals, rows_):
                pe.wait_ge(pt_out, g + 1)
                if h == 0 and bt >= 2:
                    pe.wait_ge(normed, bt - 1)
                n = len(rows_)
                for i in range(n):
                    k = rows_[i]
                    m = pe.matmul(bank[6 + bt % 2][0:S, h * DH:(h + 1) * DH], PTs[0:k, g % 2, i * S:(i + 1) * S], vals(i, k),
                                  start=i == 0, stop=i == n - 1)
                m.then_inc(pvd, 1)

            pe.wait_ge(ld_x, 32)

            def project(b):
                s = b % 2
                key = (b, 0)
                pe.wait_ge(xn0, b + 1)
                empty(J1, key, E1)
                for k in range(KD):
                    m = pe.transpose(J1.bank(key)[:, k * S:(k + 1) * S], XN[:, b, k * 128:(k + 1) * 128], ident[0:S, 0:S])
                m.then_inc(j1, 1)
                if b == 0:
                    pe.wait_ge(ld_w0, 96)
                key = (b, 1)
                emptied(J1, (b, 0), E1)
                empty(J1, key, E1)
                for c in range(4):
                    for k in range(KD):
                        m = pe.matmul(J1.bank(key)[:, c * S:(c + 1) * S], Wq0[:, k, c * 128:(c + 1) * 128], xnT0[:, s, k, :],
                                      start=k == 0, stop=k == KD - 1)
                m.then_inc(j1, 1)
                pe.wait_ge(ld_ct[s], 32 * (b // 2 + 1))
                for c in range(4):
                    key = (b, 2 + c)
                    empty(J1, key, E1)
                    for k, r in ((0, 128), (1, CR)):
                        m = pe.matmul(J1.bank(key)[:, 0:L], Wk0[0:r, k, c * 128:(c + 1) * 128], cT[0:r, s, k, :],
                                      start=k == 0, stop=k == 1)
                    m.then_inc(j1, 1)
                for i in range(LT):
                    key = (b, 6 + i)
                    n = min(128, L - i * 128)
                    empty(J1, key, E1)
                    for k, r in ((0, 128), (1, CR)):
                        m = pe.matmul(J1.bank(key)[0:n, :], cT[0:r, s, k, i * 128:i * 128 + n], Wv0[0:r, k, :],
                                      start=k == 0, stop=k == 1)
                    m.then_inc(j1, 1)

            def output0(b):
                s = b % 2
                key = (b, 9)
                pe.wait_ge(normed, b + 1)
                empty(J1, key, E1)
                for c in range(4):
                    m = pe.transpose(J1.bank(key)[:, c * S:(c + 1) * S], osb[:, s, c * 128:(c + 1) * 128], ident[0:S, 0:S])
                m.then_inc(j1, 1)
                emptied(J1, key, E1)
                key = (b, 10)
                empty(J1, key, E1)
                for c in range(4):
                    m = pe.matmul(J1.bank(key)[0:S, 0:D], oT[:, s, c, :], Wo0[:, c, :], start=c == 0, stop=c == 3)
                m.then_inc(j1, 1)

            def attend0(b):
                s = b % 2
                for j in range(1, 9):
                    emptied(J1, (b, j), E1)

                def sc(h):
                    o = 64 * (h % 2)
                    head(b * H0 + h, qT0[o:o + 64, s, h // 2, :], kT0[s][o:o + 64, h // 2, :], L, None)

                def pv(h):
                    values(b * H0 + h, h, b, lambda i, k: v0[s][0:k, i, h * DH:(h + 1) * DH], [128, 128, LR])

                sc(0)
                sc(1)
                for h in range(H0):
                    turn(b * H0 + h, LT)
                    if h + 2 < H0:
                        sc(h + 2)
                    if h:
                        pv(h - 1)
                pv(H0 - 1)

            pe.wait_ge(init, 8)
            for b in range(NB):
                project(b)
                if b:
                    output0(b - 1)
                attend0(b)
            output0(NB - 1)

            pe.wait_ge(ld_wf, 16)
            pe.wait_ge(ld_w1, 80)
            pe.wait_ge(ld_small, 64)
            pe.wait_ge(e1v, J1.total["dve"])
            pe.wait_ge(e1a, J1.total["act"])
            pe.wait_ge(pt_out, HEADS0)
            pe.wait_ge(expd, HEADS0)
            pe.wait_ge(normed, NB)
            for b in range(NB):
                key = ("xt", b)
                pe.wait_ge(xn1, b + 1)
                empty(J2, key, E2)
                for k in range(KD):
                    m = pe.transpose(J2.bank(key)[:, k * S:(k + 1) * S], XN[:, b, k * 128:(k + 1) * 128], ident[0:S, 0:S])
                m.then_inc(j2, 1)

            def context_turn(b):
                s = b % 2
                pe.wait_ge(cnd, b + 1)
                for i in range(LT):
                    key = ("ct", b, i)
                    empty(J2, key, E2)
                    for k, r in ((0, 128), (1, CR)):
                        m = pe.transpose(J2.bank(key)[0:r, k * 128:(k + 1) * 128], ctok[:, s, i, k * 128:k * 128 + r], ident[:, :])
                    m.then_inc(j2, 1)

            def context_kv(b):
                s = b % 2
                for i in range(LT):
                    key = ("kv", b, i)
                    n = min(128, L - i * 128)
                    emptied(J2, ("ct", b, i), E2)
                    empty(J2, key, E2)
                    for k, r in ((0, 128), (1, CR)):
                        m = pe.matmul(J2.bank(key)[0:n, :], cnT[0:r, s, k, i * 128:i * 128 + n], Wctx[0:r, k, :],
                                      start=k == 0, stop=k == 1)
                    m.then_inc(j2, 1)

            def key_turn(b):
                s = b % 2
                pe.wait_ge(knd, b + 1)
                for i in range(LT):
                    key = ("kt", b, i)
                    empty(J2, key, E2)
                    for k in range(KD):
                        m = pe.transpose(J2.bank(key)[:, k * 128:(k + 1) * 128], kn[:, s, i, k * 128:(k + 1) * 128], ident[:, :])
                    m.then_inc(j2, 1)

            def gates_x(t):
                if t >= 2:
                    pe.wait_ge(sigd, t - 1)
                    pe.wait_ge(tand, t - 1)
                for g in range(3):
                    for m in range(KD):
                        dst = bank[2 * (t % 2) + g // 2][:, ((g % 2) * KD + m) * S:((g % 2) * KD + m + 1) * S]
                        pe.matmul(dst, gbias[0:1, g * D + m * 128:g * D + (m + 1) * 128], ones[0:1, 0:S],
                                  start=m == 0 and g != 1, stop=False, skip_group_check=True)
                        for k in range(KD):
                            pe.matmul(dst, WF[:, g, k, m * 128:(m + 1) * 128], xT[:, k, t * S:(t + 1) * S],
                                      start=False, stop=False, skip_group_check=True)

            def gates_c(t):
                pe.wait_ge(celld, t + 1)
                for g in range(3):
                    for m in range(KD):
                        dst = bank[2 * (t % 2) + g // 2][:, ((g % 2) * KD + m) * S:((g % 2) * KD + m + 1) * S]
                        for k in range(KD):
                            last = pe.matmul(dst, WF[:, 3 + g, k, m * 128:(m + 1) * 128], cell[:, t % 2, k, :],
                                             start=False, stop=k == KD - 1, skip_group_check=True)
                    if g:
                        last.then_inc(gated, 1)

            context_turn(0)
            for b in range(NB):
                emptied(J2, ("xt", b), E2)
            gates_x(0)
            for t in range(NB):
                gates_c(t)
                if t + 1 < NB:
                    gates_x(t + 1)
                key = ("hx", t)
                empty(J2, key, E2)
                for k in range(KD):
                    m = pe.matmul(J2.bank(key)[0:S, 0:D], xT[:, k, t * S:(t + 1) * S], WF[:, 6, k, :], start=k == 0, stop=k == KD - 1)
                m.then_inc(j2, 1)
                if t + 1 < NB:
                    context_turn(t + 1)
                context_kv(t)
                if t > 0:
                    key_turn(t - 1)
            pe.wait_ge(celld, NB + 1)
            for k in range(KD):
                m = pe.matmul(bank[0][0:S, 0:D], cell[:, NB % 2, k, :], WF[:, 7, k, :], start=k == 0, stop=k == KD - 1)
            m.then_inc(cud, 1)
            key_turn(NB - 1)

            pe.wait_ge(cuv, 1)
            pe.wait_ge(e2v, J2.total["dve"])
            pe.wait_ge(e2a, J2.total["act"])
            pe.wait_ge(init, 9)

            def latents(b):
                s = b % 2
                key = ("zt", b)
                pe.wait_ge(z2d, b + 1)
                empty(J3, key, E3)
                for k in range(KD):
                    m = pe.transpose(J3.bank(key)[:, k * S:(k + 1) * S], XN[:, b, k * 128:(k + 1) * 128], ident[0:S, 0:S])
                m.then_inc(j3, 1)
                emptied(J3, key, E3)
                for key, c0, n in ((("qk", b), 0, 2 * I1), (("vl", b), 2 * I1, I1)):
                    empty(J3, key, E3)
                    for k in range(KD):
                        m = pe.matmul(J3.bank(key)[0:S, 0:n], xT[:, k, b * S:(b + 1) * S], Wlat[:, k, c0:c0 + n],
                                      start=k == 0, stop=k == KD - 1)
                    m.then_inc(j3, 1)

            def latent_turn(b):
                key = ("qt", b)
                pe.wait_ge(qknd, b + 1)
                empty(J3, key, E3)
                for c in range(4):
                    m = pe.transpose(J3.bank(key)[:, c * S:(c + 1) * S], qkraw[:, b, c * 128:(c + 1) * 128], ident[0:S, 0:S])
                m.then_inc(j3, 1)

            def attend1(b):
                emptied(J3, ("qt", b), E3)
                emptied(J3, ("vl", b), E3)
                bt = NB + b

                def sc(h):
                    o = 64 * (h % 2)
                    head(HEADS0 + b * H1 + h, qT1[o:o + 64, b, h // 2, :], kT1[o:o + 64, b, h // 2, :], NK1, maskb[0:1, b, :])

                def pv(h):
                    values(HEADS0 + b * H1 + h, h, bt, lambda i, k: V1[0:k, b, i, h * DH:(h + 1) * DH], [128, 128, LR, S])

                sc(0)
                sc(1)
                for h in range(H1):
                    turn(HEADS0 + b * H1 + h, 4)
                    if h + 2 < H1:
                        sc(h + 2)
                    if h:
                        pv(h - 1)
                pv(H1 - 1)

            def output1(b):
                s = b % 2
                key = ("ot", b)
                pe.wait_ge(normed, NB + b + 1)
                empty(J3, key, E3)
                for c in range(KD):
                    m = pe.transpose(J3.bank(key)[:, c * S:(c + 1) * S], osb[:, s, c * 128:(c + 1) * 128], ident[0:S, 0:S])
                m.then_inc(j3, 1)
                emptied(J3, key, E3)
                key = ("wo", b)
                empty(J3, key, E3)
                for c in range(KD):
                    m = pe.matmul(J3.bank(key)[0:S, 0:D], oT[:, s, c, :], Wo1[:, c, :], start=c == 0, stop=c == KD - 1)
                m.then_inc(j3, 1)

            for r in range(-2, NB + 1):
                if 0 <= r + 2 < NB:
                    latents(r + 2)
                if 0 <= r + 1 < NB:
                    latent_turn(r + 1)
                if 0 <= r - 1 < NB:
                    output1(r - 1)
                if 0 <= r < NB:
                    attend1(r)

            pe.wait_ge(e3v, J3.total["dve"])
            for b in range(NB):
                pe.wait_ge(y4, b + 1)
                if b >= 2:
                    pe.wait_ge(e4v, b - 1)
                for k in range(KD):
                    m = pe.transpose(bank[b % 2][:, k * S:(k + 1) * S], XN[:, b, k * 128:(k + 1) * 128], ident[0:S, 0:S])
                m.then_inc(j4, 1)
            for b in range(NB):
                pe.wait_ge(e4v, b + 1)
                for k in range(KD):
                    m = pe.matmul(bank[2][0:S, b * NE:(b + 1) * NE], yT[:, k, b * S:(b + 1) * S], Wrt[:, k, :],
                                  start=k == 0, stop=k == KD - 1)
            m.then_inc(j4, 1)
            pe.wait_ge(e4v, NB)

            acc = [[bank[4 + 2 * c + hf][:, 0:HALF] for hf in range(2)] for c in range(KD)]

            def expert(e, s, first, last, routed):
                for hf in range(2):
                    n = e * 2 + hf
                    lo = hf * HALF
                    if hf == 0:
                        pe.wait_ge(ld_we[s], (e - s) * 8 + 16)
                    if not first or hf:
                        pe.wait_ge(sild, n)
                    for k in range(KD):
                        m = pe.matmul(bank[0][:, 0:HALF], wexp[:, s, k * 128:(k + 1) * 128], yT[:, k, lo:lo + HALF],
                                      start=k == 0, stop=k == KD - 1)
                    m.then_inc(g_ready, 1)
                    if routed:
                        r = e - NSH
                        if routed != "first" or hf:
                            pe.wait_ge(wbd, r * 2 + hf)
                        pe.matmul(bank[3][:, 0:HALF], sel[:, bass.ds(r * 128, 128)], wT3[:, lo:lo + HALF],
                                  start=True, stop=True).then_inc(wb_ready, 1)
                    if not first or hf:
                        pe.wait_ge(hidd, n)
                    for k in range(KD):
                        m = pe.matmul(bank[1][:, 0:HALF], wexp[:, s, D + k * 128:D + (k + 1) * 128], yT[:, k, lo:lo + HALF],
                                      start=k == 0, stop=k == KD - 1)
                    m.then_inc(u_ready, 1)
                    pe.wait_ge(hidd, n + 1)
                    for c in range(KD):
                        m = pe.matmul(acc[c][hf], wexp[:, s, 2 * D + c * 128:2 * D + (c + 1) * 128], hid[:, hf, :],
                                      start=first, stop=last, skip_group_check=True)
                    m.then_inc(downd, 1)

            for e in range(NSH):
                expert(e, e % 2, e == 0, False, None)
            for b in range(NB):
                if b == 0:
                    pe.wait_ge(w3r, 1)
                if b >= 1:
                    pe.wait_ge(e4v, NB + b)
                pe.transpose(bank[3][:, :].bitcast(BF)[0:96, 0:S], w3b[:, b, :], identb[0:S, 0:S]).then_inc(j4, 1)
            pe.wait_ge(e4v, 2 * NB)
            pe.wait_ge(ld_w1, 96)
            expert(NSH, 0, False, False, "first")
            expert(NSH + 1, 1, False, False, "yes")
            with pe.Fori(NSH // 2 + 1, (NSH + NE) // 2) as i:
                for s in range(2):
                    expert(2 * i + s, s, False, False, "yes")
            for b in range(NB):
                pe.wait_ge(oev, 1)
                if b >= 2:
                    pe.wait_ge(fin, b - 1)
                for c in range(KD):
                    m = pe.transpose(bank[b % 2][0:S, c * 128:(c + 1) * 128], resT[:, c, b * S:(b + 1) * S], ident[:, :])
                m.then_inc(jf, 1)

        @block.scalar
        def _(act):
            def job(sem_in, jobs, key):
                act.wait_ge(sem_in, jobs.done(key))

            act.wait_ge(ld_small, 64)
            act.activation(gains[:, :], rowb[:, 0:4], ACT.Tanh).then_inc(tanh_g, 1)

            def exps(g, nk):
                act.wait_ge(maxed, g + 1)
                if g >= 2:
                    act.wait_ge(ptd, g - 1)
                act.activation(P[:, g % 2, 0:nk], bank[2 + g % 2][0:S, 0:nk], ACT.Exp, bias=nmax[:, g:g + 1],
                               accum_out=psum_[:, g:g + 1]).then_inc(expd, 1)

            act.wait_ge(init, 8)
            for b in range(NB):
                s = b % 2
                job(j1, J1, (b, 1))
                if b >= 2:
                    act.wait_ge(scored, H0 * (b - 1))
                act.activation(qT0[:, s, :, :], J1.bank((b, 1))[:, 0:4 * S].rearrange("p (c n) -> p c n", c=4), ACT.Copy,
                               scale=DH ** -0.5).then_inc(e1a, 1)
                for c in (0, 2, 3):
                    job(j1, J1, (b, 2 + c))
                    act.activation(kT0[s][:, c, :], J1.bank((b, 2 + c))[:, 0:L], ACT.Copy).then_inc(e1a, 1)
                if b >= 2:
                    act.wait_ge(pvd, H0 * (b - 1))
                for i in (0, 2):
                    n = min(128, L - i * 128)
                    job(j1, J1, (b, 6 + i))
                    act.activation(v0[s][0:n, i, :], J1.bank((b, 6 + i))[0:n, :], ACT.Copy).then_inc(e1a, 1)
                for h in range(H0):
                    exps(b * H0 + h, L)

            act.wait_ge(pvd, HEADS0)
            for t in range(NB):
                s = t % 2
                act.wait_ge(gated, 2 * t + 1)
                if t >= 2:
                    act.wait_ge(celld, t)
                act.activation(gate_s[:, s, :, :], bank[2 * s][:, 0:4 * S].rearrange("p (c n) -> p c n", c=4),
                               ACT.Sigmoid).then_inc(sigd, 1)
                act.wait_ge(gated, 2 * t + 2)
                act.activation(gate_t[:, s, :, :], bank[2 * s + 1][:, 0:2 * S].rearrange("p (c n) -> p c n", c=2),
                               ACT.Tanh).then_inc(tand, 1)
                job(j2, J2, ("hx", t))
                act.activation(XW[:, t, :], J2.bank(("hx", t))[0:S, 0:D], ACT.Copy).then_inc(e2a, 1)
                if t >= 2:
                    act.wait_ge(knd, t - 1)
                for i in range(LT):
                    n = min(128, L - i * 128)
                    key = ("kv", t, i)
                    job(j2, J2, key)
                    act.activation(kraw[0:n, s, i, :], J2.bank(key)[0:n, 0:I1], ACT.Copy)
                    act.activation(V1[0:n, t, i, :], J2.bank(key)[0:n, I1:2 * I1], ACT.Copy).then_inc(e2a, 1)
            for b in range(NB):
                act.wait_ge(hpre, b + 1)
                act.activation(XW[:, b, :], XW[:, b, :], ACT.Tanh).then_inc(htan, 1)

            def latents(b):
                job(j3, J3, ("qk", b))
                act.activation(qkraw[:, b, :], J3.bank(("qk", b))[0:S, :], ACT.Copy).then_inc(e3a, 1)
                job(j3, J3, ("vl", b))
                act.activation(V1[0:S, b, LT, :], J3.bank(("vl", b))[0:S, 0:I1], ACT.Copy).then_inc(e3a, 1)

            act.wait_ge(cud, 1)
            for r in range(-2, NB + 1):
                if 0 <= r + 2 < NB:
                    latents(r + 2)
                if 0 <= r < NB:
                    for h in range(H1):
                        exps(HEADS0 + r * H1 + h, NK1)

            act.wait_ge(lsub, 1)
            act.activation(logit[:, :, :], logit[:, :, :], ACT.Exp).then_inc(lexp, 1)

            def expert(e, first, routed):
                for hf in range(2):
                    n = e * 2 + hf
                    act.wait_ge(g_ready, n + 1)
                    if not first:
                        act.wait_ge(hidd, n - 1)
                    act.activation(sil[:, hf, :], bank[0][:, 0:HALF], ACT.Silu).then_inc(sild, 1)
                    if routed:
                        act.wait_ge(wb_ready, (e - NSH) * 2 + hf + 1)
                        act.activation(wbs[:, hf, :], bank[3][:, 0:HALF], ACT.Copy).then_inc(wbd, 1)

            for e in range(NSH):
                expert(e, e == 0, False)
            with act.Fori(NSH // 2, (NSH + NE) // 2) as i:
                for s in range(2):
                    expert(2 * i + s, False, True)

        @block.vector
        def _(dve):
            chain = [0]

            def own(ins):
                chain[0] += 1
                ins.then_inc(link, 1)
                dve.wait_ge(link, chain[0])

            def job(sem_in, jobs, key):
                dve.wait_ge(sem_in, jobs.done(key))

            def stats(src, bn_, mv_, n, done):
                own(dve.bn_stats(bn_, src))
                own(dve.bn_aggr(mv_, bn_))
                dve.tensor_scalar(mv_[:, 1:2], mv_[:, 1:2], 1e-5, None, ALU.add).then_inc(done, 1)

            def standardise(dst, src, mv_, rs_):
                return dve.tensor_scalar(dst, src, mv_[:, 0:1], rs_, ALU.subtract, ALU.mult)

            dve.wait_ge(ld_x, 32)
            dve.tensor_copy(identb[:, :], ident[:, :]).then_inc(initv, 1)
            for b in range(NB):
                stats(X[:, b, :], bn[0:S, b, :], mv[0:S, b, :], S, st0)
            dve.wait_ge(tanh_g, 1)
            GATE = (0, 2, 1)
            for i in range(3):
                dve.tensor_scalar(bob[:, i, :], rowb[0:S, 4 + i * D:4 + (i + 1) * D], gains[0:S, GATE[i]:GATE[i] + 1], None,
                                  ALU.mult).then_inc(initv, 1)
            own(dve.tensor_scalar(qk_gain[:, :], colv[:, 8:9], colv[:, 9:10], DH ** -0.5, ALU.mult, ALU.mult))
            dve.wait_ge(initv, 4)

            def heads(g, nk, tiles):
                dve.wait_ge(scored, g + 1)
                dve.tensor_reduce(nmax[:, g:g + 1], bank[2 + g % 2][0:S, 0:nk], AX.X, ALU.max, negate=True).then_inc(maxed, 1)

            def turned(g, tiles):
                dve.wait_ge(ptd, g + 1)
                if g >= 2:
                    dve.wait_ge(pvd, g - 1)
                dve.tensor_copy(PTs[:, g % 2, 0:tiles * S], bank[4 + g % 2][:, 0:tiles * S]).then_inc(pt_out, 1)

            def all_heads(g0, n, nk, tiles):
                heads(g0, nk, tiles)
                for h in range(n):
                    if h + 1 < n:
                        heads(g0 + h + 1, nk, tiles)
                    turned(g0 + h, tiles)

            def normalise(bt, g0, n):
                s = bt % 2
                dve.wait_ge(expd, g0 + n)
                own(dve.reciprocal(rden[:, g0:g0 + n], psum_[:, g0:g0 + n]))
                dve.wait_ge(pvd, g0 + n)
                dve.tensor_tensor(osb[:, s, 0:n * DH].rearrange("p (h d) -> p h d", d=DH),
                                  bank[6 + s][0:S, 0:n * DH].rearrange("p (h d) -> p h d", d=DH),
                                  rden[:, g0:g0 + n].unsqueeze(2).broadcast_to([S, n, DH]), ALU.mult).then_inc(normed, 1)

            def project(b):
                s = b % 2
                dve.wait_ge(rs0, b + 1)
                standardise(XN[:, b, :], X[:, b, :], mv[0:S, b, :], rstd[0:S, b:b + 1]).then_inc(xn0, 1)
                dve.wait_ge(xn0, b + 1)
                dve.tensor_tensor(X[:, b, :], X[:, b, :], bob[:, 0, :], ALU.add).then_inc(link, 1)
                chain[0] += 1
                job(j1, J1, (b, 0))
                dve.tensor_copy(xnT0[:, s, :, :], J1.bank((b, 0))[:, 0:KD * S].rearrange("p (k n) -> p k n", k=KD)).then_inc(e1v, 1)
                job(j1, J1, (b, 3))
                if b >= 2:
                    dve.wait_ge(scored, H0 * (b - 1))
                dve.tensor_copy(kT0[s][:, 1, :], J1.bank((b, 3))[:, 0:L]).then_inc(e1v, 1)
                job(j1, J1, (b, 7))
                if b >= 2:
                    dve.wait_ge(pvd, H0 * (b - 1))
                dve.tensor_copy(v0[s][:, 1, :], J1.bank((b, 7))[:, :]).then_inc(e1v, 1)

            def output0(b):
                s = b % 2
                job(j1, J1, (b, 9))
                dve.tensor_copy(oT[:, s, :, :], J1.bank((b, 9))[:, 0:4 * S].rearrange("p (c n) -> p c n", c=4)).then_inc(e1v, 1)
                job(j1, J1, (b, 10))
                dve.wait_ge(link, chain[0])
                dve.scalar_tensor_tensor(out=X[:, b, :], in0=J1.bank((b, 10))[0:S, 0:D], scalar=gains[0:S, 0:1], in1=X[:, b, :],
                                         op0=ALU.mult, op1=ALU.add).then_inc(e1v, 1)
                dve.wait_ge(e1v, J1.emptied((b, 10))[1])
                stats(X[:, b, :], bn1[0:S, b, :], mv1[0:S, b, :], S, st1)

            for b in range(NB):
                project(b)
                if b:
                    output0(b - 1)
                all_heads(b * H0, H0, L, LT)
                normalise(b, b * H0, H0)
            output0(NB - 1)

            for b in range(NB):
                dve.wait_ge(rs1, b + 1)
                standardise(XN[:, b, :], X[:, b, :], mv1[0:S, b, :], rstd1[0:S, b:b + 1]).then_inc(xn1, 1)

            def context_norm(b):
                s = b % 2
                dve.wait_ge(crs, b + 1)
                for i in range(LT):
                    last = standardise(ctok[:, s, i, :], ctok[:, s, i, :], mvc[:, s, i, :], rstdc[:, s, i:i + 1])
                last.then_inc(cnd, 1)

            def context_stats(b):
                s = b % 2
                dve.wait_ge(ld_ck[s], 32 * (b // 2 + 1))
                for i in range(LT):
                    dve.bn_stats(bnc[:, s, i, :], ctok[:, s, i, :]).then_inc(link, 1)
                chain[0] += LT
                dve.wait_ge(link, chain[0])
                for i in range(LT):
                    dve.bn_aggr(mvc[:, s, i, :], bnc[:, s, i, :]).then_inc(link, 1)
                chain[0] += LT
                dve.wait_ge(link, chain[0])
                dve.tensor_scalar(mvc[:, s, :, 1], mvc[:, s, :, 1], 1e-5, None, ALU.add).then_inc(cst, 1)

            def context_turn(b):
                s = b % 2
                for i in range(LT):
                    key = ("ct", b, i)
                    job(j2, J2, key)
                    if b >= 2:
                        dve.wait_ge(j2, J2.done(("kv", b - 2, i)))
                    for k, r in ((0, 128), (1, CR)):
                        last = dve.tensor_scalar(cnT[0:r, s, k, i * 128:(i + 1) * 128], J2.bank(key)[0:r, k * 128:(k + 1) * 128],
                                                 colv[0:r, k:k + 1], colv[0:r, 2 + k:3 + k], ALU.mult, ALU.add)
                    last.then_inc(e2v, 1)

            def key_sums(b):
                s = b % 2
                dve.wait_ge(ksqd, b + 1)
                own(dve.tensor_reduce(ssk[:, s, :], ksq[:, s, :, :].rearrange("p t (h d) -> p (t h) d", d=DH), AX.X, ALU.add))
                dve.tensor_scalar(ssk[:, s, :], ssk[:, s, :], 1.0 / DH, 1e-16, ALU.mult, ALU.max).then_inc(kss, 1)

            def key_turn(b):
                for i in range(LT):
                    key = ("kt", b, i)
                    job(j2, J2, key)
                    dve.tensor_copy(kT1[:, b, :, i * 128:(i + 1) * 128],
                                    J2.bank(key)[:, 0:D].rearrange("p (k n) -> p k n", k=KD)).then_inc(e2v, 1)

            context_stats(0)
            context_norm(0)
            for k in range(KD):
                own(dve.tensor_copy(cell[:, 0, k, :], colv[:, 10 + k:11 + k].broadcast_to([128, S])))
            dve.engine_nop().then_inc(celld, 1) if False else dve.tensor_copy(fc[:, :, :], cell[:, 0, :, :]).then_inc(celld, 1)
            for b in range(NB):
                job(j2, J2, ("xt", b))
                dve.tensor_copy(xT[:, :, b * S:(b + 1) * S], J2.bank(("xt", b))[:, 0:KD * S].rearrange("p (k n) -> p k n", k=KD)).then_inc(e2v, 1)
            context_turn(0)
            context_stats(1)
            context_norm(1)
            for t in range(NB):
                s = t % 2
                dve.wait_ge(sigd, t + 1)
                if t == 0:
                    dve.wait_ge(celld, 1)
                own(dve.tensor_tensor(fc[:, :, :], gate_s[:, s, 0:2, :], cell[:, s, :, :], ALU.mult))
                dve.wait_ge(tand, t + 1)
                own(dve.tensor_tensor(ig[:, :, :], gate_s[:, s, 2:4, :], gate_t[:, s, :, :], ALU.mult))
                dve.tensor_tensor(cell[:, 1 - s, :, :], fc[:, :, :], ig[:, :, :], ALU.add).then_inc(celld, 1)
                dve.wait_ge(celld, t + 2)
                if t + 1 < NB:
                    context_turn(t + 1)
                if t > 0:
                    key_sums(t - 1)
                if t + 2 < NB:
                    context_stats(t + 2)
                    context_norm(t + 2)
                if t > 0:
                    key_turn(t - 1)
            dve.wait_ge(cud, 1)
            dve.tensor_tensor(cu[:, :], bank[0][0:S, 0:D], rowb[0:S, 4 + D:4 + 2 * D], ALU.add).then_inc(cuv, 1)
            dve.wait_ge(cuv, 1)
            key_sums(NB - 1)
            key_turn(NB - 1)

            for b in range(NB):
                dve.wait_ge(e2a, J2.emptied(("hx", b))[1])
                dve.tensor_tensor(XW[:, b, :], XW[:, b, :], cu[:, :], ALU.add).then_inc(hpre, 1)
            for b in range(NB):
                dve.wait_ge(htan, b + 1)
                own(dve.scalar_tensor_tensor(out=X[:, b, :], in0=XW[:, b, :], scalar=gains[0:S, 2:3], in1=X[:, b, :],
                                             op0=ALU.mult, op1=ALU.add))
                stats(X[:, b, :], bn2[0:S, b, :], mv2[0:S, b, :], S, st2)
            for b in range(NB):
                dve.wait_ge(rs2, b + 1)
                own(standardise(XN[:, b, :], X[:, b, :], mv2[0:S, b, :], rstd2[0:S, b:b + 1]))
                own(dve.tensor_tensor(X[:, b, :], X[:, b, :], bob[:, 2, :], ALU.add))
                stats(XN[:, b, :], bn3[0:S, b, :], mv3[0:S, b, :], S, st3)
            for b in range(NB):
                dve.wait_ge(rs3, b + 1)
                standardise(XN[:, b, :], XN[:, b, :], mv3[0:S, b, :], rstd3[0:S, b:b + 1]).then_inc(z2d, 1)

            def latents(b):
                job(j3, J3, ("zt", b))
                for k in range(KD):
                    last = dve.tensor_scalar(xT[:, k, b * S:(b + 1) * S], J3.bank(("zt", b))[:, k * S:(k + 1) * S],
                                             colv[:, 4 + k:5 + k], colv[:, 6 + k:7 + k], ALU.mult, ALU.add)
                last.then_inc(e3v, 1)

            def latent_norm(b):
                dve.wait_ge(e3a, J3.emptied(("qk", b))[1])
                view = qkraw[:, b, :].rearrange("p (h d) -> p h d", d=DH)
                own(dve.tensor_tensor(XW[:, 2 * (b % 2):2 * (b % 2) + 2, :].rearrange("p a n -> p (a n)"), qkraw[:, b, :], qkraw[:, b, :], ALU.mult))
                own(dve.tensor_reduce(ssq[:, b, :], XW[:, 2 * (b % 2):2 * (b % 2) + 2, :].rearrange("p a (h d) -> p (a h) d", d=DH), AX.X, ALU.add))
                dve.tensor_scalar(ssq[:, b, :], ssq[:, b, :], 1.0 / DH, 1e-16, ALU.mult, ALU.max).then_inc(qss, 1)

            def latent_scale(b):
                view = qkraw[:, b, :].rearrange("p (h d) -> p h d", d=DH)
                dve.wait_ge(qrs, b + 1)
                dve.tensor_tensor(view, view, rq[:, b, :].unsqueeze(2).broadcast_to([S, 8, DH]), ALU.mult).then_inc(qknd, 1)

            def latent_turn(b):
                job(j3, J3, ("qt", b))
                src = J3.bank(("qt", b))
                dve.tensor_scalar(qT1[:, b, :, :], src[:, 0:2 * S].rearrange("p (k n) -> p k n", k=KD), qk_gain[:, 0:1], None, ALU.mult)
                dve.tensor_copy(kT1[:, b, :, LP:NK1], src[:, 2 * S:4 * S].rearrange("p (k n) -> p k n", k=KD)).then_inc(e3v, 1)

            def output1(b):
                s = b % 2
                job(j3, J3, ("ot", b))
                dve.tensor_copy(oT[:, s, 0:2, :], J3.bank(("ot", b))[:, 0:2 * S].rearrange("p (c n) -> p c n", c=2)).then_inc(e3v, 1)
                job(j3, J3, ("wo", b))
                dve.scalar_tensor_tensor(out=X[:, b, :], in0=J3.bank(("wo", b))[0:S, 0:D], scalar=gains[0:S, 1:2], in1=X[:, b, :],
                                         op0=ALU.mult, op1=ALU.add).then_inc(e3v, 1)
                dve.wait_ge(e3v, J3.emptied(("wo", b))[1])
                stats(X[:, b, :], bn4[0:S, b, :], mv4[0:S, b, :], S, st4)

            for r in range(-2, NB + 1):
                if 0 <= r + 2 < NB:
                    latents(r + 2)
                if 0 <= r + 1 < NB:
                    if r == -1:
                        latent_norm(0)
                        latent_scale(0)
                    latent_turn(r + 1)
                if 0 <= r - 1 < NB:
                    output1(r - 1)
                if 0 <= r < NB:
                    if r + 2 < NB:
                        latent_norm(r + 2)
                    all_heads(HEADS0 + r * H1, H1, NK1, 4)
                    if r + 2 < NB:
                        latent_scale(r + 2)
                    normalise(NB + r, HEADS0 + r * H1, H1)
                if r == -1:
                    latent_norm(1)
                    latent_scale(1)

            for b in range(NB):
                dve.wait_ge(rs4, b + 1)
                standardise(XN[:, b, :], X[:, b, :], mv4[0:S, b, :], rstd4[0:S, b:b + 1]).then_inc(y4, 1)
            for b in range(NB):
                dve.wait_ge(j4, b + 1)
                dve.tensor_copy(yT[:, :, b * S:(b + 1) * S], bank[b % 2][:, 0:KD * S].rearrange("p (k n) -> p k n", k=KD)).then_inc(e4v, 1)
            dve.wait_ge(j4, NB + 1)
            own(dve.tensor_tensor(logit[:, :, :], bank[2][0:S, 0:NB * NE].rearrange("p (b n) -> p b n", b=NB),
                                  rowb[0:S, 4 + 3 * D:ROWS].unsqueeze(1).broadcast_to([S, NB, NE]), ALU.add))
            own(dve.memset(prob[:, :, NE:NE + 8], -1.0))
            own(dve.tensor_reduce(lmax[:, :], logit[:, :, :], AX.X, ALU.max))
            dve.tensor_tensor(logit[:, :, :], logit[:, :, :], lmax[:, :].unsqueeze(2).broadcast_to([S, NB, NE]), ALU.subtract).then_inc(lsub, 1)
            dve.wait_ge(lexp, 1)
            own(dve.tensor_reduce(lsum[:, :], logit[:, :, :], AX.X, ALU.add))
            own(dve.reciprocal(lrec[:, :], lsum[:, :]))
            own(dve.tensor_tensor(prob[:, :, 0:NE], logit[:, :, :], lrec[:, :].unsqueeze(2).broadcast_to([S, NB, NE]), ALU.mult))
            for b in range(NB):
                dve.max(top[:, b, :], prob[:, b, 0:NE]).then_inc(link, 1)
            chain[0] += NB
            dve.wait_ge(link, chain[0])
            own(dve.memset(top[:, :, 4:8], -1.0))
            for b in range(NB):
                dve.match_replace(rest[:, b, :], in_to_replace=top[:, b, :], in_values=prob[:, b, :], imm_value=0.0).then_inc(link, 1)
            chain[0] += NB
            dve.wait_ge(link, chain[0])
            own(dve.tensor_tensor(logit[:, :, :], prob[:, :, 0:NE], rest[:, :, 0:NE], ALU.subtract))
            own(dve.tensor_reduce(lsum[:, :], logit[:, :, :], AX.X, ALU.add))
            own(dve.tensor_scalar(lsum[:, :], lsum[:, :], 1e-12, None, ALU.max))
            own(dve.reciprocal(lrec[:, :], lsum[:, :]))
            own(dve.tensor_tensor(w3f[:, :, 0, :], logit[:, :, :], lrec[:, :].unsqueeze(2).broadcast_to([S, NB, NE]), ALU.mult))
            w3 = w3b[:, :, :].rearrange("p b (i n) -> p b i n", i=3)
            for i in range(3):
                own(dve.tensor_copy(w3[:, :, i, :], w3f[:, :, i, :]))
                if i < 2:
                    own(dve.tensor_tensor(w3f[:, :, i + 1, :], w3f[:, :, i, :], w3[:, :, i, :], ALU.subtract))
            dve.tensor_copy(w3f[:, 0, 0, 0:8], w3f[:, 0, 1, 0:8]).then_inc(w3r, 1)

            def expert(e, routed, early):
                for hf in range(2):
                    n = e * 2 + hf
                    dve.wait_ge(u_ready, n + 1)
                    dve.wait_ge(sild, n + 1)
                    if not early:
                        dve.wait_ge(downd, n - 1)
                    if routed:
                        dve.tensor_tensor(sil[:, hf, :], sil[:, hf, :], bank[1][:, 0:HALF], ALU.mult).then_inc(link, 1)
                        if routed == "loop":
                            dve.wait_ge(link, (e - NSH) * 2 + hf + 1 + chain[0])
                        dve.wait_ge(wbd, (e - NSH) * 2 + hf + 1)
                        dve.tensor_tensor(hid[:, hf, :], sil[:, hf, :], wbs[:, hf, :], ALU.mult).then_inc(hidd, 1)
                    else:
                        dve.tensor_tensor(hid[:, hf, :], sil[:, hf, :], bank[1][:, 0:HALF], ALU.mult).then_inc(hidd, 1)

            for e in range(NSH):
                expert(e, None, e == 0)
            for b in range(NB):
                dve.wait_ge(j4, NB + 2 + b)
                dve.tensor_copy(wT3[:, b * S:(b + 1) * S], bank[3][:, :].bitcast(BF)[0:96, 0:S]).then_inc(e4v, 1)
            with dve.Fori(NSH // 2, (NSH + NE) // 2) as i:
                for s in range(2):
                    expert(2 * i + s, "loop", False)
            dve.wait_ge(downd, 2 * (NSH + NE))
            for c in range(KD):
                for hf in range(2):
                    last = dve.tensor_scalar(resT[:, c, hf * HALF:(hf + 1) * HALF], bank[4 + 2 * c + hf][:, 0:HALF], gains[:, 3:4], None, ALU.mult)
            last.then_inc(oev, 1)
            for b in range(NB):
                dve.wait_ge(jf, b + 1)
                dve.tensor_tensor(X[:, b, :], bank[b % 2][0:S, 0:D], X[:, b, :], ALU.add).then_inc(fin, 1)


def kernel(**inputs):
    import numpy as np
    import concourse.bacc as bacc
    from concourse.bass_utils import run_bass_kernel_spmd as run

    a = {k: np.asarray(v) for k, v in inputs.items()}
    eye = np.eye(128, dtype=np.float32)
    sel = np.kron(np.tile(np.eye(NE, dtype=np.float32), (3, 1)), np.ones((1, 128), np.float32))
    bf16 = mybir.dt.np(mybir.dt.bfloat16)

    def chunks(w):
        return w.reshape(-1, KD, 128, 128).transpose(0, 2, 1, 3).reshape(-1, 128, D)

    def pad(v):
        return np.concatenate([v, np.zeros(128 * KD - v.shape[0], v.dtype)]).reshape(KD, 128)

    gate_w = np.concatenate([a["L1_ffn_sgate_w"].reshape(NSH, 128, D), a["L1_ffn_gate_w"]])
    up_w = np.concatenate([a["L1_ffn_sup_w"].reshape(NSH, 128, D), a["L1_ffn_up_w"]])
    down_w = np.concatenate([a["L1_ffn_sdown_w"].reshape(D, NSH, 128).transpose(1, 0, 2), a["L1_ffn_down_w"]])
    cols = np.concatenate([pad(a["L1_xattn_ln_x_g"]), pad(a["L1_xattn_ln_x_b"]), pad(a["L1_xattn_ln_l_g"]), pad(a["L1_xattn_ln_l_b"]),
                           np.tile(a["L1_xattn_qn_g"], 2)[None], np.tile(a["L1_xattn_kn_g"], 2)[None], pad(a["L0_ffn_in_c"])])
    arrays = {
        "x": a["x"],
        "ctx": a["ctx_768"],
        "ctx_t": a["ctx_768"].transpose(2, 0, 1),
        "mask": a["mask_BxS2_bk0"][None],
        "rows": np.concatenate([a["g_xattn"], a["g_ffn"], a["L0_xattn_bo"], a["L0_ffn_bo"], a["L1_xattn_bo"], a["L1_ffn_router_bias"]]),
        "gate_rows": np.concatenate([a["L0_ffn_bf"], a["L0_ffn_bi"], a["L0_ffn_bc"]])[None],
        "cols": cols.T,
        "wq0": a["L0_xattn_Wq"],
        "wk0": a["L0_xattn_Wk"],
        "wv0": a["L0_xattn_Wv"],
        "wo0": a["L0_xattn_Wo"],
        "wffn": np.stack([a["L0_ffn_" + n].T for n in ("wf", "wi", "wc", "uf", "ui", "uc", "wo", "uo")]),
        "wlat": np.concatenate([a["L1_xattn_Wq"].T, a["L1_xattn_Wlkv"].T], 1),
        "wctx": a["L1_xattn_Wkv"].T,
        "wo1": a["L1_xattn_Wo"].T,
        "wrt": a["L1_ffn_router_w"].T,
        "wmoe": np.concatenate([chunks(gate_w.transpose(0, 2, 1)), chunks(up_w.transpose(0, 2, 1)), down_w.transpose(0, 2, 1)], 2),
        "ident_in": eye,
        "sel_in": sel.astype(bf16),
    }
    nc = bacc.Bacc("TRN2", target_bir_lowering=False, num_devices=1)
    feeds, aps = {}, []
    for name, v in arrays.items():
        v = np.ascontiguousarray(v)
        feeds["in_" + name] = v
        aps.append(nc.dram_tensor("in_" + name, v.shape, mybir.dt.from_np(v.dtype), kind="ExternalInput").ap())
    out = nc.dram_tensor("out_0", (NB, S, D), mybir.dt.float32, kind="ExternalOutput").ap()
    build(nc, *aps, out)
    r = run(nc, [feeds], core_ids=[0])
    return r.results[0]["out_0"]
```

```python
import concourse.bass as bass
from concourse import mybir
from contextlib import ExitStack

NB = 8
S = 100
D = 256
KD = D // 128
C = 192
CR = C - 128
L = 361
LT = 3
LP = LT * 128
LR = L - 2 * 128
H0 = 8
H1 = 4
DH = 64
I0 = H0 * DH
I1 = H1 * DH
NK1 = LP + S
NE = 32
NSH = 4
TOK = NB * S
HALF = TOK // 2
BIG = 1e30


class Jobs:

    def __init__(self, banks, seq):
        self.banks = banks
        self.at, self.kind, self.count, self.high = {}, {}, {}, {}
        self.left = []
        self.total = {"act": 0, "dve": 0}
        highs = 0
        for n, (key, kind) in enumerate(seq):
            eng = "act" if kind == "act" else "dve"
            self.total[eng] += 1
            self.at[key] = n
            self.count[key] = (eng, self.total[eng])
            if kind == "both":
                highs += 1
                self.high[key] = highs
            self.left.append(self.count[key])

    def bank(self, key):
        return self.banks[self.at[key] % len(self.banks)]

    def done(self, key):
        return self.at[key] + 1

    def emptied(self, key):
        return self.count[key]

    def before(self, key):
        n = self.at[key] - len(self.banks)
        return self.left[n] if n >= 0 else None


def build(nc, x, ctx, ctx_t, mask, rows, gate_rows, cols, w0, wo0, wffn, wlat, wctx, wo1, wrt, wmoe, ident_in, sel_in, out):
    F = mybir.dt.float32
    R = mybir.dt.float32r
    BF = mybir.dt.bfloat16
    ALU = mybir.AluOpType
    ACT = mybir.ActivationFunctionType
    AX = mybir.AxisListType
    LE = L + 1

    with ExitStack() as stack, ExitStack() as early, ExitStack() as mid, ExitStack() as late:
        def sb(name, shape, dt=F, where=stack):
            return where.enter_context(nc.sbuf_tensor(name, shape, dt))

        def sem(name):
            return stack.enter_context(nc.semaphore(name))

        ident = sb("ident", [128, 128])
        identb = sb("identb", [128, 128], BF)
        ROWS = 4 + NE
        rowb = sb("rowb", [128, ROWS])
        GB = sb("GB", [2, 4 * D], R)
        ones2 = sb("ones2", [2, 128], R)
        onesb = sb("onesb", [1, 128], BF)
        maskb = sb("maskb", [2, NB, NK1], BF)
        colv = sb("colv", [128, 12])
        gains = sb("gains", [128, 4])
        qk_gain = sb("qk_gain", [128, 1])
        unit = sb("unit", [128, 1])
        nhalf = sb("nhalf", [128, 16])
        X = sb("X", [S, NB, D])
        xnfull = sb("XN", [128, NB * D])
        XN = xnfull[0:S, :].rearrange("p (b n) -> p b n", b=NB)
        WH = sb("WH", [128, 8 * KD * D], R)
        WL = sb("WL", [128, 8 * KD * D], R)
        Wrt = sb("Wrt", [128, KD, NE])
        Wrts = [sb(n, [128, KD, NE], R) for n in ("WrtH", "WrtL")]
        P = sb("P", [S, 3, 512])
        PTs = sb("PTs", [128, 2, 4 * S])
        osb = sb("osb", [S, 2, I0])
        oTh = sb("oTh", [128, 2, 4, S], R)
        oTl = sb("oTl", [128, 2, 4, S], R)
        bn = sb("bn", [S, 6])
        bnc = sb("bnc", [128, LT, 6])
        MV = sb("MV", [128, 4, NB, 2])
        RS = sb("RS", [128, 4, NB])
        mvc = sb("mvc", [128, 2, LT, 2])
        rstdc = sb("rstdc", [128, 2, LT])
        ssk = sb("ssk", [128, 2, LT * H1])
        rk = sb("rk", [128, 2, LT * H1])
        ssq = sb("ssq", [S, NB, 8])
        rq = sb("rq", [S, NB, 8])
        nmax = sb("nmax", [S, 96])
        esum = sb("esum", [S, 96])
        rden = sb("rden", [S, 96])
        bob = sb("bob", [S, 3, D])
        lmax = sb("lmax", [S, NB])
        lsum = sb("lsum", [S, NB])
        lrec = sb("lrec", [S, NB])

        def halves(t, lo, hi, k):
            return t[:, lo:hi].rearrange("p (k n) -> p k n", k=k)

        WF = [t[:, :].rearrange("p (g k n) -> p g k n", g=8, k=KD) for t in (WH, WL)]
        Wlat = [halves(t, 0, 6 * D, KD) for t in (WH, WL)]
        Wo1 = [halves(t, 6 * D, 8 * D, KD) for t in (WH, WL)]
        Wexp = [halves(t, 8 * D, 14 * D, 2) for t in (WH, WL)]

        xTH = sb("xTH", [128, KD, TOK], R)
        xTL = sb("xTL", [128, KD, TOK], R)

        W0 = [sb(n, [128, 4, KD, I0], R, early) for n in ("W0H", "W0L")]
        Wk0, Wv0, Wq0, Wo0 = ([t[:, i, :, :] for t in W0] for i in range(4))
        Wo0 = [t.rearrange("p k (a n) -> p (k a) n", n=D) for t in Wo0]
        kT0 = [sb(n, [128, 2, 4, LE], R, early) for n in ("kT0H", "kT0L")]
        v0 = sb("v0", [128, 2, LT, I0], F, early)
        cT = sb("cT", [128, 2, 2, LE], F, early)
        cTs = [sb(n, [128, 2, 2, LE], R, early) for n in ("cTH", "cTL")]
        qT0 = [sb(n, [128, 2, 4, 2 * S], R, early) for n in ("qT0H", "qT0L")]
        xnT0 = [sb(n, [128, KD, 2 * S], R, early) for n in ("xnT0H", "xnT0L")]
        raw = sb("raw", [128, 2, KD * I0], F, early)
        rawq = xnfull[:, 4 * D:8 * D]
        GBraw = maskb[:, :, :].rearrange("p b n -> p (b n)")[:, 0:8 * D].bitcast(F)
        early.close()

        kT1 = sb("kT1", [128, NB, KD, NK1], F, mid)
        V1 = sb("V1", [128, NB, LT + 1, I1], F, mid)
        k1flat = kT1[:, :, :, :].rearrange("p b k n -> p (b k n)")
        v1flat = V1[:, :, :, :].rearrange("p b t n -> p (b t n)")
        ctok = xnfull[:, 0:2 * LT * C].rearrange("p (s t n) -> p s t n", s=2, t=LT)
        cval = xnfull[:, 2 * LT * C:2 * LT * C + 2 * LP].rearrange("p (k n) -> p k n", k=2)
        cells = [sb(n, [128, KD, S], R, mid) for n in ("cellH", "cellL")]
        mask8 = sb("mask8", [1, NB, L], mybir.dt.uint8, mid)
        th = sb("th", [S, 2, D], F, mid)
        rawlat = sb("rawlat", [128, 8 * D], F, mid)
        kraw = sb("kraw", [128, 2, LT, I1], F, late)
        ksq = sb("ksq", [128, LT, I1], F, late)
        cnT = [sb(n, [128, 2, LP], R, late) for n in ("cnTH", "cnTL")]
        Wctx = [sb(n, [128, 2, 2 * I1], R, late) for n in ("WctxH", "WctxL")]
        ctxraw = kraw[:, :, :, :].rearrange("p s t n -> p (s t n)")[:, 0:4 * I1].rearrange("p (k n) -> p k n", k=2)
        gate_s = sb("gate_s", [S, 2 * D], F, late)
        gate_t = sb("gate_t", [S, D], F, late)
        fc = sb("fc", [S, D], F, late)
        ig = sb("ig", [S, D], F, late)
        cell = sb("cell", [S, 2, D], F, late)
        late.close()
        after = mid
        qkraw = sb("qkraw", [S, 2, 2 * I1], F, after)
        qT1 = sb("qT1", [128, NB, KD, S], F, after)
        sqs = sb("sqs", [S, 2 * I1], F, after)[:, :]
        wraw = sb("wraw", [128, 2, 3 * D], F, after)
        logit = sb("logit", [S, NB, NE], F, after)
        zval = sb("zval", [128, KD, S], F, after)
        hidH = sb("hidH", [128, 2, HALF], R, after)
        hidL = sb("hidL", [128, 2, HALF], R, after)

        def take(flat, n, parts=128):
            take.o += n
            return flat[0:parts, take.o - n:take.o]

        take.o = 0
        sil, wbs, sw, hid = (take(k1flat, TOK).rearrange("p (h n) -> p h n", h=2) for _ in range(4))
        resT = take(k1flat, 2 * TOK).rearrange("p (k n) -> p k n", k=KD)
        take.o = 0
        prob = take(v1flat, NB * (NE + 8), S).rearrange("p (b n) -> p b n", b=NB)
        rest = take(v1flat, NB * (NE + 8), S).rearrange("p (b n) -> p b n", b=NB)
        top = take(v1flat, NB * 8, S).rearrange("p (b n) -> p b n", b=NB)
        w3f = take(v1flat, NB * 3 * NE, S).rearrange("p (b i n) -> p b i n", b=NB, i=3)
        w3b = take(v1flat, NB * 3 * NE // 2, S).bitcast(BF).rearrange("p (b n) -> p b n", b=NB)
        wT3 = take(v1flat, TOK // 2, 96).bitcast(BF)
        sel = take(v1flat, NE * 64, 96).bitcast(BF)
        mid.close()
        bank = [stack.enter_context(nc.psum_tensor(f"bank{i}", [128, 512], F)) for i in range(8)]

        names = ["ld_x", "ld_small", "ld_wk", "ld_wv", "ld_wq", "ld_wo", "ld_w1", "ld_lat", "ld_sel", "ld_mask", "ld_c0", "mask_set", "ctd",
                 "init",
                 "initv",
                 "link",
                 "plink",
                 "alink",
                 "tanh_g", "whi", "wsplit0", "wo_split", "wf_split", "gb_split", "ct_split",
                 "st0", "rs0", "xn0",
                 "j1", "e1a", "e1v", "h1",
                 "scored", "maxed", "expd", "ptd", "pt_a", "pt_v", "pvd", "normed",
                 "st1", "rs1", "xn1", "j2", "e2a", "e2v", "h2",
                 "gated", "sigd", "tand", "celld", "cell_hi", "cell_lo",
                 "cst", "cnd", "cnh", "cnl", "kss", "knd", "wrt_split", "wctx_hi", "wctx_split", "lat_hi", "lat_lo",
                 "st2", "rs2", "z2d", "zh", "zl", "j3", "e3a", "e3v", "h3", "qss", "qknd",
                 "st3", "rs3", "y4", "j4", "e4v", "lsub", "lexp", "w3r",
                 "g_ready", "u_ready", "wb_ready", "sild", "wbd", "swd", "prodd", "hhi", "hlo", "downd", "wes",
                 "oev", "oea", "jf", "fin", "stored"]
        sems = {n: sem(n) for n in names}
        (ld_x, ld_small, ld_wk, ld_wv, ld_wq, ld_wo, ld_w1, ld_lat, ld_sel, ld_mask, ld_c0, mask_set, ctd, init, initv, link, plink, alink,
         tanh_g, whi, wsplit0, wo_split, wf_split, gb_split, ct_split, st0, rs0, xn0, j1, e1a, e1v, h1, scored, maxed, expd, ptd,
         pt_a, pt_v, pvd, normed, st1, rs1, xn1, j2, e2a, e2v, h2, gated, sigd, tand, celld, cell_hi, cell_lo, cst, cnd,
         cnh, cnl, kss, knd, wrt_split, wctx_hi, wctx_split, lat_hi, lat_lo, st2, rs2, z2d, zh, zl, j3, e3a, e3v, h3, qss, qknd,
         st3, rs3, y4, j4, e4v, lsub, lexp, w3r, g_ready, u_ready, wb_ready, sild, wbd, swd, prodd, hhi, hlo, downd, wes,
         oev, oea, jf, fin, stored) = (sems[n] for n in names)
        ld_ct = [sem("ld_ct0"), sem("ld_ct1")]
        ld_ck = [sem("ld_ck0"), sem("ld_ck1")]
        ld_wf = [sem("ld_wf0"), sem("ld_wf1")]
        ld_we = [sem("ld_we0"), sem("ld_we1")]

        def beside0(b, h):
            n = b + 1
            table = {0: [("xt", n)], 1: [("k", n, 0)], 2: [("q", n, 0), ("ot", b - 1)], 3: [("q", n, 1), ("k", n, 1)],
                     4: [("k", n, 2), ("wo", b - 1)], 5: [("k", n, 3), ("x1", b - 2)], 6: [("v", n, 0), ("v", n, 1)], 7: [("v", n, 2)]}
            return [key for key in table[h] if 0 <= key[1] < NB and (key[0] not in ("xt", "q") or key[1] % 2 == 0)]

        BEFORE0 = [("xt", 0)] + [("k", 0, c) for c in range(4)] + [("q", 0, i) for i in range(2)] + [("v", 0, i) for i in range(LT)]
        AFTER0 = [("x1", NB - 2), ("ot", NB - 1), ("wo", NB - 1), ("x1", NB - 1)]

        def left_by(key):
            if key[0] == "v":
                return "dve" if key[2] == LT - 1 else "act"
            return "dve" if key[0] == "wo" else "both"

        J1 = Jobs(bank[0:2], [(key, left_by(key)) for key in BEFORE0 + [k for b in range(NB) for h in range(H0) for k in beside0(b, h)] + AFTER0])
        seq = []
        for t in range(NB + 1):
            if t > 0:
                seq += [(("kv", t - 1, i), "act") for i in range(LT)]
            if t < NB:
                seq += [(("ct", t, i), "dve") for i in range(LT)]
            if t > 1:
                seq += [(("kt", t - 2, i), "act") for i in range(LT)]
        HX0 = 4
        seq += [(("hx", b), "act") for b in range(HX0)] + [(("kt", NB - 1, i), "act") for i in range(LT)]
        J2 = Jobs([bank[0], bank[1], bank[6], bank[7]], seq)
        ROUNDS = range(-1, NB + 3)

        def real(b):
            return 0 <= b < NB

        BEFORE1 = [("zt", 0), ("hx", HX0), ("qk", 0), ("vl", 0), ("zt", 1), ("hx", HX0 + 1), ("qk", 1), ("vl", 1), ("qt", 0), ("hx", HX0 + 2)]

        def beside1(r, h):
            if (r, h) == (-1, 0):
                return BEFORE1
            table = {0: [("qt", r + 1)], 1: [("qk", r + 2), ("vl", r + 2), ("lg", r - 3)], 2: [("ot", r - 1)],
                     3: [("zt", r + 3), ("wo", r - 1), ("yt", r - 2)]}
            if (r, h) == (0, 2):
                return [("hx", NB - 1)]
            return [key for key in table[h] if real(key[1]) and key not in BEFORE1]

        LEFT1 = {"hx": "act", "zt": "dve", "qt": "dve", "ot": "both", "qk": "act", "vl": "act", "wo": "dve", "yt": "both", "lg": "dve"}
        SLOTS1 = [(r, h) for r in ROUNDS for h in range(H1)]
        J3 = Jobs(bank[0:2], [(key, LEFT1[key[0]]) for r, h in SLOTS1 for key in beside1(r, h)])
        HEADS0 = NB * H0
        HEADS1 = NB * H1
        FIRST = (bank[2], bank[3])
        SBANK = [bank[2], bank[3], bank[6]]

        block = stack.enter_context(nc.Block())

        @block.sync
        def _(sp):
            def load_ct(b):
                s = b % 2
                if b >= 2:
                    sp.wait_ge(ct_split, b - 1)
                sp.dma_start(cT[:, s, :, :], ctx_t[:, b, :].rearrange("(k p) n -> p k n", p=128)).then_inc(ld_ct[s], 16)

            def load_ck(b):
                s = b % 2
                if b >= 2:
                    sp.wait_ge(j2, J2.done(("ct", b - 2, LT - 1)))
                sp.dma_start(ctok[:, s, :, :], ctx[b, :, :].rearrange("(t p) c -> p t c", p=128)).then_inc(ld_ck[s], 16)

            def as_rows(w):
                return w.rearrange("(k p) n -> p k n", p=128)

            load_ct(0)
            for g, s in ((0, ld_wk), (1, ld_wv)):
                sp.dma_start(raw[:, g, :].rearrange("p (k n) -> p k n", k=KD), as_rows(w0[g, :, :])).then_inc(s, 16)
                if g == 0:
                    sp.dma_start(ident[:, :], ident_in).then_inc(ld_x, 16)
                    sp.dma_start(X[:, :, :], x.rearrange("b s d -> s b d")).then_inc(ld_x, 16)
                    sp.dma_start(rawq.rearrange("p (k n) -> p k n", k=KD), as_rows(w0[2, :, :])).then_inc(ld_wq, 16)
            load_ct(1)
            sp.wait_ge(wsplit0, 1)
            sp.dma_start(raw[:, 0, :].rearrange("p (k n) -> p k n", k=4), as_rows(wo0)).then_inc(ld_wo, 16)
            sp.dma_start(Wrt[:, :, :], as_rows(wrt)).then_inc(ld_w1, 16)
            for i in range(4):
                if i == 0:
                    sp.wait_ge(wsplit0, 2)
                elif i == 1:
                    sp.wait_ge(wo_split, 1)
                else:
                    sp.wait_ge(wf_split, i - 1)
                sp.dma_start(raw[:, (i + 1) % 2, :].rearrange("p (g k n) -> p g k n", g=2, k=KD),
                             wffn[2 * i:2 * i + 2, :, :].rearrange("g (k p) n -> p g k n", p=128)).then_inc(ld_wf[(i + 1) % 2], 16)
                if i + 2 < NB:
                    load_ct(i + 2)
            for b in range(6, NB):
                load_ct(b)
            sp.wait_ge(j1, len(J1.left))
            sp.wait_ge(wf_split, 4)
            sp.dma_start(ctxraw, as_rows(wctx)).then_inc(ld_w1, 16)
            load_ck(0)
            load_ck(1)
            sp.dma_start(cell[:, 0, :], rows[4 + 3 * D + NE:4 + 4 * D + NE].partition_broadcast(S)).then_inc(ld_c0, 16)
            sp.dma_start(mask8[:, :, :], mask).then_inc(ld_mask, 16)
            sp.dma_start(rawlat[:, 0:6 * D].rearrange("p (k n) -> p k n", k=KD), as_rows(wlat)).then_inc(ld_lat, 16)
            sp.dma_start(rawlat[:, 6 * D:8 * D].rearrange("p (k n) -> p k n", k=KD), as_rows(wo1)).then_inc(ld_lat, 16)
            for b in range(2, NB):
                load_ck(b)
            sp.wait_ge(j2, len(J2.left))
            sp.wait_ge(cell_lo, NB + 1)
            for e in range(2):
                sp.dma_start(wraw[:, e, :], wmoe[e, :, :]).then_inc(ld_we[e], 16)
            sp.wait_ge(pvd, HEADS0 + NB * H1)
            sp.dma_start(sel, sel_in).then_inc(ld_sel, 16)
            for e in range(2, NSH):
                sp.wait_ge(wes, 4 * (e - 1))
                sp.dma_start(wraw[:, e % 2, :], wmoe[e, :, :]).then_inc(ld_we[e % 2], 16)
            with sp.Fori(NSH // 2, (NSH + NE) // 2) as i:
                for s in range(2):
                    sp.wait_ge(wes, 8 * i + (4 * s - 4))
                    sp.dma_start(wraw[:, s, :], wmoe[bass.ds(2 * i + s, 1), :, :].rearrange("a p n -> p (a n)")).then_inc(ld_we[s], 16)
            for b in range(NB):
                sp.wait_ge(fin, b + 1)
                sp.dma_start(out[b, :, :], X[:, b, :]).then_inc(stored, 16)
            sp.wait_ge(stored, 16 * NB)

        @block.gpsimd
        def _(pool):
            chain = [0]

            def own(ins):
                chain[0] += 1
                ins.then_inc(plink, 1)
                pool.wait_ge(plink, chain[0])

            def split(dst, src, done):
                own(pool.tensor_copy(dst[0], src))
                pool.tensor_tensor(dst[1], src, dst[0].bitcast(F), ALU.subtract).then_inc(done, 1)

            def power(dst, src, width):
                return pool.tensor_tensor(dst, src, nhalf[0:dst.shape[0], 0:width], ALU.pow)

            pool.dma_start(rowb[:, 0:4], rows[0:4].partition_broadcast(128)).then_inc(ld_small, 16)
            pool.dma_start(bob[:, :, :], rows[4:4 + 3 * D].partition_broadcast(S)).then_inc(ld_small, 16)
            pool.dma_start(colv[:, :], cols).then_inc(ld_small, 16)
            pool.dma_start(GBraw, gate_rows).then_inc(ld_small, 16)
            pool.dma_start(rowb[:, 4:ROWS], rows[4 + 3 * D:4 + 3 * D + NE].partition_broadcast(128)).then_inc(ld_small, 16)
            pool.memset(nhalf[:, :], -0.5).then_inc(init, 1)
            pool.memset(unit[:, :], 1.0).then_inc(init, 1)
            own(pool.memset(P[:, :, :], 0.0))
            pool.tensor_scalar(ones2[:, :], P[0:2, 0, 0:128], 1.0, None, ALU.add).then_inc(init, 1)
            pool.memset(onesb[:, :], 1.0).then_inc(init, 1)

            def split_ct(b):
                s = b % 2
                pool.wait_ge(ld_ct[s], 16 * (b // 2 + 1))
                pool.wait_ge(ct_split, b)
                if b >= 2:
                    pool.wait_ge(j1, J1.done(("v", b - 2, 2)))
                own(pool.tensor_copy(cTs[0][:, s, :, :], cT[:, s, :, :]))
                pool.tensor_tensor(cTs[1][:, s, :, :], cT[:, s, :, :], cTs[0][:, s, :, :].bitcast(F), ALU.subtract).then_inc(ct_split, 1)

            pool.wait_ge(init, 4)

            def power0(b):
                pool.wait_ge(st0, b + 1)
                power(RS[0:S, 0, b:b + 1], MV[0:S, 0, b, 1:2], 1).then_inc(rs0, 1)

            power0(0)
            power0(1)
            split_ct(1)
            pool.wait_ge(ld_wo, 16)
            split([Wo0[i].rearrange("p k n -> p (k n)") for i in range(2)], raw[:, 0, :], wo_split)
            for b in range(NB):
                if b + 2 < NB:
                    split_ct(b + 2)
                if b % 2 == 0 and b + 2 < NB:
                    power0(b + 2)
                    power0(b + 3)
                if b:
                    pool.wait_ge(st1, b)
                    power(RS[0:S, 1, b - 1:b], MV[0:S, 1, b - 1, 1:2], 1).then_inc(rs1, 1)
                if b < 4:
                    n = 2 * KD * D
                    pool.wait_ge(ld_wf[(b + 1) % 2], 16 * (b // 2 + 1))
                    split([WH[:, b * n:(b + 1) * n], WL[:, b * n:(b + 1) * n]], raw[:, (b + 1) % 2, :], wf_split)
            pool.wait_ge(st1, NB)
            power(RS[0:S, 1, NB - 1:NB], MV[0:S, 1, NB - 1, 1:2], 1).then_inc(rs1, 1)

            def context_scale(b):
                s = b % 2
                pool.wait_ge(cst, b + 1)
                own(power(rstdc[:, s, :], mvc[:, s, :, 1], LT))
                for i in range(LT):
                    last = pool.tensor_scalar(ctok[:, s, i, :], ctok[:, s, i, :], mvc[:, s, i, 0:1], rstdc[:, s, i:i + 1],
                                              ALU.subtract, ALU.mult)
                last.then_inc(cnd, 1)

            def scale_keys(b):
                s = b % 2
                pool.wait_ge(kss, b + 1)
                own(power(rk[:, s, :], ssk[:, s, :], LT * H1))
                view = kraw[:, s, :, :].rearrange("p t (h d) -> p (t h) d", d=DH)
                pool.tensor_tensor(view, view,
                                   rk[:, s, :].unsqueeze(2).broadcast_to([128, LT * H1, DH]), ALU.mult).then_inc(knd, 1)

            def latent_scale(b):
                pool.wait_ge(st2, b + 1)
                power(RS[0:S, 2, b:b + 1], MV[0:S, 2, b, 1:2], 1).then_inc(rs2, 1)

            context_scale(0)
            context_scale(1)
            pool.wait_ge(ld_mask, 16)
            pool.wait_ge(gb_split, 1)
            for t in range(NB + 1):
                if t > 0:
                    scale_keys(t - 1)
                if t + 2 < NB:
                    context_scale(t + 2)
                if t < NB:
                    pool.memset(maskb[0:1, t, L:LP], -BIG)
                    pool.memset(maskb[0:1, t, LP:NK1], 0.0)
                    pool.tensor_scalar(maskb[0:1, t, 0:L], mask8[:, t, :], BIG, -BIG, ALU.mult, ALU.add).then_inc(mask_set, 1)
                if t == NB - 1:
                    pool.wait_ge(lat_hi, 1)
                    pool.tensor_tensor(WL[:, 0:8 * D], rawlat[:, :], WH[:, 0:8 * D].bitcast(F), ALU.subtract).then_inc(lat_lo, 1)
            for b in range(HX0):
                latent_scale(b)

            def split_expert(e, s, first):
                pool.wait_ge(ld_we[s], (e - s) * 8 + 16)
                for i, (lo, hi, used) in enumerate(((0, 2 * D, u_ready), (2 * D, 3 * D, downd))):
                    if not first:
                        pool.wait_ge(used, (e - 1) * 2)
                    width = [128, hi - lo]
                    pool.tensor_tensor(Wexp[0][:, s, lo:hi], wraw[:, s, lo:hi], unit[:, 0:1].broadcast_to(width), ALU.mult).then_inc(wes, 1)
                    pool.wait_ge(wes, e * 4 + (2 * i + 1))
                    pool.tensor_tensor(Wexp[1][:, s, lo:hi], wraw[:, s, lo:hi], Wexp[0][:, s, lo:hi].bitcast(F), ALU.subtract).then_inc(wes, 1)

            def scale_qk(b):
                view = qkraw[:, b % 2, :].rearrange("p (h d) -> p h d", d=DH)
                pool.wait_ge(qss, b + 1)
                own(power(rq[:, b, :], ssq[:, b, :], 8))
                pool.tensor_tensor(view, view, rq[:, b, :].unsqueeze(2).broadcast_to([S, 8, DH]), ALU.mult).then_inc(qknd, 1)

            for r, h in SLOTS1:
                for name, b in beside1(r, h):
                    if name == "vl":
                        scale_qk(b)
                    elif name == "hx":
                        latent_scale(b)
                if h == 3 and real(r - 1):
                    b = r - 1
                    pool.wait_ge(st3, b + 1)
                    power(RS[0:S, 3, b:b + 1], MV[0:S, 3, b, 1:2], 1).then_inc(rs3, 1)
                if h == 0 and r in (5, 6):
                    if r == 5:
                        pool.wait_ge(j3, J3.done(("hx", NB - 1)))
                    split_expert(r - 5, r - 5, True)

            for e in range(2, NSH):
                split_expert(e, e % 2, False)
            with pool.Fori(NSH // 2, (NSH + NE) // 2) as i:
                for s in range(2):
                    split_expert(2 * i + s, s, False)

        @block.tensor
        def _(pe):
            def empty(jobs, key, ev):
                before = jobs.before(key)
                if before:
                    pe.wait_ge(ev[before[0]], before[1])

            def emptied(jobs, key, ev):
                eng, n = jobs.emptied(key)
                pe.wait_ge(ev[eng], n)

            E1 = {"act": e1a, "dve": e1v}
            E2 = {"act": e2a, "dve": e2v}
            E3 = {"act": e3a, "dve": e3v}

            def product(dst, w, v, start, stop, skip=False):
                pe.matmul(dst, w[0], v[0], start=start, stop=False, skip_group_check=skip)
                pe.matmul(dst, w[0], v[1], start=False, stop=False, skip_group_check=skip)
                return pe.matmul(dst, w[1], v[0], start=False, stop=stop, skip_group_check=skip)

            def at(pair, *index):
                return [t[index] for t in pair]

            def score(g, q, k, nk, mask_row):
                if g >= 3:
                    pe.wait_ge(expd, g - 2)
                dst = SBANK[g % 3][0:S, 0:nk]
                if mask_row is not None:
                    pe.matmul(dst, onesb[0:1, 0:S], mask_row, start=True, stop=False)
                    pe.matmul(dst, q, k, start=False, stop=True).then_inc(scored, 1)
                else:
                    product(dst, q, k, True, True).then_inc(scored, 1)

            def pt_wait(g):
                pe.wait_ge(pt_v if g % 2 else pt_a, g // 2 + 1)

            def turn(g, tiles):
                pe.wait_ge(expd, g + 1)
                if g >= 2:
                    pt_wait(g - 2)
                for i in range(tiles):
                    m = pe.transpose(bank[4 + g % 2][:, i * S:(i + 1) * S], P[:, g % 3, i * 128:(i + 1) * 128], ident[0:S, 0:S])
                m.then_inc(ptd, 1)

            def values(g, h, bt, vals, rows_):
                pt_wait(g)
                if h == 0 and bt >= 1:
                    pe.wait_ge(normed, bt)
                n = len(rows_)
                for i, k in enumerate(rows_):
                    m = pe.matmul(bank[7][0:S, h * DH:(h + 1) * DH], PTs[0:k, g % 2, i * S:(i + 1) * S], vals(i, k),
                                  start=i == 0, stop=i == n - 1)
                m.then_inc(pvd, 1)

            def turn_rows(jobs, key, sem_out, src, n):
                for k in range(n):
                    m = pe.transpose(jobs.bank(key)[:, k * S:(k + 1) * S], src[:, k * 128:(k + 1) * 128], ident[0:S, 0:S])
                m.then_inc(sem_out, 1)

            def beside(key):
                name, b = key[0:2]
                empty(J1, key, E1)
                dst = J1.bank(key)
                if name == "xt":
                    pe.wait_ge(xn0, b + 2)
                    for k in range(KD):
                        for i in range(2):
                            m = pe.transpose(dst[:, (k * 2 + i) * S:(k * 2 + i + 1) * S], XN[:, b + i, k * 128:(k + 1) * 128], ident[0:S, 0:S])
                elif name == "x1":
                    pe.wait_ge(xn1, b + 1)
                    turn_rows(J1, key, j1, XN[:, b, :], KD)
                elif name == "k":
                    c = key[2]
                    pe.wait_ge(ct_split, b + 1)
                    if b == 0:
                        pe.wait_ge(wsplit0, 1)
                    for k, r in ((0, 128), (1, CR)):
                        m = product(dst[:, 0:LE], [w[0:r, k, c * 128:(c + 1) * 128] for w in Wk0],
                                    [t[0:r, b % 2, k, :] for t in cTs], k == 0, k == 1)
                elif name == "v":
                    i = key[2]
                    n = min(128, L - i * 128)
                    if b == 0:
                        pe.wait_ge(wsplit0, 2)
                    for k, r in ((0, 128), (1, CR)):
                        m = product(dst[0:n, :], [t[0:r, b % 2, k, i * 128:i * 128 + n] for t in cTs],
                                    [w[0:r, k, :] for w in Wv0], k == 0, k == 1)
                elif name == "q":
                    if b == 0:
                        pe.wait_ge(wsplit0, 3)
                    emptied(J1, ("xt", b), E1)
                    for i in range(2):
                        c = key[2] * 2 + i
                        for k in range(KD):
                            m = product(dst[:, i * 2 * S:(i + 1) * 2 * S], [w[:, k, c * 128:(c + 1) * 128] for w in Wq0],
                                        [t[:, k, :] for t in xnT0], k == 0, k == KD - 1)
                elif name == "ot":
                    pe.wait_ge(normed, b + 1)
                    turn_rows(J1, key, j1, osb[:, b % 2, :], 4)
                else:
                    if b == 0:
                        pe.wait_ge(wo_split, 1)
                    emptied(J1, ("ot", b), E1)
                    for c in range(4):
                        m = product(dst[0:S, 0:D], [t[:, b % 2, c, :] for t in (oTh, oTl)], [w[:, c, :] for w in Wo0], c == 0, c == 3)
                if name in ("x1", "ot"):
                    return
                m.then_inc(j1, 1)

            def score0(g):
                b, h = divmod(g, H0)
                o = 64 * (h % 2)
                if h == 0:
                    emptied(J1, ("q", b - b % 2, 1), E1)
                if h % 2 == 0:
                    emptied(J1, ("k", b, h // 2), E1)
                lo = b % 2 * S
                score(g, [t[o:o + 64, b // 2 % 2, h // 2, lo:lo + S] for t in qT0], [t[o:o + 64, b % 2, h // 2, :] for t in kT0], LE, None)

            def values0(g):
                b, h = divmod(g, H0)
                if h == 0:
                    for i in range(LT):
                        emptied(J1, ("v", b, i), E1)
                values(g, h, b, lambda i, k: v0[0:k, b % 2, i, h * DH:(h + 1) * DH], [128, 128, LR])

            pe.wait_ge(ld_x, 32)
            for key in BEFORE0:
                beside(key)
            for g in range(3):
                score0(g)
            pe.wait_ge(init, 4)
            for g in range(HEADS0):
                turn(g, LT)
                if g + 3 < HEADS0:
                    score0(g + 3)
                for key in beside0(g // H0, g % H0):
                    beside(key)
                if g:
                    values0(g - 1)
            values0(HEADS0 - 1)
            for key in AFTER0:
                beside(key)

            pe.wait_ge(wf_split, 4)
            pe.wait_ge(gb_split, 1)
            pe.wait_ge(e1v, J1.total["dve"])
            pt_wait(HEADS0 - 2)
            pt_wait(HEADS0 - 1)
            pe.wait_ge(normed, NB)
            def context_turn(b):
                s = b % 2
                pe.wait_ge(cnd, b + 1)
                for i in range(LT):
                    key = ("ct", b, i)
                    empty(J2, key, E2)
                    for k, r in ((0, 128), (1, CR)):
                        m = pe.transpose(J2.bank(key)[0:r, k * 128:(k + 1) * 128], ctok[:, s, i, k * 128:k * 128 + r], ident[:, :])
                    m.then_inc(j2, 1)

            def context_kv(b, tiles):
                if b == 0:
                    pe.wait_ge(wctx_split, 1)
                pe.wait_ge(cnl, b + 1)
                for i in tiles:
                    key = ("kv", b, i)
                    empty(J2, key, E2)
                    for k, r in ((0, 128), (1, CR)):
                        m = product(J2.bank(key)[:, :], [t[0:r, k, i * 128:(i + 1) * 128] for t in cnT],
                                    [w[0:r, k, :] for w in Wctx], k == 0, k == 1)
                    m.then_inc(j2, 1)

            def key_turn(b):
                pe.wait_ge(knd, b + 1)
                for i in range(LT):
                    key = ("kt", b, i)
                    empty(J2, key, E2)
                    for k in range(KD):
                        m = pe.transpose(J2.bank(key)[:, k * 128:(k + 1) * 128], kraw[:, b % 2, i, k * 128:(k + 1) * 128], ident[:, :])
                    m.then_inc(j2, 1)

            def gate_banks(t):
                a = 2 + 2 * (t % 2)
                return (bank[a][0:S, :], slice(0, 2)), (bank[a + 1][0:S, 0:D], slice(2, 3))

            def gates_x(t):
                if t >= 2:
                    pe.wait_ge(sigd, t - 1)
                    pe.wait_ge(tand, t - 1)
                for dst, g in gate_banks(t):
                    pe.matmul(dst, ones2[:, 0:S], GB[:, g.start * D:g.stop * D], start=True, stop=False, skip_group_check=True)
                    for k in range(KD):
                        product(dst, [v[:, k, t * S:(t + 1) * S] for v in (xTH, xTL)], [w[:, g, k, :] for w in WF], False, False, True)

            def gates_c(t):
                pe.wait_ge(cell_hi, t + 1)
                for dst, g in gate_banks(t):
                    for k in range(KD):
                        for w in WF:
                            pe.matmul(dst, cells[0][:, k, :], w[:, slice(3 + g.start, 3 + g.stop), k, :], start=False, stop=False,
                                      skip_group_check=True)
                pe.wait_ge(cell_lo, t + 1)
                for dst, g in gate_banks(t):
                    for k in range(KD):
                        last = pe.matmul(dst, cells[1][:, k, :], WF[0][:, slice(3 + g.start, 3 + g.stop), k, :], start=False,
                                         stop=k == KD - 1, skip_group_check=True)
                    last.then_inc(gated, 1)

            def cell_turn(t):
                pe.wait_ge(celld, t + 1)
                for k in range(KD):
                    m = pe.transpose(bank[3 + 2 * (t % 2)][:, D + k * S:D + (k + 1) * S], cell[:, 1 - t % 2, k * 128:(k + 1) * 128],
                                     ident[0:S, 0:S])
                m.then_inc(ctd, 1)

            def recurrent_out(J, j, E, b):
                key = ("hx", b)
                empty(J, key, E)
                dst = J.bank(key)[0:S, 0:D]
                pe.matmul(dst, ones2[:, 0:S], GB[:, 3 * D:4 * D], start=True, stop=False)
                for k in range(KD):
                    product(dst, [v[:, k, b * S:(b + 1) * S] for v in (xTH, xTL)], [w[:, 6, k, :] for w in WF], False, False)
                for k in range(KD):
                    m = product(dst, [c[:, k, :] for c in cells], [w[:, 7, k, :] for w in WF], False, k == KD - 1)
                m.then_inc(j, 1)

            gates_x(0)
            for t in range(NB + 1):
                if t < NB:
                    gates_c(t)
                if t + 1 < NB:
                    gates_x(t + 1)
                if t > 0:
                    context_kv(t - 1, [0])
                if t < NB:
                    cell_turn(t)
                if t > 0:
                    context_kv(t - 1, range(1, LT))
                if t < NB:
                    context_turn(t)
                if t > 1:
                    key_turn(t - 2)
            pe.wait_ge(cell_lo, NB + 1)
            for b in range(HX0):
                recurrent_out(J2, j2, E2, b)
            key_turn(NB - 1)

            pe.wait_ge(e2v, J2.total["dve"])
            pe.wait_ge(e2a, J2.total["act"])
            pe.wait_ge(mask_set, NB)

            def beside(key):
                name, b = key
                s = b % 2
                if name == "hx":
                    recurrent_out(J3, j3, E3, b)
                    return
                empty(J3, key, E3)
                dst = J3.bank(key)
                if name == "zt":
                    pe.wait_ge(z2d, b + 1)
                    turn_rows(J3, key, j3, XN[:, b, :], KD)
                elif name == "qt":
                    pe.wait_ge(qknd, b + 1)
                    turn_rows(J3, key, j3, qkraw[:, s, :], 4)
                elif name == "ot":
                    pe.wait_ge(normed, NB + b + 1)
                    turn_rows(J3, key, j3, osb[:, s, :], KD)
                elif name == "yt":
                    pe.wait_ge(y4, b + 1)
                    turn_rows(J3, key, j3, XN[:, b, :], KD)
                elif name == "lg":
                    if b == 0:
                        pe.wait_ge(wrt_split, 1)
                    emptied(J3, ("yt", b), E3)
                    for k in range(KD):
                        m = product(dst[0:S, 0:NE], [v[:, k, b * S:(b + 1) * S] for v in (xTH, xTL)], [w[:, k, :] for w in Wrts],
                                    k == 0, k == KD - 1)
                    m.then_inc(j3, 1)
                elif name == "wo":
                    emptied(J3, ("ot", b), E3)
                    for c in range(KD):
                        m = product(dst[0:S, 0:D], [t[:, s, c, :] for t in (oTh, oTl)], [w[:, c, :] for w in Wo1], c == 0, c == KD - 1)
                    m.then_inc(j3, 1)
                else:
                    if name == "qk":
                        if b == 0:
                            pe.wait_ge(lat_lo, 1)
                        pe.wait_ge(zl, b + 1)
                    c0, n = (0, 2 * I1) if name == "qk" else (2 * I1, I1)
                    for k in range(KD):
                        m = product(dst[0:S, 0:n], [v[:, k, b * S:(b + 1) * S] for v in (xTH, xTL)],
                                    [w[:, k, c0:c0 + n] for w in Wlat], k == 0, k == KD - 1)
                    m.then_inc(j3, 1)

            def score1(g):
                b, h = divmod(g, H1)
                o = 64 * (h % 2)
                if h == 0:
                    emptied(J3, ("qt", b), E3)
                score(HEADS0 + g, qT1[o:o + 64, b, h // 2, :], kT1[o:o + 64, b, h // 2, :], NK1, maskb[0:1, b, :])

            def values1(g):
                b, h = divmod(g, H1)
                if h == 0:
                    emptied(J3, ("vl", b), E3)
                values(HEADS0 + g, h, NB + b, lambda i, k: V1[0:k, b, i, h * DH:(h + 1) * DH], [128, 128, 128, S])

            def acc(c, hf):
                return bank[4 + 2 * c + hf][:, 0:HALF]

            def gate_up(e, s, hf, first, banks=(bank[0], bank[1])):
                n = e * 2 + hf
                lo = hf * HALF
                if hf == 0:
                    pe.wait_ge(wes, e * 4 + 2)
                for i, bk, ready, free in ((0, banks[0], g_ready, sild), (1, banks[1], u_ready, prodd)):
                    if not first:
                        pe.wait_ge(free, n)
                    for k in range(KD):
                        m = product(bk[:, 0:HALF], [w[:, s, i * D + k * 128:i * D + (k + 1) * 128] for w in Wexp],
                                    [v[:, k, lo:lo + HALF] for v in (xTH, xTL)], k == 0, k == KD - 1)
                    m.then_inc(ready, 1)

            for r, h in SLOTS1:
                g = r * H1 + h
                if 0 <= g < HEADS1:
                    turn(HEADS0 + g, 4)
                if 0 <= g + 3 < HEADS1:
                    score1(g + 3)
                for key in beside1(r, h):
                    beside(key)
                if 0 <= g - 1 < HEADS1:
                    values1(g - 1)
                if g == HEADS1:
                    pe.wait_ge(expd, HEADS0 + HEADS1)
                    gate_up(0, 0, 0, True, FIRST)

            def down(n, s, hf, first, last):
                if hf == 0:
                    pe.wait_ge(wes, n * 2 + 2)
                pe.wait_ge(hlo, n)
                for c in range(KD):
                    m = product(acc(c, hf), [w[:, s, 2 * D + c * 128:2 * D + (c + 1) * 128] for w in Wexp],
                                [h[:, hf, :] for h in (hidH, hidL)], first, last, True)
                m.then_inc(downd, 1)

            def weigh(r, hf, first):
                if not first:
                    pe.wait_ge(wbd, r * 2 + hf)
                pe.matmul(bank[3][:, 0:HALF], sel[:, bass.ds(r * 128, 128)], wT3[:, hf * HALF:(hf + 1) * HALF],
                          start=True, stop=True).then_inc(wb_ready, 1)

            pt_wait(HEADS0 + HEADS1 - 2)
            pt_wait(HEADS0 + HEADS1 - 1)
            pe.wait_ge(normed, 2 * NB)
            pe.wait_ge(e3v, J3.total["dve"])
            for e in range(NSH):
                for hf in range(2):
                    if e or hf:
                        gate_up(e, e % 2, hf, False)
                        down(2 * e + hf, (e - 1 + hf) % 2, 1 - hf, e == 0 or (e == 1 and hf == 0), False)
            pe.wait_ge(w3r, 1)
            for b in range(NB):
                m = pe.transpose(bank[2][:, :].bitcast(BF)[0:96, b * S:(b + 1) * S], w3b[:, b, :], identb[0:S, 0:S])
            m.then_inc(j4, 1)
            pe.wait_ge(e4v, 1)
            pe.wait_ge(ld_sel, 16)
            weigh(0, 0, True)
            with pe.Fori(NSH // 2, (NSH + NE) // 2 - 1) as i:
                for s in range(2):
                    for hf in range(2):
                        e = 2 * i + s
                        gate_up(e, s, hf, False)
                        down(2 * e + hf, (s - 1 + hf) % 2, 1 - hf, False, False)
                        weigh(e - NSH + hf, 1 - hf, False)
            for s in range(2):
                for hf in range(2):
                    e = NSH + NE - 2 + s
                    gate_up(e, s, hf, False)
                    down(2 * e + hf, (s - 1 + hf) % 2, 1 - hf, False, s == 1 and hf == 1)
                    if e - NSH + hf < NE:
                        weigh(e - NSH + hf, 1 - hf, False)
            down(2 * (NSH + NE), 1, 1, False, True)
            pe.wait_ge(oev, 2)
            pe.wait_ge(oea, 2)
            for b in range(NB):
                for c in range(KD):
                    m = pe.transpose(bank[b][0:S, c * 128:(c + 1) * 128], resT[:, c, b * S:(b + 1) * S], ident[:, :])
                m.then_inc(jf, 1)

        @block.scalar
        def _(act):
            def job(sem_in, jobs, key):
                act.wait_ge(sem_in, jobs.done(key))

            def copy(dst, src, scale=1.0):
                return act.activation(dst, src, ACT.Copy, scale=scale)

            def high(dst, src):
                act.activation(dst, src, ACT.Copy).then_inc(whi, 1)

            act.wait_ge(ld_ct[0], 16)
            high(cTs[0][:, 0, :, :], cT[:, 0, :, :])
            act.wait_ge(ld_wk, 16)
            high(W0[0][:, 0, :, :], raw[:, 0, :].rearrange("p (k n) -> p k n", k=KD))
            act.wait_ge(ld_wq, 16)
            high(W0[0][:, 2, :, :], rawq.rearrange("p (k n) -> p k n", k=KD))
            act.wait_ge(ld_wv, 16)
            high(W0[0][:, 1, :, :], raw[:, 1, :].rearrange("p (k n) -> p k n", k=KD))
            act.wait_ge(ld_small, 80)
            act.activation(gains[:, :], rowb[:, 0:4], ACT.Tanh).then_inc(tanh_g, 1)

            def exps(g, nk):
                act.wait_ge(maxed, g + 1)
                if g >= 3:
                    act.wait_ge(ptd, g - 2)
                act.activation(P[:, g % 3, 0:nk], SBANK[g % 3][0:S, 0:nk], ACT.Exp, bias=nmax[:, g:g + 1],
                               accum_out=esum[:, g:g + 1]).then_inc(expd, 1)

            def turned(g, tiles):
                act.wait_ge(ptd, g + 1)
                if g >= 2:
                    act.wait_ge(pvd, g - 1)
                copy(PTs[:, g % 2, 0:tiles * S], bank[4 + g % 2][:, 0:tiles * S]).then_inc(pt_a, 1)

            def chunks(ap, k):
                return ap.rearrange("p (k n) -> p k n", k=k)

            def beside(key):
                name, b = key[0:2]
                s = b % 2
                src = J1.bank(key)
                if name == "wo" or key[0:1] + key[2:] == ("v", LT - 1):
                    return
                job(j1, J1, key)
                if name == "xt":
                    copy(xnT0[0][:, :, :], chunks(src[:, 0:4 * S], KD)).then_inc(h1, 1)
                elif name == "x1":
                    copy(xTH[:, :, b * S:(b + 1) * S], chunks(src[:, 0:KD * S], KD)).then_inc(h1, 1)
                elif name == "k":
                    if key[2] == 0 and b >= 2:
                        act.wait_ge(scored, H0 * (b - 1))
                    copy(kT0[0][:, s, key[2], :], src[:, 0:LE]).then_inc(h1, 1)
                elif name == "v":
                    if key[2] == 0 and b >= 2:
                        act.wait_ge(pvd, H0 * (b - 1))
                    copy(v0[:, s, key[2], :], src[:, :]).then_inc(e1a, 1)
                elif name == "q":
                    i = key[2] * 2
                    copy(qT0[0][:, b // 2 % 2, i:i + 2, :], chunks(src[:, 0:4 * S], 2), DH ** -0.5).then_inc(h1, 1)
                else:
                    copy(oTh[:, s, :, :], chunks(src[:, 0:4 * S], 4)).then_inc(h1, 1)

            for key in BEFORE0:
                beside(key)
            act.wait_ge(init, 4)
            for g in range(3):
                exps(g, L)
            for g in range(HEADS0):
                if g % 2 == 0:
                    turned(g, LT)
                if g + 3 < HEADS0:
                    exps(g + 3, L)
                for key in beside0(g // H0, g % H0):
                    beside(key)
            for key in AFTER0:
                beside(key)

            act.wait_ge(j1, len(J1.left))

            def context_high(b):
                act.wait_ge(e2v, J2.emptied(("ct", b, LT - 1))[1])
                if b:
                    act.wait_ge(j2, J2.done(("kv", b - 1, LT - 1)))
                copy(cnT[0][:, :, :], cval).then_inc(cnh, 1)

            def recurrent_out(J, j, e, b):
                job(j, J, ("hx", b))
                if b >= 2:
                    act.wait_ge(st2, b - 1)
                act.activation(th[:, b % 2, :], J.bank(("hx", b))[0:S, 0:D], ACT.Tanh).then_inc(e, 1)

            def key_turn(b):
                for i in range(LT):
                    key = ("kt", b, i)
                    job(j2, J2, key)
                    copy(kT1[:, b, :, i * 128:(i + 1) * 128], chunks(J2.bank(key)[:, 0:D], KD)).then_inc(e2a, 1)

            act.wait_ge(ld_w1, 32)
            copy(Wctx[0][:, :, :], ctxraw).then_inc(wctx_hi, 1)
            for t in range(NB + 1):
                if t < NB:
                    act.wait_ge(gated, 2 * t + 1)
                    if t:
                        act.wait_ge(celld, t)
                    act.activation(gate_s[:, :], bank[2 + 2 * (t % 2)][0:S, :], ACT.Sigmoid).then_inc(sigd, 1)
                    act.wait_ge(gated, 2 * t + 2)
                    act.activation(gate_t[:, :], bank[3 + 2 * (t % 2)][0:S, 0:D], ACT.Tanh).then_inc(tand, 1)
                if t > 0:
                    b = t - 1
                    if b >= 2:
                        act.wait_ge(j2, J2.done(("kt", b - 2, LT - 1)))
                    if b:
                        act.wait_ge(kss, b)
                    if b == 0:
                        act.wait_ge(wctx_split, 1)
                    for i in range(LT):
                        key = ("kv", b, i)
                        job(j2, J2, key)
                        copy(kraw[:, b % 2, i, :], J2.bank(key)[:, 0:I1])
                        act.activation(ksq[:, i, :], J2.bank(key)[:, 0:I1], ACT.Square)
                        copy(V1[:, b, i, :], J2.bank(key)[:, I1:2 * I1]).then_inc(e2a, 1)
                if t < NB:
                    context_high(t)
                if t > 1:
                    key_turn(t - 2)
                if t == NB - 1:
                    act.wait_ge(ld_lat, 32)
                    copy(WH[:, 0:8 * D], rawlat[:, :]).then_inc(lat_hi, 1)
            for b in range(HX0):
                recurrent_out(J2, j2, e2a, b)
            key_turn(NB - 1)

            def beside(key):
                name, b = key
                s = b % 2
                src = J3.bank(key)
                if name == "hx":
                    recurrent_out(J3, j3, e3a, b)
                elif name == "zt":
                    act.wait_ge(e3v, J3.emptied(key)[1])
                    copy(xTH[:, :, b * S:(b + 1) * S], zval[:, :, :]).then_inc(zh, 1)
                elif name == "ot":
                    job(j3, J3, key)
                    copy(oTh[:, s, 0:KD, :], chunks(src[:, 0:KD * S], KD)).then_inc(h3, 1)
                elif name == "qk":
                    job(j3, J3, key)
                    copy(qkraw[:, s, :], src[0:S, :])
                    if b:
                        act.wait_ge(qss, b)
                    act.activation(sqs, src[0:S, :], ACT.Square).then_inc(e3a, 1)
                elif name == "vl":
                    job(j3, J3, key)
                    copy(V1[0:S, b, LT, :], src[0:S, 0:I1]).then_inc(e3a, 1)
                elif name == "yt":
                    job(j3, J3, key)
                    copy(xTH[:, :, b * S:(b + 1) * S], chunks(src[:, 0:KD * S], KD)).then_inc(h3, 1)

            for r, h in SLOTS1:
                g = r * H1 + h
                if 0 <= g < HEADS1 and g % 2 == 0:
                    turned(HEADS0 + g, 4)
                if 0 <= g + 3 < HEADS1:
                    exps(HEADS0 + g + 3, NK1)
                for key in beside1(r, h):
                    beside(key)

            def expert(e, first, routed):
                for hf in range(2):
                    gate = FIRST[0] if first and hf == 0 else bank[0]
                    n = e * 2 + hf
                    act.wait_ge(g_ready, n + 1)
                    if not first:
                        act.wait_ge(prodd, n - 1)
                    act.activation(sil[:, hf, :], gate[:, 0:HALF], ACT.Silu).then_inc(sild, 1)
                    act.wait_ge(prodd, n + 1)
                    if not first:
                        act.wait_ge(downd, n - 1)
                    copy(hidH[:, hf, :], hid[:, hf, :]).then_inc(hhi, 1)
                    if routed:
                        weights(e - NSH + hf, 1 - hf)

            def weights(r, hf):
                act.wait_ge(wb_ready, r * 2 + hf + 1)
                copy(wbs[:, hf, :], bank[3][:, 0:HALF]).then_inc(wbd, 1)

            expert(0, True, False)
            act.wait_ge(lsub, 1)
            act.activation(logit[:, :, :], logit[:, :, :], ACT.Exp).then_inc(lexp, 1)
            for e in range(1, NSH):
                expert(e, False, False)
            weights(0, 0)
            with act.Fori(NSH // 2, (NSH + NE) // 2 - 1) as i:
                for s in range(2):
                    expert(2 * i + s, False, True)
            expert(NSH + NE - 2, False, True)
            for hf in range(2):
                n = (NSH + NE - 1) * 2 + hf
                act.wait_ge(g_ready, n + 1)
                act.wait_ge(prodd, n - 1)
                act.activation(sil[:, hf, :], bank[0][:, 0:HALF], ACT.Silu).then_inc(sild, 1)
                act.wait_ge(prodd, n + 1)
                act.wait_ge(downd, n - 1)
                copy(hidH[:, hf, :], hid[:, hf, :]).then_inc(hhi, 1)
                if hf == 0:
                    weights(NE - 1, 1)
            act.wait_ge(downd, 2 * (NSH + NE))
            for hf in range(2):
                act.activation(resT[:, 1, hf * HALF:(hf + 1) * HALF], bank[6 + hf][:, 0:HALF], ACT.Copy,
                               scale=gains[:, 3:4]).then_inc(oea, 1)

        @block.vector
        def _(dve):
            chain = [0]

            def own(ins):
                chain[0] += 1
                ins.then_inc(link, 1)
                dve.wait_ge(link, chain[0])

            def job(sem_in, jobs, key):
                dve.wait_ge(sem_in, jobs.done(key))

            def stats(src, p, b, done):
                mv = MV[0:S, p, b, :]
                own(dve.bn_stats(bn[:, :], src))
                own(dve.bn_aggr(mv, bn[:, :]))
                if p == 2:
                    dve.tensor_scalar(mv[:, 1:2], mv[:, 1:2], 1.0 + 1e-5, 1e-10, ALU.mult, ALU.add).then_inc(done, 1)
                else:
                    dve.tensor_scalar(mv[:, 1:2], mv[:, 1:2], 1e-5, None, ALU.add).then_inc(done, 1)

            def standardise(b, p):
                return dve.tensor_scalar(XN[:, b, :], X[:, b, :], MV[0:S, p, b, 0:1], RS[0:S, p, b:b + 1], ALU.subtract, ALU.mult)

            def low(jobs, key, hsem, dst, src, hi):
                dve.wait_ge(hsem, jobs.high[key])
                return dve.tensor_tensor(dst, src, hi.bitcast(F), ALU.subtract)

            def chunks(ap, k):
                return ap.rearrange("p (k n) -> p k n", k=k)

            def low_part(dst, src, hi, n, done):
                dve.wait_ge(whi, n)
                dve.tensor_tensor(dst, src, hi.bitcast(F), ALU.subtract).then_inc(done, 1)

            low_part(cTs[1][:, 0, :, :], cT[:, 0, :, :], cTs[0][:, 0, :, :], 1, ct_split)
            low_part(W0[1][:, 0, :, :], raw[:, 0, :].rearrange("p (k n) -> p k n", k=KD), W0[0][:, 0, :, :], 2, wsplit0)
            dve.wait_ge(ld_x, 32)
            stats(X[:, 0, :], 0, 0, st0)
            stats(X[:, 1, :], 0, 1, st0)
            dve.wait_ge(rs0, 1)
            standardise(0, 0).then_inc(xn0, 1)
            dve.wait_ge(rs0, 2)
            standardise(1, 0).then_inc(xn0, 1)

            def put_bias(b):
                dve.wait_ge(xn0, b + 1)
                own(dve.tensor_tensor(X[:, b, :], X[:, b, :], bob[:, 0, :], ALU.add))

            def maximum(g, nk):
                dve.wait_ge(scored, g + 1)
                dve.tensor_reduce(nmax[:, g:g + 1], SBANK[g % 3][0:S, 0:nk], AX.X, ALU.max, negate=True).then_inc(maxed, 1)

            def turned(g, tiles):
                dve.wait_ge(ptd, g + 1)
                dve.wait_ge(pvd, g - 1) if g >= 2 else None
                dve.tensor_copy(PTs[:, g % 2, 0:tiles * S], bank[4 + g % 2][:, 0:tiles * S]).then_inc(pt_v, 1)

            def normalise(bt, g0, n):
                s = bt % 2
                dve.wait_ge(expd, g0 + n)
                own(dve.reciprocal(rden[:, g0:g0 + n], esum[:, g0:g0 + n]))
                dve.wait_ge(pvd, g0 + n)
                dve.tensor_tensor(osb[:, s, 0:n * DH].rearrange("p (h d) -> p h d", d=DH),
                                  bank[7][0:S, 0:n * DH].rearrange("p (h d) -> p h d", d=DH),
                                  rden[:, g0:g0 + n].unsqueeze(2).broadcast_to([S, n, DH]), ALU.mult).then_inc(normed, 1)

            def beside(key):
                name, b = key[0:2]
                s = b % 2
                src = J1.bank(key)
                if name == "xt":
                    low(J1, key, h1, xnT0[1][:, :, :], chunks(src[:, 0:4 * S], KD), xnT0[0][:, :, :]).then_inc(e1v, 1)
                elif name == "x1":
                    low(J1, key, h1, xTL[:, :, b * S:(b + 1) * S], chunks(src[:, 0:KD * S], KD), xTH[:, :, b * S:(b + 1) * S]).then_inc(e1v, 1)
                elif name == "k":
                    c = key[2]
                    low(J1, key, h1, kT0[1][:, s, c, :], src[:, 0:LE], kT0[0][:, s, c, :]).then_inc(e1v, 1)
                elif name == "v":
                    if key[2] == LT - 1:
                        job(j1, J1, key)
                        dve.tensor_copy(v0[0:LR, s, 2, :], src[0:LR, :]).then_inc(e1v, 1)
                elif name == "q":
                    i = key[2] * 2
                    dve.wait_ge(h1, J1.high[key])
                    dve.scalar_tensor_tensor(out=qT0[1][:, b // 2 % 2, i:i + 2, :].rearrange("p k n -> p (k n)"), in0=src[:, 0:4 * S],
                                             scalar=DH ** -0.5, in1=qT0[0][:, b // 2 % 2, i:i + 2, :].bitcast(F).rearrange("p k n -> p (k n)"),
                                             op0=ALU.mult, op1=ALU.subtract).then_inc(e1v, 1)
                elif name == "ot":
                    low(J1, key, h1, oTl[:, s, :, :], chunks(src[:, 0:4 * S], 4), oTh[:, s, :, :]).then_inc(e1v, 1)
                else:
                    job(j1, J1, key)
                    dve.scalar_tensor_tensor(out=X[:, b, :], in0=src[0:S, 0:D], scalar=gains[0:S, 0:1], in1=X[:, b, :],
                                             op0=ALU.mult, op1=ALU.add).then_inc(e1v, 1)
                    dve.wait_ge(e1v, J1.emptied(key)[1])

            def split_router():
                dve.wait_ge(ld_w1, 16)
                own(dve.tensor_copy(Wrts[0][:, :, :], Wrt[:, :, :]))
                dve.tensor_tensor(Wrts[1][:, :, :], Wrt[:, :, :], Wrts[0][:, :, :].bitcast(F), ALU.subtract).then_inc(wrt_split, 1)

            def put_gate_biases():
                own(dve.tensor_copy(GB[:, :], GBraw))
                own(dve.tensor_tensor(GBraw, GBraw, GB[:, :].bitcast(F), ALU.subtract))
                own(dve.tensor_scalar(GB[:, :], GB[:, :].bitcast(F), ident[0:2, 0:1], None, ALU.mult))
                dve.scalar_tensor_tensor(out=GB[:, :], in0=GBraw, scalar=ident[0:2, 1:2], in1=GB[:, :].bitcast(F),
                                         op0=ALU.mult, op1=ALU.add).then_inc(gb_split, 1)

            for key in BEFORE0:
                if key == ("q", 0, 0):
                    low_part(W0[1][:, 2, :, :], rawq.rearrange("p (k n) -> p k n", k=KD), W0[0][:, 2, :, :], 3, wsplit0)
                if key == ("v", 0, 2):
                    pass
                if key == ("k", 0, 1):
                    low_part(W0[1][:, 1, :, :], raw[:, 1, :].rearrange("p (k n) -> p k n", k=KD), W0[0][:, 1, :, :], 4, wsplit0)
                beside(key)
            for g in range(3):
                maximum(g, L)
            for g in range(HEADS0):
                b, h = divmod(g, H0)
                if h == 1 and b:
                    normalise(b - 1, (b - 1) * H0, H0)
                if g % 2:
                    turned(g, LT)
                if g + 3 < HEADS0:
                    maximum(g + 3, L)
                if b == 0 and h == 0:
                    dve.wait_ge(tanh_g, 1)
                    GATE = (0, 2, 1)
                    for i in range(3):
                        dve.tensor_scalar(bob[:, i, :], bob[:, i, :], gains[0:S, GATE[i]:GATE[i] + 1], None, ALU.mult).then_inc(initv, 1)
                    dve.tensor_copy(identb[:, :], ident[:, :]).then_inc(initv, 1)
                    own(dve.tensor_scalar(qk_gain[:, :], colv[:, 8:9], colv[:, 9:10], DH ** -0.5, ALU.mult, ALU.mult))
                    dve.wait_ge(initv, 4)
                if b == 0 and h in (3, 4):
                    put_bias(h - 3)
                if b == 1 and h == 0:
                    put_gate_biases()
                    split_router()
                for key in beside0(b, h):
                    beside(key)
                if b % 2 == 0 and b + 2 < NB and h in (2, 3):
                    n = b + h
                    stats(X[:, n, :], 0, n, st0)
                if h == 5 and b:
                    stats(X[:, b - 1, :], 1, b - 1, st1)
                if b % 2 == 0 and b + 2 < NB and h in (4, 5):
                    n = b + h - 2
                    dve.wait_ge(rs0, n + 1)
                    if n == 4:
                        dve.wait_ge(wsplit0, 3)
                    standardise(n, 0).then_inc(xn0, 1)
                    put_bias(n)
                if h == 7 and b:
                    dve.wait_ge(rs1, b)
                    standardise(b - 1, 1).then_inc(xn1, 1)
            normalise(NB - 1, (NB - 1) * H0, H0)
            for key in AFTER0:
                if key == ("x1", NB - 1):
                    stats(X[:, NB - 1, :], 1, NB - 1, st1)
                    dve.wait_ge(rs1, NB)
                    standardise(NB - 1, 1).then_inc(xn1, 1)
                beside(key)

            def cell_parts(t, src):
                dve.tensor_copy(cells[0][:, :, :], src).then_inc(cell_hi, 1)
                dve.wait_ge(cell_hi, t + 1)
                dve.tensor_tensor(cells[1][:, :, :], src, cells[0][:, :, :].bitcast(F), ALU.subtract).then_inc(cell_lo, 1)

            def context_stats(b):
                s = b % 2
                dve.wait_ge(ld_ck[s], 16 * (b // 2 + 1))
                for i in range(LT):
                    dve.bn_stats(bnc[:, i, :], ctok[:, s, i, :]).then_inc(link, 1)
                chain[0] += LT
                dve.wait_ge(link, chain[0])
                for i in range(LT):
                    dve.bn_aggr(mvc[:, s, i, :], bnc[:, i, :]).then_inc(link, 1)
                chain[0] += LT
                dve.wait_ge(link, chain[0])
                dve.tensor_scalar(mvc[:, s, :, 1], mvc[:, s, :, 1], 1e-5, None, ALU.add).then_inc(cst, 1)

            def context_turn(b):
                if b:
                    dve.wait_ge(cnl, b)
                for i in range(LT):
                    key = ("ct", b, i)
                    job(j2, J2, key)
                    for k, r in ((0, 128), (1, CR)):
                        last = dve.tensor_scalar(cval[0:r, k, i * 128:(i + 1) * 128], J2.bank(key)[0:r, k * 128:(k + 1) * 128],
                                                 colv[0:r, k:k + 1], colv[0:r, 2 + k:3 + k], ALU.mult, ALU.add)
                    last.then_inc(e2v, 1)
                dve.wait_ge(e2v, J2.emptied(("ct", b, LT - 1))[1])

            def context_low(b):
                dve.wait_ge(cnh, b + 1)
                dve.tensor_tensor(cnT[1][:, :, :], cval, cnT[0][:, :, :].bitcast(F), ALU.subtract).then_inc(cnl, 1)

            def key_sums(b):
                s = b % 2
                dve.wait_ge(e2a, J2.emptied(("kv", b, LT - 1))[1])
                own(dve.tensor_reduce(ssk[:, s, :], ksq[:, :, :].rearrange("p t (h d) -> p (t h) d", d=DH), AX.X, ALU.add))
                dve.tensor_scalar(ssk[:, s, :], ssk[:, s, :], 1.0 / DH, 1e-16, ALU.mult, ALU.max).then_inc(kss, 1)

            dve.wait_ge(j1, len(J1.left))
            cell_parts(0, colv[:, 10:12].unsqueeze(2).broadcast_to([128, KD, S]))
            own(dve.memset(cval[:, 1, :], 0.0))
            context_stats(0)
            dve.wait_ge(wctx_hi, 1)
            dve.tensor_tensor(Wctx[1][:, :, :], ctxraw, Wctx[0][:, :, :].bitcast(F), ALU.subtract).then_inc(wctx_split, 1)
            context_stats(1)
            dve.wait_ge(ld_c0, 16)
            for t in range(NB + 1):
                if t < NB:
                    s = t % 2
                    dve.wait_ge(sigd, t + 1)
                    own(dve.tensor_tensor(fc[:, :], gate_s[:, 0:D], cell[:, s, :], ALU.mult))
                    dve.wait_ge(tand, t + 1)
                    own(dve.tensor_tensor(ig[:, :], gate_s[:, D:2 * D], gate_t[:, :], ALU.mult))
                    dve.tensor_tensor(cell[:, 1 - s, :], fc[:, :], ig[:, :], ALU.add).then_inc(celld, 1)
                    dve.wait_ge(ctd, t + 1)
                    cell_parts(t + 1, chunks(bank[3 + 2 * s][:, D:D + KD * S], KD))
                if t < NB:
                    context_turn(t)
                if t > 0:
                    key_sums(t - 1)
                if t < NB:
                    context_low(t)
                if t + 2 < NB:
                    context_stats(t + 2)

            def residual2(J, e, b):
                dve.wait_ge(e, J.emptied(("hx", b))[1])
                own(dve.scalar_tensor_tensor(out=X[:, b, :], in0=th[:, b % 2, :], scalar=gains[0:S, 2:3], in1=X[:, b, :],
                                             op0=ALU.mult, op1=ALU.add))
                stats(X[:, b, :], 2, b, st2)

            for b in range(HX0):
                residual2(J2, e2a, b)

            def latent(b):
                dve.wait_ge(rs2, b + 1)
                standardise(b, 2).then_inc(z2d, 1)
                dve.wait_ge(z2d, b + 1)
                own(dve.tensor_tensor(X[:, b, :], X[:, b, :], bob[:, 2, :], ALU.add))

            def sum_squares(b):
                dve.wait_ge(e3a, J3.emptied(("qk", b))[1])
                own(dve.tensor_reduce(ssq[:, b, :], sqs.rearrange("p (h d) -> p h d", d=DH), AX.X, ALU.add))
                dve.tensor_scalar(ssq[:, b, :], ssq[:, b, :], 1.0 / DH, 1e-16, ALU.mult, ALU.max).then_inc(qss, 1)

            latent(0)

            def beside(key):
                name, b = key
                s = b % 2
                src = J3.bank(key)
                if name == "hx":
                    residual2(J3, e3a, b)
                elif name == "zt":
                    job(j3, J3, key)
                    for k in range(KD):
                        dve.tensor_scalar(zval[:, k, :], src[:, k * S:(k + 1) * S], colv[:, 4 + k:5 + k], colv[:, 6 + k:7 + k],
                                          ALU.mult, ALU.add).then_inc(e3v if k else link, 1)
                    chain[0] += 1
                    dve.wait_ge(link, chain[0])
                    dve.wait_ge(zh, b + 1)
                    dve.tensor_tensor(xTL[:, :, b * S:(b + 1) * S], zval[:, :, :], xTH[:, :, b * S:(b + 1) * S].bitcast(F),
                                      ALU.subtract).then_inc(zl, 1)
                    if b + 1 < NB:
                        latent(b + 1)
                elif name == "lg":
                    job(j3, J3, key)
                    dve.tensor_tensor(logit[:, b, :], src[0:S, 0:NE], rowb[0:S, 4:ROWS], ALU.add).then_inc(e3v, 1)
                elif name == "vl":
                    if key in BEFORE1:
                        sum_squares(b)
                elif name == "qt":
                    job(j3, J3, key)
                    own(dve.tensor_scalar(qT1[:, b, :, :], chunks(src[:, 0:2 * S], KD), qk_gain[:, 0:1], None, ALU.mult))
                    dve.tensor_copy(kT1[:, b, :, LP:NK1], chunks(src[:, 2 * S:4 * S], KD)).then_inc(e3v, 1)
                elif name == "ot":
                    low(J3, key, h3, oTl[:, s, 0:KD, :], chunks(src[:, 0:KD * S], KD), oTh[:, s, 0:KD, :]).then_inc(e3v, 1)
                elif name == "yt":
                    low(J3, key, h3, xTL[:, :, b * S:(b + 1) * S], chunks(src[:, 0:KD * S], KD), xTH[:, :, b * S:(b + 1) * S]).then_inc(e3v, 1)
                elif name == "wo":
                    job(j3, J3, key)
                    dve.scalar_tensor_tensor(out=X[:, b, :], in0=src[0:S, 0:D], scalar=gains[0:S, 1:2], in1=X[:, b, :],
                                             op0=ALU.mult, op1=ALU.add).then_inc(e3v, 1)
                    dve.wait_ge(e3v, J3.emptied(key)[1])
                    stats(X[:, b, :], 3, b, st3)

            for r, h in SLOTS1:
                g = r * H1 + h
                if h == 1 and real(r - 1):
                    normalise(NB + r - 1, HEADS0 + (r - 1) * H1, H1)
                if 0 <= g < HEADS1 and g % 2:
                    turned(HEADS0 + g, 4)
                if 0 <= g + 3 < HEADS1:
                    maximum(HEADS0 + g + 3, NK1)
                if h == 2 and ("vl", r + 2) in beside1(r, 1):
                    sum_squares(r + 2)
                if h == 1 and real(r - 2):
                    b = r - 2
                    dve.wait_ge(rs3, b + 1)
                    standardise(b, 3).then_inc(y4, 1)
                for key in beside1(r, h):
                    beside(key)
            def router_1():
                own(dve.memset(prob[:, :, NE:NE + 8], -1.0))
                own(dve.tensor_reduce(lmax[:, :], logit[:, :, :], AX.X, ALU.max))
                dve.tensor_tensor(logit[:, :, :], logit[:, :, :], lmax[:, :].unsqueeze(2).broadcast_to([S, NB, NE]), ALU.subtract).then_inc(lsub, 1)

            def router_2():
                dve.wait_ge(lexp, 1)
                own(dve.tensor_reduce(lsum[:, :], logit[:, :, :], AX.X, ALU.add))
                own(dve.reciprocal(lrec[:, :], lsum[:, :]))
                own(dve.tensor_tensor(prob[:, :, 0:NE], logit[:, :, :], lrec[:, :].unsqueeze(2).broadcast_to([S, NB, NE]), ALU.mult))

            def router_3():
                for b in range(NB):
                    dve.max(top[:, b, :], prob[:, b, 0:NE]).then_inc(link, 1)
                chain[0] += NB
                dve.wait_ge(link, chain[0])
                own(dve.memset(top[:, :, 4:8], -1.0))

            def router_4():
                for b in range(NB):
                    dve.match_replace(rest[:, b, :], in_to_replace=top[:, b, :], in_values=prob[:, b, :], imm_value=0.0).then_inc(link, 1)
                chain[0] += NB
                dve.wait_ge(link, chain[0])

            def router_5():
                own(dve.tensor_tensor(logit[:, :, :], prob[:, :, 0:NE], rest[:, :, 0:NE], ALU.subtract))
                own(dve.tensor_reduce(lsum[:, :], logit[:, :, :], AX.X, ALU.add))
                own(dve.tensor_scalar(lsum[:, :], lsum[:, :], 1e-12, None, ALU.max))
                own(dve.reciprocal(lrec[:, :], lsum[:, :]))
                own(dve.tensor_tensor(w3f[:, :, 0, :], logit[:, :, :], lrec[:, :].unsqueeze(2).broadcast_to([S, NB, NE]), ALU.mult))

            def router_6():
                w3 = w3b.rearrange("p b (i n) -> p b i n", i=3)
                for i in range(3):
                    if i < 2:
                        own(dve.tensor_copy(w3[:, :, i, :], w3f[:, :, i, :]))
                        own(dve.tensor_tensor(w3f[:, :, i + 1, :], w3f[:, :, i, :], w3[:, :, i, :], ALU.subtract))
                    else:
                        dve.tensor_copy(w3[:, :, i, :], w3f[:, :, i, :]).then_inc(w3r, 1)

            def expert(e, hf, routed, early):
                n = e * 2 + hf
                if routed:
                    dve.wait_ge(sild, n + 1)
                    dve.wait_ge(wbd, (e - NSH) * 2 + hf + 1)
                    dve.tensor_tensor(sw[:, hf, :], sil[:, hf, :], wbs[:, hf, :], ALU.mult).then_inc(swd, 1)
                    dve.wait_ge(swd, (e - NSH) * 2 + hf + 1)
                dve.wait_ge(u_ready, n + 1)
                dve.wait_ge(sild, n + 1)
                up = FIRST[1] if early else bank[1]
                dve.tensor_tensor(hid[:, hf, :], (sw if routed else sil)[:, hf, :], up[:, 0:HALF], ALU.mult).then_inc(prodd, 1)
                dve.wait_ge(hhi, n + 1)
                dve.tensor_tensor(hidL[:, hf, :], hid[:, hf, :], hidH[:, hf, :].bitcast(F), ALU.subtract).then_inc(hlo, 1)

            router_1()
            expert(0, 0, False, True)
            expert(0, 1, False, False)
            router_2()
            expert(1, 0, False, False)
            router_3()
            expert(1, 1, False, False)
            router_4()
            expert(2, 0, False, False)
            router_5()
            expert(2, 1, False, False)
            router_6()
            expert(3, 0, False, False)
            expert(3, 1, False, False)
            dve.wait_ge(j4, 1)
            dve.tensor_copy(wT3, bank[2][:, :].bitcast(BF)[0:96, 0:TOK]).then_inc(e4v, 1)
            with dve.Fori(NSH // 2, (NSH + NE) // 2) as i:
                for s in range(2):
                    for hf in range(2):
                        expert(2 * i + s, hf, True, False)
            dve.wait_ge(downd, 2 * (NSH + NE))
            for hf in range(2):
                dve.tensor_scalar(resT[:, 0, hf * HALF:(hf + 1) * HALF], bank[4 + hf][:, 0:HALF], gains[:, 3:4], None,
                                  ALU.mult).then_inc(oev, 1)
            for b in range(NB):
                dve.wait_ge(jf, b + 1)
                dve.tensor_tensor(X[:, b, :], bank[b][0:S, 0:D], X[:, b, :], ALU.add).then_inc(fin, 1)


def kernel(**inputs):
    import numpy as np
    import concourse.bacc as bacc
    from concourse.bass_utils import run_bass_kernel_spmd as run

    a = {k: np.asarray(v) for k, v in inputs.items()}
    eye = np.eye(128, dtype=np.float32)
    sel = np.kron(np.tile(np.eye(NE, dtype=np.float32), (3, 1)), np.ones((1, 128), np.float32))
    bf16 = mybir.dt.np(mybir.dt.bfloat16)

    def chunks(w):
        return w.reshape(-1, KD, 128, 128).transpose(0, 2, 1, 3).reshape(-1, 128, D)

    def pad(v):
        return np.concatenate([v, np.zeros(128 * KD - v.shape[0], v.dtype)]).reshape(KD, 128)

    gate_w = np.concatenate([a["L1_ffn_sgate_w"].reshape(NSH, 128, D), a["L1_ffn_gate_w"]])
    up_w = np.concatenate([a["L1_ffn_sup_w"].reshape(NSH, 128, D), a["L1_ffn_up_w"]])
    down_w = np.concatenate([a["L1_ffn_sdown_w"].reshape(D, NSH, 128).transpose(1, 0, 2), a["L1_ffn_down_w"]])
    cols = np.concatenate([pad(a["L1_xattn_ln_x_g"]), pad(a["L1_xattn_ln_x_b"]), pad(a["L1_xattn_ln_l_g"]), pad(a["L1_xattn_ln_l_b"]),
                           np.tile(a["L1_xattn_qn_g"], 2)[None], np.tile(a["L1_xattn_kn_g"], 2)[None], pad(a["L0_ffn_in_c"])])
    arrays = {
        "x": a["x"],
        "ctx": np.pad(a["ctx_768"], ((0, 0), (0, LP - L), (0, 0))),
        "ctx_t": np.pad(a["ctx_768"].transpose(2, 0, 1), ((0, 256 - C), (0, 0), (0, 1))),
        "mask": a["mask_BxS2_bk0"][None],
        "rows": np.concatenate([a["g_xattn"], a["g_ffn"], a["L0_xattn_bo"], a["L0_ffn_bo"], a["L1_xattn_bo"], a["L1_ffn_router_bias"], a["L0_ffn_in_c"]]),
        "gate_rows": np.tile(np.concatenate([a["L0_ffn_bf"], a["L0_ffn_bi"], a["L0_ffn_bc"], a["L0_ffn_bo"]])[None], (2, 1)),
        "cols": cols.T,
        "w0": np.stack([np.pad(a["L0_xattn_Wk"], ((0, 256 - C), (0, 0))), np.pad(a["L0_xattn_Wv"], ((0, 256 - C), (0, 0))), a["L0_xattn_Wq"]]),
        "wo0": a["L0_xattn_Wo"],
        "wffn": np.stack([a["L0_ffn_" + n].T for n in ("wf", "wi", "wc", "uf", "ui", "uc", "wo", "uo")]),
        "wlat": np.concatenate([a["L1_xattn_Wq"].T, a["L1_xattn_Wlkv"].T], 1),
        "wctx": np.pad(a["L1_xattn_Wkv"].T, ((0, 256 - C), (0, 0))),
        "wo1": a["L1_xattn_Wo"].T,
        "wrt": a["L1_ffn_router_w"].T,
        "wmoe": np.concatenate([chunks(gate_w.transpose(0, 2, 1)), chunks(up_w.transpose(0, 2, 1)), down_w.transpose(0, 2, 1)], 2),
        "ident_in": eye,
        "sel_in": sel.astype(bf16),
    }
    nc = bacc.Bacc("TRN2", target_bir_lowering=False, num_devices=1)
    feeds, aps = {}, []
    for name, v in arrays.items():
        v = np.ascontiguousarray(v)
        feeds["in_" + name] = v
        aps.append(nc.dram_tensor("in_" + name, v.shape, mybir.dt.from_np(v.dtype), kind="ExternalInput").ap())
    out = nc.dram_tensor("out_0", (NB, S, D), mybir.dt.float32, kind="ExternalOutput").ap()
    build(nc, *aps, out)
    r = run(nc, [feeds], core_ids=[0])
    return r.results[0]["out_0"]
```

```python
import concourse.bass as bass
from concourse import mybir
from contextlib import ExitStack

NB = 8
S = 100
D = 256
KD = D // 128
C = 192
CR = C - 128
L = 361
LT = 3
LP = LT * 128
LR = L - 2 * 128
H0 = 8
H1 = 4
DH = 64
I0 = H0 * DH
I1 = H1 * DH
NK1 = LP + S
NE = 32
NSH = 4
TOK = NB * S
HALF = TOK // 2
BIG = 1e30


class Jobs:

    def __init__(self, banks, seq):
        self.banks = banks
        self.at, self.kind, self.count, self.high = {}, {}, {}, {}
        self.left = []
        self.total = {"act": 0, "dve": 0}
        highs = 0
        for n, (key, kind) in enumerate(seq):
            eng = "act" if kind == "act" else "dve"
            self.total[eng] += 1
            self.at[key] = n
            self.count[key] = (eng, self.total[eng])
            if kind == "both":
                highs += 1
                self.high[key] = highs
            self.left.append(self.count[key])

    def bank(self, key):
        return self.banks[self.at[key] % len(self.banks)]

    def done(self, key):
        return self.at[key] + 1

    def emptied(self, key):
        return self.count[key]

    def before(self, key):
        n = self.at[key] - len(self.banks)
        return self.left[n] if n >= 0 else None


def build(nc, x, ctx, ctx_t, mask, rows, gate_rows, cols, w0, wo0, wffn, wlat, wctx, wo1, wrt, wmoe, ident_in, token_w, out):
    F = mybir.dt.float32
    R = mybir.dt.float32r
    BF = mybir.dt.bfloat16
    ALU = mybir.AluOpType
    ACT = mybir.ActivationFunctionType
    AX = mybir.AxisListType
    LE = L + 1

    with ExitStack() as stack, ExitStack() as early, ExitStack() as mid, ExitStack() as late:
        def sb(name, shape, dt=F, where=stack):
            return where.enter_context(nc.sbuf_tensor(name, shape, dt))

        def sem(name):
            return stack.enter_context(nc.semaphore(name))

        ident = sb("ident", [128, 128])
        ROWS = 4 + NE
        rowb = sb("rowb", [128, ROWS])
        GB = sb("GB", [2, 4 * D], R)
        ones2 = sb("ones2", [2, 128], R)
        onesb = sb("onesb", [1, 128], BF)
        maskb = sb("maskb", [2, NB, NK1], BF)
        colv = sb("colv", [128, 12])
        gains = sb("gains", [128, 4])
        qk_gain = sb("qk_gain", [128, 1])
        unit = sb("unit", [128, 1])
        nhalf = sb("nhalf", [128, 16])
        X = sb("X", [S, NB, D])
        xnfull = sb("XN", [128, NB * D])
        XN = xnfull[0:S, :].rearrange("p (b n) -> p b n", b=NB)
        WH = sb("WH", [128, 8 * KD * D], R)
        WL = sb("WL", [128, 8 * KD * D], R)
        Wrt = sb("Wrt", [128, KD, NE])
        Wrts = [sb(n, [128, KD, NE], R) for n in ("WrtH", "WrtL")]
        P = sb("P", [S, 3, 512])
        PTs = sb("PTs", [128, 2, 4 * S])
        osb = sb("osb", [S, 2, I0])
        oTh = sb("oTh", [128, 2, 4, S], R)
        oTl = sb("oTl", [128, 2, 4, S], R)
        bn = sb("bn", [S, 6])
        bnc = sb("bnc", [128, LT, 6])
        MV = sb("MV", [128, 4, NB, 2])
        RS = sb("RS", [128, 4, NB])
        mvc = sb("mvc", [128, 2, LT, 2])
        rstdc = sb("rstdc", [128, 2, LT])
        ssk = sb("ssk", [128, 2, LT * H1])
        rk = sb("rk", [128, 2, LT * H1])
        ssq = sb("ssq", [S, NB, 8])
        rq = sb("rq", [S, NB, 8])
        nmax = sb("nmax", [S, 96])
        esum = sb("esum", [S, 96])
        bob = sb("bob", [S, 3, D])
        lmax = sb("lmax", [S, NB])
        lsum = sb("lsum", [S, NB])
        lrec = sb("lrec", [S, NB])

        def halves(t, lo, hi, k):
            return t[:, lo:hi].rearrange("p (k n) -> p k n", k=k)

        WF = [t[:, :].rearrange("p (g k n) -> p g k n", g=8, k=KD) for t in (WH, WL)]
        Wlat = [halves(t, 0, 6 * D, KD) for t in (WH, WL)]
        Wo1 = [halves(t, 6 * D, 8 * D, KD) for t in (WH, WL)]
        Wexp = [halves(t, 8 * D, 14 * D, 2) for t in (WH, WL)]

        xTH = sb("xTH", [128, KD, TOK], R)
        xTL = sb("xTL", [128, KD, TOK], R)

        cells = [sb(n, [128, KD, S], R) for n in ("cellH", "cellL")]

        W0 = [sb(n, [128, 4, KD, I0], R, early) for n in ("W0H", "W0L")]
        Wk0, Wv0, Wq0, Wo0 = ([t[:, i, :, :] for t in W0] for i in range(4))
        Wo0 = [t.rearrange("p k (a n) -> p (k a) n", n=D) for t in Wo0]
        kT0 = [sb(n, [128, 2, 4, LE], R, early) for n in ("kT0H", "kT0L")]
        v0 = sb("v0", [128, 2, LT, I0], F, early)
        cT = sb("cT", [128, 2, 2, LE], F, early)
        cTs = [sb(n, [128, 2, 2, LE], R, early) for n in ("cTH", "cTL")]
        qT0 = [sb(n, [128, 2, 4, 2 * S], R, early) for n in ("qT0H", "qT0L")]
        xnT0 = [sb(n, [128, KD, 2 * S], R, early) for n in ("xnT0H", "xnT0L")]
        raw = sb("raw", [128, 2, KD * I0], F, early)
        rawq = xnfull[:, 4 * D:8 * D]
        GBraw = maskb[:, :, :].rearrange("p b n -> p (b n)")[:, 0:8 * D].bitcast(F)
        early.close()

        kT1 = sb("kT1", [128, NB, KD, NK1], F, mid)
        V1 = sb("V1", [128, NB, LT + 1, I1], F, mid)
        k1flat = kT1[:, :, :, :].rearrange("p b k n -> p (b k n)")
        v1flat = V1[:, :, :, :].rearrange("p b t n -> p (b t n)")
        ctok = xnfull[:, 0:2 * LT * C].rearrange("p (s t n) -> p s t n", s=2, t=LT)
        cval = xnfull[:, 2 * LT * C:2 * LT * C + 2 * LP].rearrange("p (k n) -> p k n", k=2)
        mask8 = sb("mask8", [1, NB, L], mybir.dt.uint8, mid)
        th = sb("th", [S, 2, D], F, mid)
        rawlat = sb("rawlat", [128, 8 * D], F, mid)
        kraw = sb("kraw", [128, 2, LT, I1], F, late)
        ksq = sb("ksq", [128, LT, I1], F, late)
        cnT = [sb(n, [128, 2, LP], R, late) for n in ("cnTH", "cnTL")]
        Wctx = [sb(n, [128, 2, 2 * I1], R, late) for n in ("WctxH", "WctxL")]
        ctxraw = kraw[:, :, :, :].rearrange("p s t n -> p (s t n)")[:, 0:4 * I1].rearrange("p (k n) -> p k n", k=2)
        gate_s = sb("gate_s", [S, 2 * D], F, late)
        gate_t = sb("gate_t", [S, D], F, late)
        fc = sb("fc", [S, D], F, late)
        ig = sb("ig", [S, D], F, late)
        cell = sb("cell", [S, 2, D], F, late)
        late.close()
        after = mid
        hidH = sb("hidH", [128, 2, HALF], R, after)
        hidL = sb("hidL", [128, 2, HALF], R, after)
        qkraw = sb("qkraw", [S, 2, 2 * I1], F, after)
        qT1 = sb("qT1", [128, NB, KD, S], F, after)
        sqs = sb("sqs", [S, 2 * I1], F, after)[:, :]
        wraw = sb("wraw", [128, 2, 3 * D], F, after)
        logit = sb("logit", [S, NB, NE], F, after)
        zval = sb("zval", [128, KD, S], F, after)

        def take(flat, n, parts=128):
            take.o += n
            return flat[0:parts, take.o - n:take.o]

        take.o = 0
        sil, sw, hid = (take(k1flat, TOK).rearrange("p (h n) -> p h n", h=2) for _ in range(3))
        wbs = take(k1flat, 2 * TOK).rearrange("p (s n) -> p s n", s=2)
        resT = take(k1flat, 2 * TOK).rearrange("p (k n) -> p k n", k=KD)
        take.o = 0
        prob = take(v1flat, NB * (NE + 8), S).rearrange("p (b n) -> p b n", b=NB)
        rest = take(v1flat, NB * (NE + 8), S).rearrange("p (b n) -> p b n", b=NB)
        top = take(v1flat, NB * 8, S).rearrange("p (b n) -> p b n", b=NB)
        w = take(v1flat, NB * NE, S).rearrange("p (b n) -> p b n", b=NB)
        wT = take(v1flat, TOK, NE)
        mid.close()
        bank = [stack.enter_context(nc.psum_tensor(f"bank{i}", [128, 512], F)) for i in range(8)]

        names = ["ld_x", "ld_small", "ld_wk", "ld_wv", "ld_wq", "ld_wo", "ld_w1", "ld_lat", "w_stored", "ld_mask", "ld_c0", "mask_set", "ctd",
                 "init",
                 "initv",
                 "link",
                 "plink",
                 "alink",
                 "tanh_g", "whi", "zeroed", "wsplit0", "wo_split", "wf_split", "gb_split", "ct_split",
                 "st0", "rs0", "xn0",
                 "j1", "e1a", "e1v", "h1",
                 "scored", "maxed", "expd", "ptd", "pt_a", "pt_v", "pvd", "normed",
                 "st1", "rs1", "xn1", "j2", "e2a", "e2v", "h2",
                 "gated", "sigd", "tand", "celld", "cell_hi", "cell_lo",
                 "cst", "cnd", "crs", "cnh", "cnl", "kss", "knd", "wrt_split", "wctx_hi", "wctx_split", "lat_hi", "lat_lo", "wo1_lo",
                 "st2", "rs2", "z2d", "zh", "zl", "j3", "e3a", "e3v", "h3", "qss", "qknd",
                 "st3", "rs3", "y4", "j4", "e4v", "lsub", "lexp", "w_done",
                 "g_ready", "u_ready", "sild", "swd", "prodd", "hhi", "hlo", "downd", "wes",
                 "oev", "oea", "jf", "fin", "stored"]
        sems = {n: sem(n) for n in names}
        (ld_x, ld_small, ld_wk, ld_wv, ld_wq, ld_wo, ld_w1, ld_lat, w_stored, ld_mask, ld_c0, mask_set, ctd, init, initv, link, plink, alink,
         tanh_g, whi, zeroed, wsplit0, wo_split, wf_split, gb_split, ct_split, st0, rs0, xn0, j1, e1a, e1v, h1, scored, maxed, expd, ptd,
         pt_a, pt_v, pvd, normed, st1, rs1, xn1, j2, e2a, e2v, h2, gated, sigd, tand, celld, cell_hi, cell_lo, cst, cnd, crs,
         cnh, cnl, kss, knd, wrt_split, wctx_hi, wctx_split, lat_hi, lat_lo, wo1_lo, st2, rs2, z2d, zh, zl, j3, e3a, e3v, h3, qss, qknd,
         st3, rs3, y4, j4, e4v, lsub, lexp, w_done, g_ready, u_ready, sild, swd, prodd, hhi, hlo, downd, wes,
         oev, oea, jf, fin, stored) = (sems[n] for n in names)
        ld_ct = [sem("ld_ct0"), sem("ld_ct1")]
        ld_ck = [sem("ld_ck0"), sem("ld_ck1")]
        ld_wf = [sem("ld_wf0"), sem("ld_wf1")]
        ld_wb = [sem("ld_wb0"), sem("ld_wb1")]
        ld_we = [sem("ld_we0"), sem("ld_we1")]

        def beside0(b, h):
            n = b + 1
            table = {0: [("xt", n)], 1: [("k", n, 0)], 2: [("q", n, 0), ("ot", b - 1)], 3: [("q", n, 1), ("k", n, 1)],
                     4: [("k", n, 2), ("wo", b - 1)], 5: [("k", n, 3), ("x1", b - 2)], 6: [("v", n, 0), ("v", n, 1)], 7: [("v", n, 2)]}
            return [key for key in table[h] if 0 <= key[1] < NB and (key[0] not in ("xt", "q") or key[1] % 2 == 0)]

        BEFORE0 = [("k", 0, c) for c in range(4)] + [("xt", 0), ("v", 0, 0), ("v", 0, 1), ("q", 0, 0), ("q", 0, 1), ("v", 0, 2)]
        AFTER0 = [("x1", NB - 2), ("ot", NB - 1), ("wo", NB - 1), ("x1", NB - 1)]

        def left_by(key):
            if key[0] == "v":
                return "dve" if key[2] == LT - 1 else "act"
            return "dve" if key[0] == "wo" else "both"

        J1 = Jobs([bank[0], bank[1], bank[6]], [(key, left_by(key)) for key in BEFORE0 + [k for b in range(NB) for h in range(H0) for k in beside0(b, h)] + AFTER0])
        seq = []
        for t in range(NB + 1):
            if t == NB:
                seq += [(("hx", 0), "act"), (("hx", 1), "act")]
            if t > 0:
                seq += [(("kv", t - 1, i), "act") for i in range(LT)]
            if t < NB:
                seq += [(("ct", t, i), "dve") for i in range(LT)]
            else:
                seq += [(("hx", 2), "act")]
            if t > 1:
                seq += [(("kt", t - 2, i), "act") for i in range(LT)]
        HX0 = 4
        seq += [(("hx", 3), "act")]
        J2 = Jobs([bank[0], bank[1], bank[6], bank[7]], seq)
        ROUNDS = range(-1, NB + 3)

        def real(b):
            return 0 <= b < NB

        BEFORE1 = [("zt", 0), ("hx", HX0)] + [("kt", i) for i in range(LT)] + [("qk", 0), ("vl", 0), ("zt", 1), ("hx", HX0 + 1), ("qk", 1), ("vl", 1), ("qt", 0), ("hx", HX0 + 2)]

        def beside1(r, h):
            if (r, h) == (-1, 0):
                return BEFORE1
            table = {0: [("qt", r + 1)], 1: [("qk", r + 2), ("vl", r + 2), ("lg", r - 3)], 2: [("ot", r - 1)],
                     3: [("zt", r + 3), ("wo", r - 1), ("yt", r - 2)]}
            if (r, h) == (0, 2):
                return [("hx", NB - 1)]
            return [key for key in table[h] if real(key[1]) and key not in BEFORE1]

        LEFT1 = {"hx": "act", "zt": "dve", "qt": "dve", "ot": "both", "qk": "act", "vl": "act", "wo": "dve", "yt": "both", "lg": "dve", "kt": "act"}
        SLOTS1 = [(r, h) for r in ROUNDS for h in range(H1)]
        J3 = Jobs([bank[0], bank[1], bank[6]], [(key, LEFT1[key[0]]) for r, h in SLOTS1 for key in beside1(r, h)])
        HEADS0 = NB * H0
        HEADS1 = NB * H1
        FIRST = (bank[2], bank[3])
        SBANK = [bank[2], bank[3]]
        AHEAD = len(SBANK)

        block = stack.enter_context(nc.Block())

        @block.sync
        def _(sp):
            def load_ct(b):
                s = b % 2
                if b >= 2:
                    sp.wait_ge(ct_split, b - 1)
                sp.dma_start(cT[:, s, :, :], ctx_t[:, b, :].rearrange("(k p) n -> p k n", p=128)).then_inc(ld_ct[s], 16)

            def load_ck(b):
                s = b % 2
                if b >= 2:
                    sp.wait_ge(j2, J2.done(("ct", b - 2, LT - 1)))
                sp.dma_start(ctok[:, s, :, :], ctx[b, :, :].rearrange("(t p) c -> p t c", p=128)).then_inc(ld_ck[s], 16)

            def as_rows(w):
                return w.rearrange("(k p) n -> p k n", p=128)

            load_ct(0)
            for g, s in ((0, ld_wk), (1, ld_wv)):
                sp.dma_start(raw[:, g, :].rearrange("p (k n) -> p k n", k=KD), as_rows(w0[g, :, :])).then_inc(s, 16)
                if g == 1:
                    sp.dma_start(ident[:, :], ident_in).then_inc(ld_x, 16)
                    sp.dma_start(X[:, :, :], x.rearrange("b s d -> s b d")).then_inc(ld_x, 16)
                    sp.dma_start(rawq.rearrange("p (k n) -> p k n", k=KD), as_rows(w0[2, :, :])).then_inc(ld_wq, 16)
            load_ct(1)
            sp.wait_ge(wsplit0, 1)
            sp.dma_start(raw[:, 0, :].rearrange("p (k n) -> p k n", k=4), as_rows(wo0)).then_inc(ld_wo, 16)
            sp.dma_start(Wrt[:, :, :], as_rows(wrt)).then_inc(ld_w1, 16)
            for i in range(4):
                load_ct(i + 2)
                if i == 0:
                    sp.wait_ge(wsplit0, 2)
                elif i == 1:
                    sp.wait_ge(wo_split, 1)
                else:
                    sp.wait_ge(wf_split, i - 1)
                sp.dma_start(raw[:, (i + 1) % 2, :].rearrange("p (g k n) -> p g k n", g=2, k=KD),
                             wffn[2 * i:2 * i + 2, :, :].rearrange("g (k p) n -> p g k n", p=128)).then_inc(ld_wf[(i + 1) % 2], 16)
            for b in range(6, NB):
                load_ct(b)
            sp.wait_ge(j1, J1.done(("x1", NB // 2)))
            load_ck(0)
            load_ck(1)
            sp.wait_ge(j1, len(J1.left))
            sp.wait_ge(wf_split, 4)
            sp.dma_start(cell[:, 0, :], rows[4 + 3 * D + NE:4 + 4 * D + NE].partition_broadcast(S)).then_inc(ld_c0, 16)
            sp.dma_start(ctxraw, as_rows(wctx)).then_inc(ld_w1, 16)
            sp.dma_start(mask8[:, :, :], mask).then_inc(ld_mask, 16)
            sp.dma_start(rawlat[:, 0:6 * D].rearrange("p (k n) -> p k n", k=KD), as_rows(wlat)).then_inc(ld_lat, 16)
            sp.dma_start(rawlat[:, 6 * D:8 * D].rearrange("p (k n) -> p k n", k=KD), as_rows(wo1)).then_inc(ld_lat, 16)
            for b in range(2, NB):
                load_ck(b)
            sp.wait_ge(j2, len(J2.left))
            sp.wait_ge(cell_lo, NB + 1)
            for e in range(2):
                sp.dma_start(wraw[:, e, :], wmoe[e, :, :]).then_inc(ld_we[e], 16)
            sp.wait_ge(pvd, HEADS0 + NB * H1)
            def load_expert(e, s):
                sp.dma_start(wraw[:, s, :], wmoe[bass.ds(e, 1), :, :].rearrange("a p n -> p (a n)")).then_inc(ld_we[s], 16)

            def load_weights(r, s):
                sp.dma_start(wbs[:, s, :], token_w[bass.ds(r, 1), :].rearrange("a n -> (a n)").partition_broadcast(128)).then_inc(ld_wb[s], 16)

            for e in range(2, NSH):
                sp.wait_ge(wes, 4 * (e - 1))
                load_expert(e, e % 2)
            for s in range(2):
                sp.wait_ge(wes, 4 * (NSH + s - 1))
                load_expert(NSH + s, s)
                if s == 0:
                    sp.wait_ge(e4v, 2)
                    sp.dma_start(token_w, wT).then_inc(w_stored, 16)
                    sp.wait_ge(w_stored, 16)
                load_weights(s, s)
            with sp.Fori(NSH // 2 + 1, (NSH + NE) // 2) as i:
                for s in range(2):
                    sp.wait_ge(wes, 8 * i + (4 * s - 4))
                    load_expert(2 * i + s, s)
                    sp.wait_ge(swd, 4 * i + (2 * s - 2 * NSH - 2))
                    load_weights(2 * i + (s - NSH), s)
            for b in range(NB):
                sp.wait_ge(fin, b + 1)
                sp.dma_start(out[b, :, :], X[:, b, :]).then_inc(stored, 16)
            sp.wait_ge(stored, 16 * NB)

        @block.gpsimd
        def _(pool):
            chain = [0]

            def own(ins):
                chain[0] += 1
                ins.then_inc(plink, 1)
                pool.wait_ge(plink, chain[0])

            def split(dst, src, done):
                own(pool.tensor_tensor(dst[0], src, unit[:, 0:1].broadcast_to(list(src.shape)), ALU.mult))
                pool.tensor_tensor(dst[1], src, dst[0].bitcast(F), ALU.subtract).then_inc(done, 1)

            def power(dst, src, width):
                return pool.tensor_tensor(dst, src, nhalf[0:dst.shape[0], 0:width], ALU.pow)

            pool.dma_start(rowb[:, 0:4], rows[0:4].partition_broadcast(128)).then_inc(ld_small, 16)
            pool.dma_start(bob[:, :, :], rows[4:4 + 3 * D].partition_broadcast(S)).then_inc(ld_small, 16)
            pool.dma_start(colv[:, :], cols).then_inc(ld_small, 16)
            pool.dma_start(GBraw, gate_rows).then_inc(ld_small, 16)
            pool.dma_start(rowb[:, 4:ROWS], rows[4 + 3 * D:4 + 3 * D + NE].partition_broadcast(128)).then_inc(ld_small, 16)
            pool.memset(nhalf[:, :], -0.5).then_inc(init, 1)
            pool.memset(unit[:, :], 1.0).then_inc(init, 1)
            pool.wait_ge(zeroed, 1)
            pool.tensor_scalar(ones2[:, :], P[0:2, 0, 0:128], 1.0, None, ALU.add).then_inc(init, 1)
            pool.memset(onesb[:, :], 1.0).then_inc(init, 1)

            def split_ct(b):
                s = b % 2
                pool.wait_ge(ld_ct[s], 16 * (b // 2 + 1))
                pool.wait_ge(ct_split, b)
                if b >= 2:
                    pool.wait_ge(j1, J1.done(("v", b - 2, 2)))
                own(pool.tensor_tensor(cTs[0][:, s, :, :], cT[:, s, :, :], unit[:, 0:1].unsqueeze(2).broadcast_to([128, 2, LE]), ALU.mult))
                pool.tensor_tensor(cTs[1][:, s, :, :], cT[:, s, :, :], cTs[0][:, s, :, :].bitcast(F), ALU.subtract).then_inc(ct_split, 1)

            pool.wait_ge(init, 4)
            pool.wait_ge(ld_small, 80)
            pool.wait_ge(ld_x, 32)

            def power0(b):
                pool.wait_ge(st0, b + 1)
                power(RS[0:S, 0, b:b + 1], MV[0:S, 0, b, 1:2], 1).then_inc(rs0, 1)

            power0(0)
            power0(1)
            split_ct(1)
            pool.wait_ge(ld_wo, 16)
            split([Wo0[i].rearrange("p k n -> p (k n)") for i in range(2)], raw[:, 0, :], wo_split)
            def context_scale(b):
                s = b % 2
                pool.wait_ge(cst, b + 1)
                power(rstdc[:, s, :], mvc[:, s, :, 1], LT).then_inc(crs, 1)

            for b in range(NB):
                if b + 2 < NB:
                    split_ct(b + 2)
                if b == NB - 1:
                    context_scale(0)
                    context_scale(1)
                if b % 2 == 0 and b + 2 < NB:
                    power0(b + 2)
                    power0(b + 3)
                if b:
                    pool.wait_ge(st1, b)
                    power(RS[0:S, 1, b - 1:b], MV[0:S, 1, b - 1, 1:2], 1).then_inc(rs1, 1)
                if b == 2:
                    width = [2, 4 * D]
                    own(pool.tensor_tensor(GB[:, :], GBraw, unit[0:2, 0:1].broadcast_to(width), ALU.mult))
                    own(pool.tensor_tensor(GBraw, GBraw, GB[:, :].bitcast(F), ALU.subtract))
                    own(pool.tensor_tensor(GBraw, GBraw, ident[0:2, 1:2].broadcast_to(width), ALU.mult))
                    own(pool.tensor_tensor(GB[:, :], GB[:, :].bitcast(F), ident[0:2, 0:1].broadcast_to(width), ALU.mult))
                    pool.tensor_tensor(GB[:, :], GBraw, GB[:, :].bitcast(F), ALU.add).then_inc(gb_split, 1)
                if b % 2:
                    i, n = b // 2, 2 * KD * D
                    pool.wait_ge(ld_wf[(i + 1) % 2], 16 * (i // 2 + 1))
                    split([WH[:, i * n:(i + 1) * n], WL[:, i * n:(i + 1) * n]], raw[:, (i + 1) % 2, :], wf_split)
            pool.wait_ge(st1, NB)
            power(RS[0:S, 1, NB - 1:NB], MV[0:S, 1, NB - 1, 1:2], 1).then_inc(rs1, 1)

            def scale_keys(b):
                s = b % 2
                pool.wait_ge(kss, b + 1)
                own(power(rk[:, s, :], ssk[:, s, :], LT * H1))
                view = kraw[:, s, :, :].rearrange("p t (h d) -> p (t h) d", d=DH)
                pool.tensor_tensor(view, view,
                                   rk[:, s, :].unsqueeze(2).broadcast_to([128, LT * H1, DH]), ALU.mult).then_inc(knd, 1)

            def latent_scale(b):
                pool.wait_ge(st2, b + 1)
                power(RS[0:S, 2, b:b + 1], MV[0:S, 2, b, 1:2], 1).then_inc(rs2, 1)

            pool.wait_ge(ld_mask, 16)
            pool.wait_ge(gb_split, 1)
            for t in range(NB + 1):
                if t == NB:
                    latent_scale(0)
                    latent_scale(1)
                if t > 0:
                    scale_keys(t - 1)
                if t + 2 < NB:
                    context_scale(t + 2)
                if t < NB:
                    pool.memset(maskb[0:1, t, L:LP], -BIG)
                    pool.memset(maskb[0:1, t, LP:NK1], 0.0)
                    pool.tensor_scalar(maskb[0:1, t, 0:L], mask8[:, t, :], BIG, -BIG, ALU.mult, ALU.add).then_inc(mask_set, 1)
                if t == NB - 1:
                    pool.wait_ge(lat_hi, 1)
                    pool.tensor_tensor(WL[:, 6 * D:8 * D], rawlat[:, 6 * D:8 * D], WH[:, 6 * D:8 * D].bitcast(F), ALU.subtract).then_inc(wo1_lo, 1)
            for b in range(2, HX0):
                latent_scale(b)

            def split_expert(e, s, first):
                pool.wait_ge(ld_we[s], (e - s) * 8 + 16)
                for i, (lo, hi, used) in enumerate(((0, 2 * D, u_ready), (2 * D, 3 * D, downd))):
                    if not first:
                        pool.wait_ge(used, (e - 1) * 2)
                    width = [128, hi - lo]
                    pool.tensor_tensor(Wexp[0][:, s, lo:hi], wraw[:, s, lo:hi], unit[:, 0:1].broadcast_to(width), ALU.mult).then_inc(wes, 1)
                    pool.wait_ge(wes, e * 4 + (2 * i + 1))
                    pool.tensor_tensor(Wexp[1][:, s, lo:hi], wraw[:, s, lo:hi], Wexp[0][:, s, lo:hi].bitcast(F), ALU.subtract).then_inc(wes, 1)

            def scale_qk(b):
                view = qkraw[:, b % 2, :].rearrange("p (h d) -> p h d", d=DH)
                pool.wait_ge(qss, b + 1)
                own(power(rq[:, b, :], ssq[:, b, :], 8))
                pool.tensor_tensor(view, view, rq[:, b, :].unsqueeze(2).broadcast_to([S, 8, DH]), ALU.mult).then_inc(qknd, 1)

            for r, h in SLOTS1:
                for name, b in beside1(r, h):
                    if name == "vl":
                        scale_qk(b)
                    elif name == "hx":
                        latent_scale(b)
                if h == 3 and real(r - 1):
                    b = r - 1
                    pool.wait_ge(st3, b + 1)
                    power(RS[0:S, 3, b:b + 1], MV[0:S, 3, b, 1:2], 1).then_inc(rs3, 1)
                if h == 0 and r in (5, 6):
                    if r == 5:
                        pool.wait_ge(j3, J3.done(("hx", NB - 1)))
                    split_expert(r - 5, r - 5, True)

            for e in range(2, NSH):
                split_expert(e, e % 2, False)
            with pool.Fori(NSH // 2, (NSH + NE) // 2) as i:
                for s in range(2):
                    split_expert(2 * i + s, s, False)

        @block.tensor
        def _(pe):
            def empty(jobs, key, ev):
                before = jobs.before(key)
                if before:
                    pe.wait_ge(ev[before[0]], before[1])

            def emptied(jobs, key, ev):
                eng, n = jobs.emptied(key)
                pe.wait_ge(ev[eng], n)

            E1 = {"act": e1a, "dve": e1v}
            E2 = {"act": e2a, "dve": e2v}
            E3 = {"act": e3a, "dve": e3v}

            def product(dst, w, v, start, stop, skip=False):
                pe.matmul(dst, w[0], v[0], start=start, stop=False, skip_group_check=skip)
                pe.matmul(dst, w[0], v[1], start=False, stop=False, skip_group_check=skip)
                return pe.matmul(dst, w[1], v[0], start=False, stop=stop, skip_group_check=skip)

            def at(pair, *index):
                return [t[index] for t in pair]

            def score(g, q, k, nk, mask_row):
                if g >= AHEAD:
                    pe.wait_ge(expd, g + 1 - AHEAD)
                dst = SBANK[g % AHEAD][0:S, 0:nk]
                if mask_row is not None:
                    pe.matmul(dst, onesb[0:1, 0:S], mask_row, start=True, stop=False)
                    pe.matmul(dst, q, k, start=False, stop=True).then_inc(scored, 1)
                else:
                    product(dst, q, k, True, True).then_inc(scored, 1)

            def pt_wait(g):
                pe.wait_ge(pt_v if g % 2 else pt_a, g // 2 + 1)

            def turn(g, tiles):
                pe.wait_ge(expd, g + 1)
                if g >= 2:
                    pt_wait(g - 2)
                for i in range(tiles):
                    m = pe.transpose(bank[4 + g % 2][:, i * S:(i + 1) * S], P[:, g % 3, i * 128:(i + 1) * 128], ident[0:S, 0:S])
                m.then_inc(ptd, 1)

            def values(g, h, bt, vals, rows_):
                pt_wait(g)
                if h == 0 and bt >= 1:
                    pe.wait_ge(normed, bt)
                n = len(rows_)
                for i, k in enumerate(rows_):
                    m = pe.matmul(bank[7][0:S, h * DH:(h + 1) * DH], PTs[0:k, g % 2, i * S:(i + 1) * S], vals(i, k),
                                  start=i == 0, stop=i == n - 1)
                m.then_inc(pvd, 1)

            def turn_rows(jobs, key, sem_out, src, n):
                for k in range(n):
                    m = pe.transpose(jobs.bank(key)[:, k * S:(k + 1) * S], src[:, k * 128:(k + 1) * 128], ident[0:S, 0:S])
                m.then_inc(sem_out, 1)

            def beside(key):
                name, b = key[0:2]
                empty(J1, key, E1)
                dst = J1.bank(key)
                if name == "xt":
                    if b == 0:
                        pe.wait_ge(ld_x, 32)
                    pe.wait_ge(xn0, b + 2)
                    for k in range(KD):
                        for i in range(2):
                            m = pe.transpose(dst[:, (k * 2 + i) * S:(k * 2 + i + 1) * S], XN[:, b + i, k * 128:(k + 1) * 128], ident[0:S, 0:S])
                elif name == "x1":
                    pe.wait_ge(xn1, b + 1)
                    turn_rows(J1, key, j1, XN[:, b, :], KD)
                elif name == "k":
                    c = key[2]
                    pe.wait_ge(ct_split, b + 1)
                    if b == 0:
                        pe.wait_ge(wsplit0, 1)
                    for k, r in ((0, 128), (1, CR)):
                        m = product(dst[:, 0:LE], [w[0:r, k, c * 128:(c + 1) * 128] for w in Wk0],
                                    [t[0:r, b % 2, k, :] for t in cTs], k == 0, k == 1)
                elif name == "v":
                    i = key[2]
                    n = min(128, L - i * 128)
                    if b == 0:
                        pe.wait_ge(wsplit0, 2)
                    for k, r in ((0, 128), (1, CR)):
                        m = product(dst[0:n, :], [t[0:r, b % 2, k, i * 128:i * 128 + n] for t in cTs],
                                    [w[0:r, k, :] for w in Wv0], k == 0, k == 1)
                elif name == "q":
                    if b == 0:
                        pe.wait_ge(wsplit0, 3)
                    emptied(J1, ("xt", b), E1)
                    for i in range(2):
                        c = key[2] * 2 + i
                        for k in range(KD):
                            m = product(dst[:, i * 2 * S:(i + 1) * 2 * S], [w[:, k, c * 128:(c + 1) * 128] for w in Wq0],
                                        [t[:, k, :] for t in xnT0], k == 0, k == KD - 1)
                elif name == "ot":
                    pe.wait_ge(normed, b + 1)
                    turn_rows(J1, key, j1, osb[:, b % 2, :], 4)
                else:
                    if b == 0:
                        pe.wait_ge(wo_split, 1)
                    emptied(J1, ("ot", b), E1)
                    for c in range(4):
                        m = product(dst[0:S, 0:D], [t[:, b % 2, c, :] for t in (oTh, oTl)], [w[:, c, :] for w in Wo0], c == 0, c == 3)
                if name in ("x1", "ot"):
                    return
                m.then_inc(j1, 1)

            def score0(g):
                b, h = divmod(g, H0)
                o = 64 * (h % 2)
                if h == 0:
                    emptied(J1, ("q", b - b % 2, 1), E1)
                if h % 2 == 0:
                    emptied(J1, ("k", b, h // 2), E1)
                lo = b % 2 * S
                score(g, [t[o:o + 64, b // 2 % 2, h // 2, lo:lo + S] for t in qT0], [t[o:o + 64, b % 2, h // 2, :] for t in kT0], LE, None)

            def values0(g):
                b, h = divmod(g, H0)
                if h == 0:
                    for i in range(LT):
                        emptied(J1, ("v", b, i), E1)
                values(g, h, b, lambda i, k: v0[0:k, b % 2, i, h * DH:(h + 1) * DH], [128, 128, LR])

            def keep_busy(n):
                for i in range(n):
                    pe.matmul(bank[7][0:S, :], P[:, 0, 0:S], P[:, 1, :], start=True, stop=True)

            pe.wait_ge(zeroed, 1)
            keep_busy(4)
            for key in BEFORE0:
                if key == ("k", 0, 3):
                    keep_busy(1)
                if key == ("xt", 0):
                    keep_busy(3)
                beside(key)
            for g in range(AHEAD):
                score0(g)
            pe.wait_ge(init, 4)
            for g in range(HEADS0):
                turn(g, LT)
                if g + AHEAD < HEADS0:
                    score0(g + AHEAD)
                for key in beside0(g // H0, g % H0):
                    beside(key)
                if g:
                    values0(g - 1)
            def gate_banks(t):
                a = 2 + 2 * (t % 2)
                return (bank[a][0:S, :], slice(0, 2)), (bank[a + 1][0:S, 0:D], slice(2, 3))

            def gates_x(t):
                if t >= 2:
                    pe.wait_ge(sigd, t - 1)
                    pe.wait_ge(tand, t - 1)
                for dst, g in gate_banks(t):
                    pe.matmul(dst, ones2[:, 0:S], GB[:, g.start * D:g.stop * D], start=True, stop=False, skip_group_check=True)
                    for k in range(KD):
                        product(dst, [v[:, k, t * S:(t + 1) * S] for v in (xTH, xTL)], [w[:, g, k, :] for w in WF], False, False, True)

            def gates_c(t):
                pe.wait_ge(cell_hi, t + 1)
                for dst, g in gate_banks(t):
                    for k in range(KD):
                        for w in WF:
                            pe.matmul(dst, cells[0][:, k, :], w[:, slice(3 + g.start, 3 + g.stop), k, :], start=False, stop=False,
                                      skip_group_check=True)
                pe.wait_ge(cell_lo, t + 1)
                for dst, g in gate_banks(t):
                    for k in range(KD):
                        last = pe.matmul(dst, cells[1][:, k, :], WF[0][:, slice(3 + g.start, 3 + g.stop), k, :], start=False,
                                         stop=k == KD - 1, skip_group_check=True)
                    last.then_inc(gated, 1)

            values0(HEADS0 - 1)
            for key in AFTER0:
                if key == ("ot", NB - 1):
                    pe.wait_ge(gb_split, 1)
                    pe.wait_ge(wf_split, 2)
                    pe.wait_ge(expd, HEADS0)
                    gates_x(0)
                if key == ("wo", NB - 1):
                    pt_wait(HEADS0 - 2)
                    pt_wait(HEADS0 - 1)
                    gates_x(1)
                if key == ("x1", NB - 1):
                    pe.wait_ge(wf_split, 3)
                    gates_c(0)
                beside(key)

            pe.wait_ge(wf_split, 4)
            pe.wait_ge(e1v, J1.total["dve"])
            pe.wait_ge(normed, NB)
            def context_turn(b):
                s = b % 2
                pe.wait_ge(cnd, b + 1)
                for i in range(LT):
                    key = ("ct", b, i)
                    empty(J2, key, E2)
                    for k, r in ((0, 128), (1, CR)):
                        m = pe.transpose(J2.bank(key)[0:r, k * 128:(k + 1) * 128], ctok[:, s, i, k * 128:k * 128 + r], ident[:, :])
                    m.then_inc(j2, 1)

            def context_kv(b, tiles):
                if b == 0:
                    pe.wait_ge(wctx_split, 1)
                pe.wait_ge(cnl, b + 1)
                for i in tiles:
                    key = ("kv", b, i)
                    empty(J2, key, E2)
                    for k, r in ((0, 128), (1, CR)):
                        m = product(J2.bank(key)[:, :], [t[0:r, k, i * 128:(i + 1) * 128] for t in cnT],
                                    [w[0:r, k, :] for w in Wctx], k == 0, k == 1)
                    m.then_inc(j2, 1)

            def key_turn(b):
                pe.wait_ge(knd, b + 1)
                for i in range(LT):
                    key = ("kt", b, i)
                    empty(J2, key, E2)
                    for k in range(KD):
                        m = pe.transpose(J2.bank(key)[:, k * 128:(k + 1) * 128], kraw[:, b % 2, i, k * 128:(k + 1) * 128], ident[:, :])
                    m.then_inc(j2, 1)

            def cell_turn(t):
                pe.wait_ge(celld, t + 1)
                for k in range(KD):
                    m = pe.transpose(bank[3 + 2 * (t % 2)][:, D + k * S:D + (k + 1) * S], cell[:, 1 - t % 2, k * 128:(k + 1) * 128],
                                     ident[0:S, 0:S])
                m.then_inc(ctd, 1)

            def recurrent_out(J, j, E, b):
                key = ("hx", b)
                empty(J, key, E)
                dst = J.bank(key)[0:S, 0:D]
                pe.matmul(dst, ones2[:, 0:S], GB[:, 3 * D:4 * D], start=True, stop=False)
                for k in range(KD):
                    product(dst, [v[:, k, b * S:(b + 1) * S] for v in (xTH, xTL)], [w[:, 6, k, :] for w in WF], False, False)
                for k in range(KD):
                    m = product(dst, [c[:, k, :] for c in cells], [w[:, 7, k, :] for w in WF], False, k == KD - 1)
                m.then_inc(j, 1)

            for t in range(NB + 1):
                if 0 < t < NB:
                    gates_c(t)
                elif t == NB:
                    pe.wait_ge(cell_lo, NB + 1)
                    recurrent_out(J2, j2, E2, 0)
                    recurrent_out(J2, j2, E2, 1)
                if 0 < t < NB - 1:
                    gates_x(t + 1)
                if t > 0:
                    context_kv(t - 1, [0])
                if t < NB:
                    cell_turn(t)
                if t > 0:
                    context_kv(t - 1, range(1, LT))
                if t < NB:
                    context_turn(t)
                else:
                    recurrent_out(J2, j2, E2, 2)
                if t > 1:
                    key_turn(t - 2)
            recurrent_out(J2, j2, E2, 3)

            pe.wait_ge(e2v, J2.total["dve"])
            pe.wait_ge(e2a, J2.total["act"])
            pe.wait_ge(mask_set, NB)

            def beside(key):
                name, b = key
                s = b % 2
                if name == "hx":
                    recurrent_out(J3, j3, E3, b)
                    return
                empty(J3, key, E3)
                dst = J3.bank(key)
                if name == "zt":
                    pe.wait_ge(z2d, b + 1)
                    turn_rows(J3, key, j3, XN[:, b, :], KD)
                elif name == "qt":
                    pe.wait_ge(qknd, b + 1)
                    turn_rows(J3, key, j3, qkraw[:, s, :], 4)
                elif name == "ot":
                    pe.wait_ge(normed, NB + b + 1)
                    turn_rows(J3, key, j3, osb[:, s, :], KD)
                elif name == "yt":
                    pe.wait_ge(y4, b + 1)
                    turn_rows(J3, key, j3, XN[:, b, :], KD)
                elif name == "kt":
                    pe.wait_ge(knd, NB)
                    for k in range(KD):
                        m = pe.transpose(dst[:, k * 128:(k + 1) * 128], kraw[:, (NB - 1) % 2, b, k * 128:(k + 1) * 128], ident[:, :])
                    m.then_inc(j3, 1)
                elif name == "lg":
                    if b == 0:
                        pe.wait_ge(wrt_split, 1)
                    emptied(J3, ("yt", b), E3)
                    for k in range(KD):
                        m = product(dst[0:S, 0:NE], [v[:, k, b * S:(b + 1) * S] for v in (xTH, xTL)], [w[:, k, :] for w in Wrts],
                                    k == 0, k == KD - 1)
                    m.then_inc(j3, 1)
                elif name == "wo":
                    if b == 0:
                        pe.wait_ge(wo1_lo, 1)
                    emptied(J3, ("ot", b), E3)
                    for c in range(KD):
                        m = product(dst[0:S, 0:D], [t[:, s, c, :] for t in (oTh, oTl)], [w[:, c, :] for w in Wo1], c == 0, c == KD - 1)
                    m.then_inc(j3, 1)
                else:
                    if name == "qk":
                        if b == 0:
                            pe.wait_ge(lat_lo, 1)
                        pe.wait_ge(zl, b + 1)
                    c0, n = (0, 2 * I1) if name == "qk" else (2 * I1, I1)
                    for k in range(KD):
                        m = product(dst[0:S, 0:n], [v[:, k, b * S:(b + 1) * S] for v in (xTH, xTL)],
                                    [w[:, k, c0:c0 + n] for w in Wlat], k == 0, k == KD - 1)
                    m.then_inc(j3, 1)

            def score1(g):
                b, h = divmod(g, H1)
                o = 64 * (h % 2)
                if h == 0:
                    emptied(J3, ("qt", b), E3)
                score(HEADS0 + g, qT1[o:o + 64, b, h // 2, :], kT1[o:o + 64, b, h // 2, :], NK1, maskb[0:1, b, :])

            def values1(g):
                b, h = divmod(g, H1)
                if h == 0:
                    emptied(J3, ("vl", b), E3)
                values(HEADS0 + g, h, NB + b, lambda i, k: V1[0:k, b, i, h * DH:(h + 1) * DH], [128, 128, 128, S])

            def acc(c, hf):
                return bank[4 + 2 * c + hf][:, 0:HALF]

            def gate_up(e, s, hf, first, banks=(bank[0], bank[1]), parts=(0, 1)):
                n = e * 2 + hf
                lo = hf * HALF
                if hf == 0:
                    pe.wait_ge(wes, e * 4 + 2)
                for i in parts:
                    bk, ready, free = banks[i], (g_ready, u_ready)[i], (sild, prodd)[i]
                    if not first:
                        pe.wait_ge(free, n)
                    for k in range(KD):
                        m = product(bk[:, 0:HALF], [w[:, s, i * D + k * 128:i * D + (k + 1) * 128] for w in Wexp],
                                    [v[:, k, lo:lo + HALF] for v in (xTH, xTL)], k == 0, k == KD - 1)
                    m.then_inc(ready, 1)

            for r, h in SLOTS1:
                g = r * H1 + h
                if 0 <= g < HEADS1:
                    turn(HEADS0 + g, 4)
                if h == 0:
                    for key in beside1(r, h):
                        beside(key)
                if 0 <= g + AHEAD < HEADS1:
                    score1(g + AHEAD)
                if h:
                    for key in beside1(r, h):
                        beside(key)
                if 0 <= g - 1 < HEADS1:
                    values1(g - 1)
                if g == HEADS1:
                    pe.wait_ge(expd, HEADS0 + HEADS1)
                    gate_up(0, 0, 0, True, FIRST, (0,))
                if (r, h) == (NB, 2):
                    gate_up(0, 0, 0, True, FIRST, (1,))

            def down(n, s, hf, first, last):
                if hf == 0:
                    pe.wait_ge(wes, n * 2 + 2)
                pe.wait_ge(hlo, n)
                for c in range(KD):
                    m = product(acc(c, hf), [w[:, s, 2 * D + c * 128:2 * D + (c + 1) * 128] for w in Wexp],
                                [h[:, hf, :] for h in (hidH, hidL)], first, last, True)
                m.then_inc(downd, 1)

            pt_wait(HEADS0 + HEADS1 - 2)
            pt_wait(HEADS0 + HEADS1 - 1)
            pe.wait_ge(normed, 2 * NB)
            pe.wait_ge(e3v, J3.total["dve"])
            for e in range(NSH):
                for hf in range(2):
                    if e or hf:
                        gate_up(e, e % 2, hf, False)
                        down(2 * e + hf, (e - 1 + hf) % 2, 1 - hf, e == 0 or (e == 1 and hf == 0), False)
                    if (e, hf) == (2, 1):
                        pe.wait_ge(w_done, 1)
                        for b in range(NB):
                            m = pe.transpose(bank[2 + b // 4][0:NE, (b % 4) * S:(b % 4 + 1) * S], w[:, b, :], ident[0:S, 0:S])
                        m.then_inc(j4, 1)
            with pe.Fori(NSH // 2, (NSH + NE) // 2) as i:
                for s in range(2):
                    for hf in range(2):
                        e = 2 * i + s
                        gate_up(e, s, hf, False)
                        down(2 * e + hf, (s - 1 + hf) % 2, 1 - hf, False, False)
            down(2 * (NSH + NE), 1, 1, False, True)
            for b in range(NB):
                if b % (NB // 2) == 0:
                    pe.wait_ge(oev, 2 * b // NB + 1)
                    pe.wait_ge(oea, 2 * b // NB + 1)
                for c in range(KD):
                    m = pe.transpose(bank[b][0:S, c * 128:(c + 1) * 128], resT[:, c, b * S:(b + 1) * S], ident[:, :])
                m.then_inc(jf, 1)

        @block.scalar
        def _(act):
            def job(sem_in, jobs, key):
                act.wait_ge(sem_in, jobs.done(key))

            def copy(dst, src, scale=1.0):
                return act.activation(dst, src, ACT.Copy, scale=scale)

            def high(dst, src):
                act.activation(dst, src, ACT.Copy).then_inc(whi, 1)

            act.wait_ge(ld_ct[0], 16)
            high(cTs[0][:, 0, :, :], cT[:, 0, :, :])
            act.wait_ge(ld_wk, 16)
            high(W0[0][:, 0, :, :], raw[:, 0, :].rearrange("p (k n) -> p k n", k=KD))
            act.wait_ge(ld_wv, 16)
            high(W0[0][:, 1, :, :], raw[:, 1, :].rearrange("p (k n) -> p k n", k=KD))
            act.wait_ge(ld_small, 80)
            act.activation(gains[:, :], rowb[:, 0:4], ACT.Tanh).then_inc(tanh_g, 1)

            def exps(g, nk):
                act.wait_ge(maxed, g + 1)
                if g >= 3:
                    act.wait_ge(ptd, g - 2)
                act.activation(P[:, g % 3, 0:nk], SBANK[g % AHEAD][0:S, 0:nk], ACT.Exp, bias=nmax[:, g:g + 1],
                               accum_out=esum[:, g:g + 1]).then_inc(expd, 1)

            def turned(g, tiles):
                act.wait_ge(ptd, g + 1)
                if g >= 2:
                    act.wait_ge(pvd, g - 1)
                copy(PTs[:, g % 2, 0:tiles * S], bank[4 + g % 2][:, 0:tiles * S]).then_inc(pt_a, 1)

            def chunks(ap, k):
                return ap.rearrange("p (k n) -> p k n", k=k)

            def beside(key):
                name, b = key[0:2]
                s = b % 2
                src = J1.bank(key)
                if name == "wo" or key[0:1] + key[2:] == ("v", LT - 1):
                    return
                job(j1, J1, key)
                if name == "xt":
                    copy(xnT0[0][:, :, :], chunks(src[:, 0:4 * S], KD)).then_inc(h1, 1)
                elif name == "x1":
                    copy(xTH[:, :, b * S:(b + 1) * S], chunks(src[:, 0:KD * S], KD)).then_inc(h1, 1)
                elif name == "k":
                    if key[2] == 0 and b >= 2:
                        act.wait_ge(scored, H0 * (b - 1))
                    copy(kT0[0][:, s, key[2], :], src[:, 0:LE]).then_inc(h1, 1)
                elif name == "v":
                    if key[2] == 0 and b >= 2:
                        act.wait_ge(pvd, H0 * (b - 1))
                    copy(v0[:, s, key[2], :], src[:, :]).then_inc(e1a, 1)
                elif name == "q":
                    i = key[2] * 2
                    copy(qT0[0][:, b // 2 % 2, i:i + 2, :], chunks(src[:, 0:4 * S], 2), DH ** -0.5).then_inc(h1, 1)
                else:
                    copy(oTh[:, s, :, :], chunks(src[:, 0:4 * S], 4)).then_inc(h1, 1)

            for key in BEFORE0:
                if key == ("k", 0, 2):
                    act.wait_ge(ld_wq, 16)
                    high(W0[0][:, 2, :, :], rawq.rearrange("p (k n) -> p k n", k=KD))
                beside(key)
            act.wait_ge(init, 4)
            for g in range(AHEAD):
                exps(g, L)
            for g in range(HEADS0):
                if g % 2 == 0:
                    turned(g, LT)
                if g + AHEAD < HEADS0:
                    exps(g + AHEAD, L)
                for key in beside0(g // H0, g % H0):
                    beside(key)
            for key in AFTER0:
                beside(key)

            act.wait_ge(j1, len(J1.left))

            def context_high(b):
                act.wait_ge(e2v, J2.emptied(("ct", b, LT - 1))[1])
                if b:
                    act.wait_ge(j2, J2.done(("kv", b - 1, LT - 1)))
                copy(cnT[0][:, :, :], cval).then_inc(cnh, 1)

            def recurrent_out(J, j, e, b):
                job(j, J, ("hx", b))
                if b >= 2:
                    act.wait_ge(st2, b - 1)
                act.activation(th[:, b % 2, :], J.bank(("hx", b))[0:S, 0:D], ACT.Tanh).then_inc(e, 1)

            def key_turn(b):
                for i in range(LT):
                    key = ("kt", b, i)
                    job(j2, J2, key)
                    copy(kT1[:, b, :, i * 128:(i + 1) * 128], chunks(J2.bank(key)[:, 0:D], KD)).then_inc(e2a, 1)

            for t in range(NB + 1):
                if t < NB:
                    act.wait_ge(gated, 2 * t + 1)
                    if t:
                        act.wait_ge(celld, t)
                    act.activation(gate_s[:, :], bank[2 + 2 * (t % 2)][0:S, :], ACT.Sigmoid).then_inc(sigd, 1)
                    act.wait_ge(gated, 2 * t + 2)
                    act.activation(gate_t[:, :], bank[3 + 2 * (t % 2)][0:S, 0:D], ACT.Tanh).then_inc(tand, 1)
                    if t == 0:
                        act.wait_ge(ld_w1, 32)
                        copy(Wctx[0][:, :, :], ctxraw).then_inc(wctx_hi, 1)
                else:
                    recurrent_out(J2, j2, e2a, 0)
                    recurrent_out(J2, j2, e2a, 1)
                if t > 0:
                    b = t - 1
                    if b >= 2:
                        act.wait_ge(j2, J2.done(("kt", b - 2, LT - 1)))
                    if b:
                        act.wait_ge(kss, b)
                    if b == 0:
                        act.wait_ge(wctx_split, 1)
                    for i in range(LT):
                        key = ("kv", b, i)
                        job(j2, J2, key)
                        copy(kraw[:, b % 2, i, :], J2.bank(key)[:, 0:I1])
                        act.activation(ksq[:, i, :], J2.bank(key)[:, 0:I1], ACT.Square)
                        copy(V1[:, b, i, :], J2.bank(key)[:, I1:2 * I1]).then_inc(e2a, 1)
                if t < NB:
                    context_high(t)
                else:
                    recurrent_out(J2, j2, e2a, 2)
                if t > 1:
                    key_turn(t - 2)
                if t == NB - 1:
                    act.wait_ge(ld_lat, 32)
                    copy(WH[:, 0:8 * D], rawlat[:, :]).then_inc(lat_hi, 1)
            recurrent_out(J2, j2, e2a, 3)

            def beside(key):
                name, b = key
                s = b % 2
                src = J3.bank(key)
                if name == "hx":
                    recurrent_out(J3, j3, e3a, b)
                elif name == "kt":
                    job(j3, J3, key)
                    copy(kT1[:, NB - 1, :, b * 128:(b + 1) * 128], chunks(src[:, 0:D], KD)).then_inc(e3a, 1)
                elif name == "zt":
                    act.wait_ge(e3v, J3.emptied(key)[1])
                    copy(xTH[:, :, b * S:(b + 1) * S], zval[:, :, :]).then_inc(zh, 1)
                elif name == "ot":
                    job(j3, J3, key)
                    copy(oTh[:, s, 0:KD, :], chunks(src[:, 0:KD * S], KD)).then_inc(h3, 1)
                elif name == "qk":
                    job(j3, J3, key)
                    copy(qkraw[:, s, :], src[0:S, :])
                    if b:
                        act.wait_ge(qss, b)
                    act.activation(sqs, src[0:S, :], ACT.Square).then_inc(e3a, 1)
                elif name == "vl":
                    job(j3, J3, key)
                    copy(V1[0:S, b, LT, :], src[0:S, 0:I1]).then_inc(e3a, 1)
                elif name == "yt":
                    job(j3, J3, key)
                    copy(xTH[:, :, b * S:(b + 1) * S], chunks(src[:, 0:KD * S], KD)).then_inc(h3, 1)

            for r, h in SLOTS1:
                g = r * H1 + h
                if 0 <= g < HEADS1 and g % 2 == 0:
                    turned(HEADS0 + g, 4)
                if 0 <= g + AHEAD < HEADS1:
                    exps(HEADS0 + g + AHEAD, NK1)
                for key in beside1(r, h):
                    beside(key)

            def expert(e, first):
                for hf in range(2):
                    gate = FIRST[0] if first and hf == 0 else bank[0]
                    n = e * 2 + hf
                    act.wait_ge(g_ready, n + 1)
                    if not first:
                        act.wait_ge(prodd, n - 1)
                    act.activation(sil[:, hf, :], gate[:, 0:HALF], ACT.Silu).then_inc(sild, 1)
                    act.wait_ge(prodd, n + 1)
                    if not first:
                        act.wait_ge(downd, n - 1)
                    copy(hidH[:, hf, :], hid[:, hf, :]).then_inc(hhi, 1)
            expert(0, True)
            act.wait_ge(lsub, 1)
            act.activation(logit[:, :, :], logit[:, :, :], ACT.Exp).then_inc(lexp, 1)
            for e in range(1, NSH):
                expert(e, False)
            with act.Fori(NSH // 2, (NSH + NE) // 2) as i:
                for s in range(2):
                    expert(2 * i + s, False)
            for hf in range(2):
                act.wait_ge(downd, 2 * (NSH + NE) - 1 + hf)
                act.activation(resT[:, 1, hf * HALF:(hf + 1) * HALF], bank[6 + hf][:, 0:HALF], ACT.Copy,
                               scale=gains[:, 3:4]).then_inc(oea, 1)

        @block.vector
        def _(dve):
            chain = [0]

            def own(ins):
                chain[0] += 1
                ins.then_inc(link, 1)
                dve.wait_ge(link, chain[0])

            def job(sem_in, jobs, key):
                dve.wait_ge(sem_in, jobs.done(key))

            def stats(src, p, b, done):
                mv = MV[0:S, p, b, :]
                own(dve.bn_stats(bn[:, :], src))
                own(dve.bn_aggr(mv, bn[:, :]))
                if p == 2:
                    dve.tensor_scalar(mv[:, 1:2], mv[:, 1:2], 1.0 + 1e-5, 1e-10, ALU.mult, ALU.add).then_inc(done, 1)
                else:
                    dve.tensor_scalar(mv[:, 1:2], mv[:, 1:2], 1e-5, None, ALU.add).then_inc(done, 1)

            def standardise(b, p):
                return dve.tensor_scalar(XN[:, b, :], X[:, b, :], MV[0:S, p, b, 0:1], RS[0:S, p, b:b + 1], ALU.subtract, ALU.mult)

            def low(jobs, key, hsem, dst, src, hi):
                dve.wait_ge(hsem, jobs.high[key])
                return dve.tensor_tensor(dst, src, hi.bitcast(F), ALU.subtract)

            def chunks(ap, k):
                return ap.rearrange("p (k n) -> p k n", k=k)

            def low_part(dst, src, hi, n, done):
                dve.wait_ge(whi, n)
                dve.tensor_tensor(dst, src, hi.bitcast(F), ALU.subtract).then_inc(done, 1)

            dve.memset(P[:, :, :], 0.0).then_inc(zeroed, 1)
            low_part(cTs[1][:, 0, :, :], cT[:, 0, :, :], cTs[0][:, 0, :, :], 1, ct_split)
            low_part(W0[1][:, 0, :, :], raw[:, 0, :].rearrange("p (k n) -> p k n", k=KD), W0[0][:, 0, :, :], 2, wsplit0)

            def put_bias(b):
                dve.wait_ge(xn0, b + 1)
                own(dve.tensor_tensor(X[:, b, :], X[:, b, :], bob[:, 0, :], ALU.add))

            def maximum(g, nk):
                dve.wait_ge(scored, g + 1)
                dve.tensor_reduce(nmax[:, g:g + 1], SBANK[g % AHEAD][0:S, 0:nk], AX.X, ALU.max, negate=True).then_inc(maxed, 1)

            def turned(g, tiles):
                dve.wait_ge(ptd, g + 1)
                dve.wait_ge(pvd, g - 1) if g >= 2 else None
                dve.tensor_copy(PTs[:, g % 2, 0:tiles * S], bank[4 + g % 2][:, 0:tiles * S]).then_inc(pt_v, 1)

            def normalise(bt, g0, n):
                s = bt % 2
                dve.wait_ge(expd, g0 + n)
                own(dve.reciprocal(esum[:, g0:g0 + n], esum[:, g0:g0 + n]))
                dve.wait_ge(pvd, g0 + n)
                dve.tensor_tensor(osb[:, s, 0:n * DH].rearrange("p (h d) -> p h d", d=DH),
                                  bank[7][0:S, 0:n * DH].rearrange("p (h d) -> p h d", d=DH),
                                  esum[:, g0:g0 + n].unsqueeze(2).broadcast_to([S, n, DH]), ALU.mult).then_inc(normed, 1)

            def beside(key):
                name, b = key[0:2]
                s = b % 2
                src = J1.bank(key)
                if name == "xt":
                    low(J1, key, h1, xnT0[1][:, :, :], chunks(src[:, 0:4 * S], KD), xnT0[0][:, :, :]).then_inc(e1v, 1)
                elif name == "x1":
                    low(J1, key, h1, xTL[:, :, b * S:(b + 1) * S], chunks(src[:, 0:KD * S], KD), xTH[:, :, b * S:(b + 1) * S]).then_inc(e1v, 1)
                elif name == "k":
                    c = key[2]
                    low(J1, key, h1, kT0[1][:, s, c, :], src[:, 0:LE], kT0[0][:, s, c, :]).then_inc(e1v, 1)
                elif name == "v":
                    if key[2] == LT - 1:
                        job(j1, J1, key)
                        dve.tensor_copy(v0[0:LR, s, 2, :], src[0:LR, :]).then_inc(e1v, 1)
                elif name == "q":
                    i = key[2] * 2
                    dve.wait_ge(h1, J1.high[key])
                    dve.scalar_tensor_tensor(out=qT0[1][:, b // 2 % 2, i:i + 2, :].rearrange("p k n -> p (k n)"), in0=src[:, 0:4 * S],
                                             scalar=DH ** -0.5, in1=qT0[0][:, b // 2 % 2, i:i + 2, :].bitcast(F).rearrange("p k n -> p (k n)"),
                                             op0=ALU.mult, op1=ALU.subtract).then_inc(e1v, 1)
                elif name == "ot":
                    low(J1, key, h1, oTl[:, s, :, :], chunks(src[:, 0:4 * S], 4), oTh[:, s, :, :]).then_inc(e1v, 1)
                else:
                    job(j1, J1, key)
                    dve.scalar_tensor_tensor(out=X[:, b, :], in0=src[0:S, 0:D], scalar=gains[0:S, 0:1], in1=X[:, b, :],
                                             op0=ALU.mult, op1=ALU.add).then_inc(e1v, 1)
                    dve.wait_ge(e1v, J1.emptied(key)[1])

            def split_router():
                dve.wait_ge(ld_w1, 16)
                own(dve.tensor_copy(Wrts[0][:, :, :], Wrt[:, :, :]))
                dve.tensor_tensor(Wrts[1][:, :, :], Wrt[:, :, :], Wrts[0][:, :, :].bitcast(F), ALU.subtract).then_inc(wrt_split, 1)

            def context_norm(b):
                s = b % 2
                dve.wait_ge(crs, b + 1)
                for i in range(LT):
                    last = dve.tensor_scalar(ctok[:, s, i, :], ctok[:, s, i, :], mvc[:, s, i, 0:1], rstdc[:, s, i:i + 1],
                                             ALU.subtract, ALU.mult)
                last.then_inc(cnd, 1)

            def context_stats(b):
                s = b % 2
                dve.wait_ge(ld_ck[s], 16 * (b // 2 + 1))
                for i in range(LT):
                    dve.bn_stats(bnc[:, i, :], ctok[:, s, i, :]).then_inc(link, 1)
                chain[0] += LT
                dve.wait_ge(link, chain[0])
                for i in range(LT):
                    dve.bn_aggr(mvc[:, s, i, :], bnc[:, i, :]).then_inc(link, 1)
                chain[0] += LT
                dve.wait_ge(link, chain[0])
                dve.tensor_scalar(mvc[:, s, :, 1], mvc[:, s, :, 1], 1e-5, None, ALU.add).then_inc(cst, 1)

            def cell_parts(t, src):
                dve.tensor_copy(cells[0][:, :, :], src).then_inc(cell_hi, 1)
                dve.wait_ge(cell_hi, t + 1)
                dve.tensor_tensor(cells[1][:, :, :], src, cells[0][:, :, :].bitcast(F), ALU.subtract).then_inc(cell_lo, 1)

            for key in BEFORE0:
                if key == ("k", 0, 1):
                    low_part(W0[1][:, 1, :, :], raw[:, 1, :].rearrange("p (k n) -> p k n", k=KD), W0[0][:, 1, :, :], 3, wsplit0)
                if key == ("k", 0, 2):
                    dve.wait_ge(ld_x, 32)
                    stats(X[:, 0, :], 0, 0, st0)
                    stats(X[:, 1, :], 0, 1, st0)
                if key == ("xt", 0):
                    dve.wait_ge(rs0, 1)
                    standardise(0, 0).then_inc(xn0, 1)
                    dve.wait_ge(rs0, 2)
                    standardise(1, 0).then_inc(xn0, 1)
                    low_part(W0[1][:, 2, :, :], rawq.rearrange("p (k n) -> p k n", k=KD), W0[0][:, 2, :, :], 4, wsplit0)
                beside(key)
            for g in range(AHEAD):
                maximum(g, L)
            for g in range(HEADS0):
                b, h = divmod(g, H0)
                if h == 1 and b:
                    normalise(b - 1, (b - 1) * H0, H0)
                if g % 2:
                    turned(g, LT)
                if g + AHEAD < HEADS0:
                    maximum(g + AHEAD, L)
                if b == 0 and h == 0:
                    dve.wait_ge(tanh_g, 1)
                    GATE = (0, 2, 1)
                    for i in range(3):
                        dve.tensor_scalar(bob[:, i, :], bob[:, i, :], gains[0:S, GATE[i]:GATE[i] + 1], None, ALU.mult).then_inc(initv, 1)
                    own(dve.tensor_scalar(qk_gain[:, :], colv[:, 8:9], colv[:, 9:10], DH ** -0.5, ALU.mult, ALU.mult))
                    dve.wait_ge(initv, 3)
                if b == 0 and h in (3, 4):
                    put_bias(h - 3)
                if b == 1 and h == 0:
                    split_router()
                for key in beside0(b, h):
                    beside(key)
                if b % 2 == 0 and b + 2 < NB and h in (2, 3):
                    n = b + h
                    stats(X[:, n, :], 0, n, st0)
                if h == 5 and b:
                    stats(X[:, b - 1, :], 1, b - 1, st1)
                if b == NB - 1 and h in (0, 1):
                    context_stats(h)
                if b == NB - 1 and h in (2, 3):
                    context_norm(h - 2)
                if b == NB - 2 and h == 7:
                    cell_parts(0, colv[:, 10:12].unsqueeze(2).broadcast_to([128, KD, S]))
                if b % 2 == 0 and b + 2 < NB and h in (4, 5):
                    n = b + h - 2
                    dve.wait_ge(rs0, n + 1)
                    if n == 4:
                        dve.wait_ge(wsplit0, 3)
                    standardise(n, 0).then_inc(xn0, 1)
                    put_bias(n)
                if h == 7 and b:
                    dve.wait_ge(rs1, b)
                    standardise(b - 1, 1).then_inc(xn1, 1)
            normalise(NB - 1, (NB - 1) * H0, H0)
            for key in AFTER0:
                if key == ("x1", NB - 1):
                    stats(X[:, NB - 1, :], 1, NB - 1, st1)
                    dve.wait_ge(rs1, NB)
                    standardise(NB - 1, 1).then_inc(xn1, 1)
                beside(key)

            def context_turn(b):
                if b:
                    dve.wait_ge(cnl, b)
                for i in range(LT):
                    key = ("ct", b, i)
                    job(j2, J2, key)
                    for k, r in ((0, 128), (1, CR)):
                        last = dve.tensor_scalar(cval[0:r, k, i * 128:(i + 1) * 128], J2.bank(key)[0:r, k * 128:(k + 1) * 128],
                                                 colv[0:r, k:k + 1], colv[0:r, 2 + k:3 + k], ALU.mult, ALU.add)
                    last.then_inc(e2v, 1)
                dve.wait_ge(e2v, J2.emptied(("ct", b, LT - 1))[1])

            def context_low(b):
                dve.wait_ge(cnh, b + 1)
                dve.tensor_tensor(cnT[1][:, :, :], cval, cnT[0][:, :, :].bitcast(F), ALU.subtract).then_inc(cnl, 1)

            def key_sums(b):
                s = b % 2
                dve.wait_ge(e2a, J2.emptied(("kv", b, LT - 1))[1])
                own(dve.tensor_reduce(ssk[:, s, :], ksq[:, :, :].rearrange("p t (h d) -> p (t h) d", d=DH), AX.X, ALU.add))
                dve.tensor_scalar(ssk[:, s, :], ssk[:, s, :], 1.0 / DH, 1e-16, ALU.mult, ALU.max).then_inc(kss, 1)

            dve.wait_ge(j1, len(J1.left))
            own(dve.memset(cval[:, 1, :], 0.0))

            def latent(b):
                dve.wait_ge(rs2, b + 1)
                standardise(b, 2).then_inc(z2d, 1)
                dve.wait_ge(z2d, b + 1)
                own(dve.tensor_tensor(X[:, b, :], X[:, b, :], bob[:, 2, :], ALU.add))

            def residual2(J, e, b):
                dve.wait_ge(e, J.emptied(("hx", b))[1])
                own(dve.scalar_tensor_tensor(out=X[:, b, :], in0=th[:, b % 2, :], scalar=gains[0:S, 2:3], in1=X[:, b, :],
                                             op0=ALU.mult, op1=ALU.add))
                stats(X[:, b, :], 2, b, st2)

            dve.wait_ge(ld_c0, 16)
            for t in range(NB + 1):
                if t == NB:
                    residual2(J2, e2a, 0)
                    residual2(J2, e2a, 1)
                    dve.wait_ge(lat_hi, 1)
                    dve.tensor_tensor(WL[:, 0:6 * D], rawlat[:, 0:6 * D], WH[:, 0:6 * D].bitcast(F), ALU.subtract).then_inc(lat_lo, 1)
                    latent(0)
                if t < NB:
                    s = t % 2
                    dve.wait_ge(sigd, t + 1)
                    own(dve.tensor_tensor(fc[:, :], gate_s[:, 0:D], cell[:, s, :], ALU.mult))
                    dve.wait_ge(tand, t + 1)
                    own(dve.tensor_tensor(ig[:, :], gate_s[:, D:2 * D], gate_t[:, :], ALU.mult))
                    dve.tensor_tensor(cell[:, 1 - s, :], fc[:, :], ig[:, :], ALU.add).then_inc(celld, 1)
                    dve.wait_ge(ctd, t + 1)
                    cell_parts(t + 1, chunks(bank[3 + 2 * s][:, D:D + KD * S], KD))
                    if t == 0:
                        dve.wait_ge(wctx_hi, 1)
                        dve.tensor_tensor(Wctx[1][:, :, :], ctxraw, Wctx[0][:, :, :].bitcast(F), ALU.subtract).then_inc(wctx_split, 1)
                if 0 < t < NB - 1:
                    context_norm(t + 1)
                if t < NB:
                    context_turn(t)
                if t > 0:
                    key_sums(t - 1)
                if t < NB:
                    context_low(t)
                if t + 2 < NB:
                    context_stats(t + 2)

            for b in range(2, HX0):
                residual2(J2, e2a, b)

            def sum_squares(b):
                dve.wait_ge(e3a, J3.emptied(("qk", b))[1])
                own(dve.tensor_reduce(ssq[:, b, :], sqs.rearrange("p (h d) -> p h d", d=DH), AX.X, ALU.add))
                dve.tensor_scalar(ssq[:, b, :], ssq[:, b, :], 1.0 / DH, 1e-16, ALU.mult, ALU.max).then_inc(qss, 1)

            def beside(key):
                name, b = key
                s = b % 2
                src = J3.bank(key)
                if name == "hx":
                    residual2(J3, e3a, b)
                elif name == "zt":
                    job(j3, J3, key)
                    for k in range(KD):
                        dve.tensor_scalar(zval[:, k, :], src[:, k * S:(k + 1) * S], colv[:, 4 + k:5 + k], colv[:, 6 + k:7 + k],
                                          ALU.mult, ALU.add).then_inc(e3v if k else link, 1)
                    chain[0] += 1
                    dve.wait_ge(link, chain[0])
                    dve.wait_ge(zh, b + 1)
                    dve.tensor_tensor(xTL[:, :, b * S:(b + 1) * S], zval[:, :, :], xTH[:, :, b * S:(b + 1) * S].bitcast(F),
                                      ALU.subtract).then_inc(zl, 1)
                    if b + 1 < NB:
                        latent(b + 1)
                elif name == "lg":
                    job(j3, J3, key)
                    dve.tensor_tensor(logit[:, b, :], src[0:S, 0:NE], rowb[0:S, 4:ROWS], ALU.add).then_inc(e3v, 1)
                elif name == "vl":
                    if key in BEFORE1:
                        sum_squares(b)
                elif name == "qt":
                    job(j3, J3, key)
                    own(dve.tensor_scalar(qT1[:, b, :, :], chunks(src[:, 0:2 * S], KD), qk_gain[:, 0:1], None, ALU.mult))
                    dve.tensor_copy(kT1[:, b, :, LP:NK1], chunks(src[:, 2 * S:4 * S], KD)).then_inc(e3v, 1)
                elif name == "ot":
                    low(J3, key, h3, oTl[:, s, 0:KD, :], chunks(src[:, 0:KD * S], KD), oTh[:, s, 0:KD, :]).then_inc(e3v, 1)
                elif name == "yt":
                    low(J3, key, h3, xTL[:, :, b * S:(b + 1) * S], chunks(src[:, 0:KD * S], KD), xTH[:, :, b * S:(b + 1) * S]).then_inc(e3v, 1)
                elif name == "wo":
                    job(j3, J3, key)
                    dve.scalar_tensor_tensor(out=X[:, b, :], in0=src[0:S, 0:D], scalar=gains[0:S, 1:2], in1=X[:, b, :],
                                             op0=ALU.mult, op1=ALU.add).then_inc(e3v, 1)
                    dve.wait_ge(e3v, J3.emptied(key)[1])
                    stats(X[:, b, :], 3, b, st3)

            for r, h in SLOTS1:
                g = r * H1 + h
                if h == 1 and real(r - 1):
                    normalise(NB + r - 1, HEADS0 + (r - 1) * H1, H1)
                if 0 <= g < HEADS1 and g % 2:
                    turned(HEADS0 + g, 4)
                if 0 <= g + AHEAD < HEADS1:
                    maximum(HEADS0 + g + AHEAD, NK1)
                if h == 2 and ("vl", r + 2) in beside1(r, 1):
                    sum_squares(r + 2)
                if h == 1 and real(r - 2):
                    b = r - 2
                    dve.wait_ge(rs3, b + 1)
                    standardise(b, 3).then_inc(y4, 1)
                for key in beside1(r, h):
                    beside(key)
            def router_1():
                own(dve.memset(prob[:, :, NE:NE + 8], -1.0))
                own(dve.tensor_reduce(lmax[:, :], logit[:, :, :], AX.X, ALU.max))
                dve.tensor_tensor(logit[:, :, :], logit[:, :, :], lmax[:, :].unsqueeze(2).broadcast_to([S, NB, NE]), ALU.subtract).then_inc(lsub, 1)

            def router_2():
                dve.wait_ge(lexp, 1)
                own(dve.tensor_reduce(lsum[:, :], logit[:, :, :], AX.X, ALU.add))
                own(dve.reciprocal(lrec[:, :], lsum[:, :]))
                own(dve.tensor_tensor(prob[:, :, 0:NE], logit[:, :, :], lrec[:, :].unsqueeze(2).broadcast_to([S, NB, NE]), ALU.mult))

            def router_3():
                for b in range(NB):
                    dve.max(top[:, b, :], prob[:, b, 0:NE]).then_inc(link, 1)
                chain[0] += NB
                dve.wait_ge(link, chain[0])
                own(dve.memset(top[:, :, 4:8], -1.0))

            def router_4():
                for b in range(NB):
                    dve.match_replace(rest[:, b, :], in_to_replace=top[:, b, :], in_values=prob[:, b, :], imm_value=0.0).then_inc(link, 1)
                chain[0] += NB
                dve.wait_ge(link, chain[0])

            def router_5():
                own(dve.tensor_tensor(logit[:, :, :], prob[:, :, 0:NE], rest[:, :, 0:NE], ALU.subtract))
                own(dve.tensor_reduce(lsum[:, :], logit[:, :, :], AX.X, ALU.add))
                own(dve.tensor_scalar(lsum[:, :], lsum[:, :], 1e-12, None, ALU.max))
                own(dve.reciprocal(lrec[:, :], lsum[:, :]))
                dve.tensor_tensor(w, logit[:, :, :], lrec[:, :].unsqueeze(2).broadcast_to([S, NB, NE]), ALU.mult).then_inc(w_done, 1)

            def router_6():
                dve.wait_ge(j4, 1)
                for i in range(2):
                    dve.tensor_copy(wT[:, i * HALF:(i + 1) * HALF], bank[2 + i][0:NE, 0:HALF]).then_inc(e4v, 1)

            def expert(e, hf, routed, early, s=None):
                n = e * 2 + hf
                if routed:
                    dve.wait_ge(sild, n + 1)
                    if hf == 0:
                        dve.wait_ge(ld_wb[s], (e - s) * 8 - 8 * NSH + 16)
                    dve.tensor_tensor(sw[:, hf, :], sil[:, hf, :], wbs[:, s, hf * HALF:(hf + 1) * HALF], ALU.mult).then_inc(swd, 1)
                    dve.wait_ge(swd, (e - NSH) * 2 + hf + 1)
                dve.wait_ge(u_ready, n + 1)
                dve.wait_ge(sild, n + 1)
                up = FIRST[1] if early else bank[1]
                dve.tensor_tensor(hid[:, hf, :], (sw if routed else sil)[:, hf, :], up[:, 0:HALF], ALU.mult).then_inc(prodd, 1)
                dve.wait_ge(hhi, n + 1)
                dve.tensor_tensor(hidL[:, hf, :], hid[:, hf, :], hidH[:, hf, :].bitcast(F), ALU.subtract).then_inc(hlo, 1)

            router_1()
            expert(0, 0, False, True)
            expert(0, 1, False, False)
            router_2()
            expert(1, 0, False, False)
            router_3()
            expert(1, 1, False, False)
            router_4()
            expert(2, 0, False, False)
            router_5()
            expert(2, 1, False, False)
            router_6()
            expert(3, 0, False, False)
            expert(3, 1, False, False)
            with dve.Fori(NSH // 2, (NSH + NE) // 2) as i:
                for s in range(2):
                    for hf in range(2):
                        expert(2 * i + s, hf, True, False, s)
            for hf in range(2):
                dve.wait_ge(downd, 2 * (NSH + NE) - 1 + hf)
                dve.tensor_scalar(resT[:, 0, hf * HALF:(hf + 1) * HALF], bank[4 + hf][:, 0:HALF], gains[:, 3:4], None,
                                  ALU.mult).then_inc(oev, 1)
            for b in range(NB):
                dve.wait_ge(jf, b + 1)
                dve.tensor_tensor(X[:, b, :], bank[b][0:S, 0:D], X[:, b, :], ALU.add).then_inc(fin, 1)


def kernel(**inputs):
    import numpy as np
    import concourse.bacc as bacc
    from concourse.bass_utils import run_bass_kernel_spmd as run

    a = {k: np.asarray(v) for k, v in inputs.items()}
    eye = np.eye(128, dtype=np.float32)

    def chunks(w):
        return w.reshape(-1, KD, 128, 128).transpose(0, 2, 1, 3).reshape(-1, 128, D)

    def pad(v):
        return np.concatenate([v, np.zeros(128 * KD - v.shape[0], v.dtype)]).reshape(KD, 128)

    gate_w = np.concatenate([a["L1_ffn_sgate_w"].reshape(NSH, 128, D), a["L1_ffn_gate_w"]])
    up_w = np.concatenate([a["L1_ffn_sup_w"].reshape(NSH, 128, D), a["L1_ffn_up_w"]])
    down_w = np.concatenate([a["L1_ffn_sdown_w"].reshape(D, NSH, 128).transpose(1, 0, 2), a["L1_ffn_down_w"]])
    cols = np.concatenate([pad(a["L1_xattn_ln_x_g"]), pad(a["L1_xattn_ln_x_b"]), pad(a["L1_xattn_ln_l_g"]), pad(a["L1_xattn_ln_l_b"]),
                           np.tile(a["L1_xattn_qn_g"], 2)[None], np.tile(a["L1_xattn_kn_g"], 2)[None], pad(a["L0_ffn_in_c"])])
    arrays = {
        "x": a["x"],
        "ctx": np.pad(a["ctx_768"], ((0, 0), (0, LP - L), (0, 0))),
        "ctx_t": np.pad(a["ctx_768"].transpose(2, 0, 1), ((0, 256 - C), (0, 0), (0, 1))),
        "mask": a["mask_BxS2_bk0"][None],
        "rows": np.concatenate([a["g_xattn"], a["g_ffn"], a["L0_xattn_bo"], a["L0_ffn_bo"], a["L1_xattn_bo"], a["L1_ffn_router_bias"], a["L0_ffn_in_c"]]),
        "gate_rows": np.tile(np.concatenate([a["L0_ffn_bf"], a["L0_ffn_bi"], a["L0_ffn_bc"], a["L0_ffn_bo"]])[None], (2, 1)),
        "cols": cols.T,
        "w0": np.stack([np.pad(a["L0_xattn_Wk"], ((0, 256 - C), (0, 0))), np.pad(a["L0_xattn_Wv"], ((0, 256 - C), (0, 0))), a["L0_xattn_Wq"]]),
        "wo0": a["L0_xattn_Wo"],
        "wffn": np.stack([a["L0_ffn_" + n].T for n in ("wf", "wi", "wc", "uf", "ui", "uc", "wo", "uo")]),
        "wlat": np.concatenate([a["L1_xattn_Wq"].T, a["L1_xattn_Wlkv"].T], 1),
        "wctx": np.pad(a["L1_xattn_Wkv"].T, ((0, 256 - C), (0, 0))),
        "wo1": a["L1_xattn_Wo"].T,
        "wrt": a["L1_ffn_router_w"].T,
        "wmoe": np.concatenate([chunks(gate_w.transpose(0, 2, 1)), chunks(up_w.transpose(0, 2, 1)), down_w.transpose(0, 2, 1)], 2),
        "ident_in": eye,
    }
    nc = bacc.Bacc("TRN2", target_bir_lowering=False, num_devices=1)
    feeds, aps = {}, []
    for name, v in arrays.items():
        v = np.ascontiguousarray(v)
        feeds["in_" + name] = v
        aps.append(nc.dram_tensor("in_" + name, v.shape, mybir.dt.from_np(v.dtype), kind="ExternalInput").ap())
    out = nc.dram_tensor("out_0", (NB, S, D), mybir.dt.float32, kind="ExternalOutput").ap()
    token_w = nc.dram_tensor("token_w", (NE, TOK), mybir.dt.float32, kind="Internal").ap()
    build(nc, *aps, token_w, out)
    r = run(nc, [feeds], core_ids=[0])
    return r.results[0]["out_0"]
```
